# Optimizing a Trainium2 kernel written in Bass

```python
import numpy as np
import jax
import jax.numpy as jnp

def _softmax(x, axis=-1):
    return jax.nn.softmax(x, axis=axis)

def _gelu(x):
    return jax.nn.gelu(x, approximate=True)

def _silu(x):
    return jax.nn.silu(x)

def _sigmoid(x):
    return jax.nn.sigmoid(x)

def _layernorm(x, axis=-1, eps=1e-05):
    m = jnp.mean(x, axis=axis, keepdims=True)
    v = jnp.var(x, axis=axis, keepdims=True)
    return (x - m) / jnp.sqrt(v + eps)

def _scatter_add(tgt, idx, src, axis=0):
    return tgt.at[idx].add(src)

def _segment_sum(src, seg, n):
    return jax.ops.segment_sum(src, seg, n)
kernel_name = 'mk_gnn_preln_d4_gnn_r8_ca07e9'

def setup_inputs(seed: int=0):
    np.random.seed(seed)
    _w = jnp.asarray

    def _rec_inputs():
        import jax
        import jax.numpy as jnp
        _gk = jax.random.key(seed)
        x = -8.776e-05 + 1 * jax.random.normal(jax.random.fold_in(_gk, 1), (5000, 128), jnp.float32)
        src = jax.random.randint(jax.random.fold_in(_gk, 2), (80000,), 0, 5000, jnp.int32)
        dst = jax.random.randint(jax.random.fold_in(_gk, 3), (80000,), 0, 5000, jnp.int32)
        _o = jnp.argsort(dst, stable=True)
        src = src[_o]
        dst = dst[_o]
        edge_attr_128 = 1.67468e-05 + 0.10002 * jax.random.normal(jax.random.fold_in(_gk, 12), (80000, 128), jnp.float32)
        edge_attr_4 = jax.random.uniform(jax.random.fold_in(_gk, 13), (80000, 4), jnp.float32, 0.0, 1)
        return (x, src, dst, edge_attr_128, edge_attr_4)
    x, src, dst, edge_attr_128, edge_attr_4 = _rec_inputs()

    def _L0_gnn_setup():
        import jax, jax.numpy as jnp
        import numpy as np
        N, E, H, HEADS, T = (5000, 40000, 128, 4, 3)
        DH = H // HEADS

        def _ln(x, g, b, eps=1e-12):
            u = jnp.mean(x, axis=-1, keepdims=True)
            s = jnp.mean((x - u) ** 2, axis=-1, keepdims=True)
            return g * (x - u) / jnp.sqrt(s + eps) + b

        def _gat(x, src, dst, edge_attr, wq, bq, wk, bk, wv, bv):
            x_i = x[dst]
            x_j = x[src] + edge_attr
            q = (x_i @ wq.T + bq).reshape(-1, HEADS, DH)
            k = (x_j @ wk.T + bk).reshape(-1, HEADS, DH)
            v = (x_j @ wv.T + bv).reshape(-1, HEADS, DH)
            alpha = jnp.sum(q * k, axis=-1) / jnp.sqrt(jnp.float32(DH))
            m = jax.ops.segment_max(alpha, dst, num_segments=N)
            m = jnp.where(jnp.isfinite(m), m, jnp.zeros_like(m))
            a = jnp.exp(alpha - m[dst])
            s = jax.ops.segment_sum(a, dst, num_segments=N)
            a = a / (s[dst] + 1e-16)
            out = jax.ops.segment_sum(a[..., None] * v, dst, num_segments=N)
            return out.reshape(N, H)
        key = jax.random.key(seed)
        ks = jax.random.split(key, 32)
        f32 = jnp.float32

        def w(k, shape, s=0.05):
            return (s * jax.random.normal(k, shape)).astype(f32)
        inp = {'x': jax.random.normal(ks[0], (N, H), dtype=f32), 'edge_index': jax.random.randint(ks[1], (2, E), 0, N, dtype=jnp.int32), 'edge_attr': 0.1 * jax.random.normal(ks[2], (E, H), dtype=f32), 'wq': w(ks[3], (H, H)), 'bq': w(ks[4], (H,)), 'wk': w(ks[5], (H, H)), 'bk': w(ks[6], (H,)), 'wv': w(ks[7], (H, H)), 'bv': w(ks[8], (H,)), 'w_ao': w(ks[9], (H, H)), 'b_ao': w(ks[10], (H,)), 'ln1_g': jnp.ones((H,), f32), 'ln1_b': jnp.zeros((H,), f32), 'w_int': w(ks[11], (4 * H, H)), 'b_int': w(ks[12], (4 * H,)), 'w_out': w(ks[13], (H, 4 * H)), 'b_out': w(ks[14], (H,)), 'ln2_g': jnp.ones((H,), f32), 'ln2_b': jnp.zeros((H,), f32), 'w_ih': w(ks[15], (3 * H, H)), 'w_hh': w(ks[16], (3 * H, H)), 'b_ih': w(ks[17], (3 * H,)), 'b_hh': w(ks[18], (3 * H,)), 'ln3_g': jnp.ones((H,), f32), 'ln3_b': jnp.zeros((H,), f32)}
        return inp
    _L0_gnn_all = _L0_gnn_setup()
    _L0_gnn_in = {k: v for k, v in _L0_gnn_all.items() if k in ('wq', 'bq', 'wk', 'bk', 'wv', 'bv', 'w_ao', 'b_ao', 'ln1_g', 'ln1_b', 'w_int', 'b_int', 'w_out', 'b_out', 'ln2_g', 'ln2_b', 'w_ih', 'w_hh', 'b_ih', 'b_hh', 'ln3_g', 'ln3_b')}
    del _L0_gnn_all

    def _L1_gnn_setup():
        import jax, jax.numpy as jnp
        import numpy as np
        N, E, D = (5000, 80000, 128)
        BN_EPS = 1e-05
        key = jax.random.key(seed)
        ks = jax.random.split(key, 6)
        x = jax.random.normal(ks[0], (N, D), dtype=jnp.float32)
        src = jax.random.randint(ks[1], (E,), 0, N, dtype=jnp.int64)
        dst = jax.random.randint(ks[2], (E,), 0, N, dtype=jnp.int64)
        W1 = jax.random.normal(ks[3], (D, D), dtype=jnp.float32) * (1.0 / np.sqrt(D))
        b1 = jnp.zeros((D,), dtype=jnp.float32)
        gamma = jnp.ones((D,), dtype=jnp.float32)
        beta = jnp.zeros((D,), dtype=jnp.float32)
        W2 = jax.random.normal(ks[4], (D, D), dtype=jnp.float32) * (1.0 / np.sqrt(D))
        b2 = jnp.zeros((D,), dtype=jnp.float32)
        eps = jnp.zeros((1,), dtype=jnp.float32)
        return {'x': x, 'src': src, 'dst': dst, 'W1': W1, 'b1': b1, 'gamma': gamma, 'beta': beta, 'W2': W2, 'b2': b2, 'eps': eps}
    _L1_gnn_all = _L1_gnn_setup()
    _L1_gnn_in = {k: v for k, v in _L1_gnn_all.items() if k in ('W1', 'b1', 'gamma', 'beta', 'W2', 'b2', 'eps')}
    del _L1_gnn_all

    def _L2_gnn_setup():
        import jax, jax.numpy as jnp
        import numpy as np
        N_NODES = 12500
        N_EDGES = 200000
        HIDDEN = 128
        N_ETYPES = 4
        N_STEPS = 4

        def _gru_cell(x, h, W_ih, W_hh, b_ih, b_hh):
            gi = x @ W_ih.T + b_ih
            gh = h @ W_hh.T + b_hh
            ir, iz, inn = jnp.split(gi, 3, axis=1)
            hr, hz, hn = jnp.split(gh, 3, axis=1)
            r = jax.nn.sigmoid(ir + hr)
            z = jax.nn.sigmoid(iz + hz)
            n = jnp.tanh(inn + r * hn)
            return (1.0 - z) * n + z * h
        key = jax.random.key(seed)
        ks = jax.random.split(key, 10)
        s = 1.0 / np.sqrt(HIDDEN)
        node_feat = jax.random.normal(ks[0], (N_NODES, HIDDEN), dtype=jnp.float32)
        edge_index = jax.random.randint(ks[1], (2, N_EDGES), 0, N_NODES)
        edge_feat = jax.random.uniform(ks[2], (N_EDGES, N_ETYPES), dtype=jnp.float32)
        W_edge = jax.random.uniform(ks[3], (N_ETYPES, HIDDEN, HIDDEN), minval=-s, maxval=s, dtype=jnp.float32)
        b_edge = jax.random.uniform(ks[4], (N_ETYPES, HIDDEN), minval=-s, maxval=s, dtype=jnp.float32)
        W_ih = jax.random.uniform(ks[5], (3 * HIDDEN, HIDDEN), minval=-s, maxval=s, dtype=jnp.float32)
        W_hh = jax.random.uniform(ks[6], (3 * HIDDEN, HIDDEN), minval=-s, maxval=s, dtype=jnp.float32)
        b_ih = jax.random.uniform(ks[7], (3 * HIDDEN,), minval=-s, maxval=s, dtype=jnp.float32)
        b_hh = jax.random.uniform(ks[8], (3 * HIDDEN,), minval=-s, maxval=s, dtype=jnp.float32)
        return {'node_feat': node_feat, 'edge_index': edge_index, 'edge_feat': edge_feat, 'W_edge': W_edge, 'b_edge': b_edge, 'W_ih': W_ih, 'W_hh': W_hh, 'b_ih': b_ih, 'b_hh': b_hh}
    _L2_gnn_all = _L2_gnn_setup()
    _L2_gnn_in = {k: v for k, v in _L2_gnn_all.items() if k in ('W_edge', 'b_edge', 'W_ih', 'W_hh', 'b_ih', 'b_hh')}
    del _L2_gnn_all

    def _L3_gnn_setup():
        import jax, jax.numpy as jnp
        import numpy as np
        N, E = (6250, 100000)
        D, H = (128, 8)
        DH = D // H
        DFF = 2 * D
        EPS_BN = 1e-05

        def _batch_norm(x, g, b):
            mu = jnp.mean(x, axis=0)
            var = jnp.mean((x - mu) ** 2, axis=0)
            return (x - mu) * jax.lax.rsqrt(var + EPS_BN) * g + b
        key = jax.random.key(seed)
        ks = jax.random.split(key, 12)
        s = 1.0 / np.sqrt(D)
        inp = {'h': jax.random.normal(ks[0], (N, D), dtype=jnp.float32), 'src': jax.random.randint(ks[1], (E,), 0, N, dtype=jnp.int32), 'dst': jax.random.randint(ks[2], (E,), 0, N, dtype=jnp.int32), 'Wq': jax.random.normal(ks[3], (D, D), dtype=jnp.float32) * s, 'Wk': jax.random.normal(ks[4], (D, D), dtype=jnp.float32) * s, 'Wv': jax.random.normal(ks[5], (D, D), dtype=jnp.float32) * s, 'Wo': jax.random.normal(ks[6], (D, D), dtype=jnp.float32) * s, 'bo': jnp.zeros((D,), dtype=jnp.float32), 'W1': jax.random.normal(ks[7], (D, DFF), dtype=jnp.float32) * s, 'b1': jnp.zeros((DFF,), dtype=jnp.float32), 'W2': jax.random.normal(ks[8], (DFF, D), dtype=jnp.float32) * (1.0 / np.sqrt(DFF)), 'b2': jnp.zeros((D,), dtype=jnp.float32), 'bn1_g': jnp.ones((D,), dtype=jnp.float32), 'bn1_b': jnp.zeros((D,), dtype=jnp.float32), 'bn2_g': jnp.ones((D,), dtype=jnp.float32), 'bn2_b': jnp.zeros((D,), dtype=jnp.float32)}
        return inp
    _L3_gnn_all = _L3_gnn_setup()
    _L3_gnn_in = {k: v for k, v in _L3_gnn_all.items() if k in ('Wq', 'Wk', 'Wv', 'Wo', 'bo', 'W1', 'b1', 'W2', 'b2', 'bn1_g', 'bn1_b', 'bn2_g', 'bn2_b')}
    del _L3_gnn_all
    return {'x': x, 'src': src, 'dst': dst, 'edge_attr_128': edge_attr_128, 'edge_attr_4': edge_attr_4, 'L0_gnn_wq': _L0_gnn_in['wq'], 'L0_gnn_bq': _L0_gnn_in['bq'], 'L0_gnn_wk': _L0_gnn_in['wk'], 'L0_gnn_bk': _L0_gnn_in['bk'], 'L0_gnn_wv': _L0_gnn_in['wv'], 'L0_gnn_bv': _L0_gnn_in['bv'], 'L0_gnn_w_ao': _L0_gnn_in['w_ao'], 'L0_gnn_b_ao': _L0_gnn_in['b_ao'], 'L0_gnn_ln1_g': _L0_gnn_in['ln1_g'], 'L0_gnn_ln1_b': _L0_gnn_in['ln1_b'], 'L0_gnn_w_int': _L0_gnn_in['w_int'], 'L0_gnn_b_int': _L0_gnn_in['b_int'], 'L0_gnn_w_out': _L0_gnn_in['w_out'], 'L0_gnn_b_out': _L0_gnn_in['b_out'], 'L0_gnn_ln2_g': _L0_gnn_in['ln2_g'], 'L0_gnn_ln2_b': _L0_gnn_in['ln2_b'], 'L0_gnn_w_ih': _L0_gnn_in['w_ih'], 'L0_gnn_w_hh': _L0_gnn_in['w_hh'], 'L0_gnn_b_ih': _L0_gnn_in['b_ih'], 'L0_gnn_b_hh': _L0_gnn_in['b_hh'], 'L0_gnn_ln3_g': _L0_gnn_in['ln3_g'], 'L0_gnn_ln3_b': _L0_gnn_in['ln3_b'], 'L1_gnn_W1': _L1_gnn_in['W1'], 'L1_gnn_b1': _L1_gnn_in['b1'], 'L1_gnn_gamma': _L1_gnn_in['gamma'], 'L1_gnn_beta': _L1_gnn_in['beta'], 'L1_gnn_W2': _L1_gnn_in['W2'], 'L1_gnn_b2': _L1_gnn_in['b2'], 'L1_gnn_eps': _L1_gnn_in['eps'], 'L2_gnn_W_edge': _L2_gnn_in['W_edge'], 'L2_gnn_b_edge': _L2_gnn_in['b_edge'], 'L2_gnn_W_ih': _L2_gnn_in['W_ih'], 'L2_gnn_W_hh': _L2_gnn_in['W_hh'], 'L2_gnn_b_ih': _L2_gnn_in['b_ih'], 'L2_gnn_b_hh': _L2_gnn_in['b_hh'], 'L3_gnn_Wq': _L3_gnn_in['Wq'], 'L3_gnn_Wk': _L3_gnn_in['Wk'], 'L3_gnn_Wv': _L3_gnn_in['Wv'], 'L3_gnn_Wo': _L3_gnn_in['Wo'], 'L3_gnn_bo': _L3_gnn_in['bo'], 'L3_gnn_W1': _L3_gnn_in['W1'], 'L3_gnn_b1': _L3_gnn_in['b1'], 'L3_gnn_W2': _L3_gnn_in['W2'], 'L3_gnn_b2': _L3_gnn_in['b2'], 'L3_gnn_bn1_g': _L3_gnn_in['bn1_g'], 'L3_gnn_bn1_b': _L3_gnn_in['bn1_b'], 'L3_gnn_bn2_g': _L3_gnn_in['bn2_g'], 'L3_gnn_bn2_b': _L3_gnn_in['bn2_b']}

def reference(x, src, dst, edge_attr_128, edge_attr_4, L0_gnn_wq, L0_gnn_bq, L0_gnn_wk, L0_gnn_bk, L0_gnn_wv, L0_gnn_bv, L0_gnn_w_ao, L0_gnn_b_ao, L0_gnn_ln1_g, L0_gnn_ln1_b, L0_gnn_w_int, L0_gnn_b_int, L0_gnn_w_out, L0_gnn_b_out, L0_gnn_ln2_g, L0_gnn_ln2_b, L0_gnn_w_ih, L0_gnn_w_hh, L0_gnn_b_ih, L0_gnn_b_hh, L0_gnn_ln3_g, L0_gnn_ln3_b, L1_gnn_W1, L1_gnn_b1, L1_gnn_gamma, L1_gnn_beta, L1_gnn_W2, L1_gnn_b2, L1_gnn_eps, L2_gnn_W_edge, L2_gnn_b_edge, L2_gnn_W_ih, L2_gnn_W_hh, L2_gnn_b_ih, L2_gnn_b_hh, L3_gnn_Wq, L3_gnn_Wk, L3_gnn_Wv, L3_gnn_Wo, L3_gnn_bo, L3_gnn_W1, L3_gnn_b1, L3_gnn_W2, L3_gnn_b2, L3_gnn_bn1_g, L3_gnn_bn1_b, L3_gnn_bn2_g, L3_gnn_bn2_b):
    import jax
    import jax.numpy as jnp

    def _L0_gnn_ref(x, edge_index, edge_attr, wq, bq, wk, bk, wv, bv, w_ao, b_ao, ln1_g, ln1_b, w_int, b_int, w_out, b_out, ln2_g, ln2_b, w_ih, w_hh, b_ih, b_hh, ln3_g, ln3_b):
        import jax, jax.numpy as jnp
        import numpy as np
        N, E, H, HEADS, T = (5000, 40000, 128, 4, 3)
        DH = H // HEADS

        def _ln(x, g, b, eps=1e-12):
            u = jnp.mean(x, axis=-1, keepdims=True)
            s = jnp.mean((x - u) ** 2, axis=-1, keepdims=True)
            return g * (x - u) / jnp.sqrt(s + eps) + b

        def _gat(x, src, dst, edge_attr, wq, bq, wk, bk, wv, bv):
            x_i = x[dst]
            x_j = x[src] + edge_attr
            q = (x_i @ wq.T + bq).reshape(-1, HEADS, DH)
            k = (x_j @ wk.T + bk).reshape(-1, HEADS, DH)
            v = (x_j @ wv.T + bv).reshape(-1, HEADS, DH)
            alpha = jnp.sum(q * k, axis=-1) / jnp.sqrt(jnp.float32(DH))
            m = jax.ops.segment_max(alpha, dst, num_segments=N)
            m = jnp.where(jnp.isfinite(m), m, jnp.zeros_like(m))
            a = jnp.exp(alpha - m[dst])
            s = jax.ops.segment_sum(a, dst, num_segments=N)
            a = a / (s[dst] + 1e-16)
            out = jax.ops.segment_sum(a[..., None] * v, dst, num_segments=N)
            return out.reshape(N, H)
        src, dst = (edge_index[0], edge_index[1])
        h = x
        for _ in range(T):
            att = _gat(x, src, dst, edge_attr, wq, bq, wk, bk, wv, bv)
            att = _ln(att @ w_ao.T + b_ao + x, ln1_g, ln1_b)
            inter = jax.nn.gelu(att @ w_int.T + b_int, approximate=False)
            m = _ln(inter @ w_out.T + b_out + att, ln2_g, ln2_b)
            gi = m @ w_ih.T + b_ih
            gh = h @ w_hh.T + b_hh
            ir, iz, inn = jnp.split(gi, 3, axis=-1)
            hr, hz, hn = jnp.split(gh, 3, axis=-1)
            r = jax.nn.sigmoid(ir + hr)
            z = jax.nn.sigmoid(iz + hz)
            n = jnp.tanh(inn + r * hn)
            h = (1.0 - z) * n + z * h
            x = _ln(h, ln3_g, ln3_b)
        return x

    def _L1_gnn_ref(x, src, dst, W1, b1, gamma, beta, W2, b2, eps):
        import jax, jax.numpy as jnp
        import numpy as np
        N, E, D = (5000, 80000, 128)
        BN_EPS = 1e-05
        m = jax.nn.relu(x[src])
        agg = jax.ops.segment_sum(m, dst, num_segments=N)
        h = (1.0 + eps[0]) * x + agg
        h = h @ W1.T + b1
        mu = jnp.mean(h, axis=0)
        var = jnp.var(h, axis=0)
        h = (h - mu) * jax.lax.rsqrt(var + BN_EPS) * gamma + beta
        h = jax.nn.relu(h)
        return h @ W2.T + b2

    def _L2_gnn_ref(node_feat, edge_index, edge_feat, W_edge, b_edge, W_ih, W_hh, b_ih, b_hh):
        import jax, jax.numpy as jnp
        import numpy as np
        N_NODES = 12500
        N_EDGES = 200000
        HIDDEN = 128
        N_ETYPES = 4
        N_STEPS = 4

        def _gru_cell(x, h, W_ih, W_hh, b_ih, b_hh):
            gi = x @ W_ih.T + b_ih
            gh = h @ W_hh.T + b_hh
            ir, iz, inn = jnp.split(gi, 3, axis=1)
            hr, hz, hn = jnp.split(gh, 3, axis=1)
            r = jax.nn.sigmoid(ir + hr)
            z = jax.nn.sigmoid(iz + hz)
            n = jnp.tanh(inn + r * hn)
            return (1.0 - z) * n + z * h
        etypes = jnp.argmax(edge_feat, axis=1)
        src, dst = (edge_index[0], edge_index[1])
        N = node_feat.shape[0]
        h = node_feat
        for _ in range(N_STEPS):
            trans = jnp.einsum('nd,tod->tno', h, W_edge) + b_edge[:, None, :]
            msg = trans[etypes, src]
            a = jax.ops.segment_sum(msg, dst, num_segments=N)
            h = _gru_cell(a, h, W_ih, W_hh, b_ih, b_hh)
        return h

    def _L3_gnn_ref(h, src, dst, Wq, Wk, Wv, Wo, bo, W1, b1, W2, b2, bn1_g, bn1_b, bn2_g, bn2_b):
        import jax, jax.numpy as jnp
        import numpy as np
        N, E = (6250, 100000)
        D, H = (128, 8)
        DH = D // H
        DFF = 2 * D
        EPS_BN = 1e-05

        def _batch_norm(x, g, b):
            mu = jnp.mean(x, axis=0)
            var = jnp.mean((x - mu) ** 2, axis=0)
            return (x - mu) * jax.lax.rsqrt(var + EPS_BN) * g + b
        n = h.shape[0]
        Q = (h @ Wq).reshape(n, H, DH)
        K = (h @ Wk).reshape(n, H, DH)
        V = (h @ Wv).reshape(n, H, DH)
        score = K[src] * Q[dst] / np.sqrt(DH)
        s = jnp.exp(jnp.clip(jnp.sum(score, axis=-1), -5.0, 5.0))
        s = s[..., None]
        wV = jax.ops.segment_sum(V[src] * s, dst, num_segments=n)
        z = jax.ops.segment_sum(s, dst, num_segments=n)
        h_attn = (wV / (z + 1e-06)).reshape(n, D)
        hx = h_attn @ Wo + bo
        hx = h + hx
        hx = _batch_norm(hx, bn1_g, bn1_b)
        h2 = jax.nn.relu(hx @ W1 + b1) @ W2 + b2
        hx = _batch_norm(hx + h2, bn2_g, bn2_b)
        return hx
    edge_index = jnp.stack([src, dst])
    h = jnp.maximum(_layernorm(x, axis=-1), 0.0)
    x = x + _L0_gnn_ref(h, edge_index, edge_attr_128, L0_gnn_wq, L0_gnn_bq, L0_gnn_wk, L0_gnn_bk, L0_gnn_wv, L0_gnn_bv, L0_gnn_w_ao, L0_gnn_b_ao, L0_gnn_ln1_g, L0_gnn_ln1_b, L0_gnn_w_int, L0_gnn_b_int, L0_gnn_w_out, L0_gnn_b_out, L0_gnn_ln2_g, L0_gnn_ln2_b, L0_gnn_w_ih, L0_gnn_w_hh, L0_gnn_b_ih, L0_gnn_b_hh, L0_gnn_ln3_g, L0_gnn_ln3_b)
    h = jnp.maximum(_layernorm(x, axis=-1), 0.0)
    x = x + _L1_gnn_ref(h, src, dst, L1_gnn_W1, L1_gnn_b1, L1_gnn_gamma, L1_gnn_beta, L1_gnn_W2, L1_gnn_b2, L1_gnn_eps)
    h = jnp.maximum(_layernorm(x, axis=-1), 0.0)
    x = x + _L2_gnn_ref(h, edge_index, edge_attr_4, L2_gnn_W_edge, L2_gnn_b_edge, L2_gnn_W_ih, L2_gnn_W_hh, L2_gnn_b_ih, L2_gnn_b_hh)
    h = jnp.maximum(_layernorm(x, axis=-1), 0.0)
    x = x + _L3_gnn_ref(h, src, dst, L3_gnn_Wq, L3_gnn_Wk, L3_gnn_Wv, L3_gnn_Wo, L3_gnn_bo, L3_gnn_W1, L3_gnn_b1, L3_gnn_W2, L3_gnn_b2, L3_gnn_bn1_g, L3_gnn_bn1_b, L3_gnn_bn2_g, L3_gnn_bn2_b)
    return x

_drawn_inputs = setup_inputs


def setup_inputs(seed=0):
    import zlib

    import numpy as np

    out = dict(_drawn_inputs(seed))
    spreads = {'L0_gnn_ln1_g': (1.0, 0.2),
     'L0_gnn_ln1_b': (0.0, 0.1),
     'L0_gnn_ln2_g': (1.0, 0.2),
     'L0_gnn_ln2_b': (0.0, 0.1),
     'L0_gnn_ln3_g': (1.0, 0.2),
     'L0_gnn_ln3_b': (0.0, 0.1),
     'L1_gnn_b1': (0.0, 0.8),
     'L1_gnn_gamma': (1.0, 0.2),
     'L1_gnn_beta': (0.0, 0.1),
     'L1_gnn_b2': (0.0, 0.1),
     'L3_gnn_bo': (0.0, 0.8),
     'L3_gnn_b1': (0.0, 0.46),
     'L3_gnn_b2': (0.0, 0.8),
     'L3_gnn_bn1_g': (1.0, 0.2),
     'L3_gnn_bn1_b': (0.0, 0.533),
     'L3_gnn_bn2_g': (1.0, 0.2),
     'L3_gnn_bn2_b': (0.0, 0.1)}
    factors = {'edge_attr_128': 5.797,
     'L0_gnn_wq': 2.832,
     'L0_gnn_bq': 8.0,
     'L0_gnn_wk': 2.818,
     'L0_gnn_bk': 8.0,
     'L2_gnn_b_hh': 3.368}
    for name, (base, spread) in spreads.items():
        noise = np.random.default_rng([zlib.crc32(name.encode()), seed]).standard_normal(out[name].shape)
        drawn = base * np.exp(spread * noise) if base else spread * noise
        out[name] = jnp.asarray(drawn.astype(out[name].dtype))
    for name, factor in factors.items():
        out[name] = (out[name] * factor).astype(out[name].dtype)
    return out
```

```python
from contextlib import ExitStack, contextmanager

import concourse.bass as bass
from concourse import mybir

F32 = mybir.dt.float32
I32 = mybir.dt.int32
ALU = mybir.AluOpType
ACT = mybir.ActivationFunctionType
AX_X = mybir.AxisListType.X

P = 128
N, E, D = 5000, 80000, 128
TILES = E // P
BLOCKS = -(-N // P)
NP = BLOCKS * P
FULL_BLOCKS = N // P
TAIL = N - FULL_BLOCKS * P
GROUP = 4
REGIONS = 4
ROW_C, ROW_K = 7, 96
STEPS = ROW_C * ROW_K
LOOPS = STEPS // (GROUP * REGIONS)
assert STEPS == LOOPS * GROUP * REGIONS and STEPS >= TILES + BLOCKS - 1
PADDED = STEPS + GROUP
ACC_W = 136
ACC_BLOCKS = BLOCKS + 1
CHUNK = 512
CHUNKS = NP // CHUNK
U = 5
BIG = 1.0e38
GAT_HEADS, GAT_ITERS, GAT_FF = 4, 3, 4
L3_HEADS, L2_STEPS = 8, 4
LN_EPS, BN_EPS = 1e-5, 1e-5
BN_CHUNK = N // CHUNKS


def bank4(ap):
    return ap.rearrange("p (a b) -> p a b", b=P)


def program(nc, io, out):
    ctx = ExitStack()
    with ctx:
        def sb(name, shape, dt=F32, where=ctx):
            return where.enter_context(nc.sbuf_tensor(name, shape, dt))

        def sems(*names):
            return [ctx.enter_context(nc.semaphore(n)) for n in names]

        spent = []

        @contextmanager
        def block(name, *used):
            with nc.Block(name) as b:
                cleared = [s for s in spent if s not in used]
                assert len(cleared) == len(spent), name
                spent.clear()

                @b.sync
                def _(sp):
                    for s in cleared:
                        sp.sem_clear(s)
                yield b
            spent.extend(used)

        def clear_block(name):
            with block(name):
                pass

        table_x = nc.dram_tensor("table_x", [NP, D], F32)
        table_kv = nc.dram_tensor("table_kv", [NP, 2 * D], F32)
        table_typed = nc.dram_tensor("table_typed", [NP, 4 * D], F32)
        values_dram = nc.dram_tensor("values_dram", [STEPS // GROUP, P, GROUP * D], F32)
        type_dram = nc.dram_tensor("type_dram", [TILES, P], F32)
        step_block_dram = nc.dram_tensor("step_block_dram", [1, STEPS], I32)
        step_row_dram = nc.dram_tensor("step_row_dram", [1, STEPS], I32)
        ends_dram = nc.dram_tensor("ends_dram", [3, STEPS], F32)

        ident = sb("ident", [P, P])
        iota_row = sb("iota_row", [P, P])
        ones = sb("ones", [P, P])
        (WK, WV, WQ, WAO, WINT, WOUT, GIH, GHH, GIN1, GIN2, WEDGE, GGIH, GGHH, NW) = (
            0, 1, 2, 3, 4, 8, 12, 15, 18, 19, 20, 24, 27, 30)
        wt = sb("wt", [P, NW, P])
        w3 = sb("w3", [P, 8, P])
        VEC = {}
        vec_list = [("b_ao", 1), ("ln1_g", 1), ("ln1_b", 1), ("b_int", 4), ("b_out", 1), ("ln2_g", 1), ("ln2_b", 1),
                    ("b_ih", 3), ("b_hh", 3), ("ln3_g", 1), ("ln3_b", 1), ("1_b1", 1), ("1_gamma", 1), ("1_beta", 1),
                    ("1_b2", 1), ("2_b_ih", 3), ("2_b_hh", 3), ("3_bo", 1), ("3_b1", 2), ("3_b2", 1), ("3_bn1_g", 1),
                    ("3_bn1_b", 1), ("3_bn2_g", 1), ("3_bn2_b", 1)]
        n_vec = 0
        for vname, k in vec_list:
            VEC[vname] = n_vec
            n_vec += k
        vec = sb("vec", [P, n_vec])
        gate_bias = sb("gate_bias", [P, 2, 2])
        eps_col = sb("eps_col", [P, 1])
        bq_rows = sb("bq_rows", [P, D])
        bkv_rows = sb("bkv_rows", [P, GROUP, 2 * D])
        bedge_rows = sb("bedge_rows", [P, 4 * D])
        src_idx = sb("src_idx", [P, PADDED], I32)
        typed_idx = sb("typed_idx", [P, PADDED], I32)
        dst_local = sb("dst_local", [P, PADDED])
        step_block = sb("step_block", [1, STEPS], I32)
        step_row = sb("step_row", [1, STEPS], I32)
        key_pen_f = sb("key_pen_f", [ROW_K, ROW_C * P])
        key_pen_b = sb("key_pen_b", [ROW_K, ROW_C * P])
        first_pen = sb("first_pen", [ROW_K, ROW_C, P])
        last_pen = sb("last_pen", [ROW_K, ROW_C, P])
        chain_pen = sb("chain_pen", [GAT_HEADS, 2, STEPS])
        enter_pen = sb("enter_pen", [GAT_HEADS, 2, STEPS])
        xT = sb("xT", [P, NP])
        hT = sb("hT", [P, NP])
        resT = sb("resT", [P, NP])
        t1 = sb("t1", [P, ACC_BLOCKS * D])
        acc = sb("acc", [P, ACC_BLOCKS * ACC_W])
        psum = ctx.enter_context(nc.psum_tensor("psum", [P, 8, CHUNK], F32))

        gathered = sems(*(f"gathered{r}" for r in range(REGIONS)))
        gather_go, act_go = sems("gather_go", "act_go")

        def wcol(name, k=0):
            return vec[:, VEC[name] + k:VEC[name] + k + 1]

        s_load, s_const, s_wt, s_wcopy = sems("weights_loaded", "constant_made", "weight_turned", "weight_copied")
        s_xl, s_rows = sems("x_loaded", "bias_spread")
        with ExitStack() as tmp:
            wn = sb("wn", [P, NW, P], F32, tmp)
            vrow = sb("vrow", [n_vec, P], F32, tmp)
            brow = sb("brow", [1, D + 2 * D + 4 * D + 1], F32, tmp)
            xrows = acc[:, 0:NP].rearrange("p (b f) -> p b f", f=D)
            loads = []

            def rows_of(w):
                return w.rearrange("(k p) f -> p k f", p=P)
            loads += [(wn[:, WK, :], io["L0_gnn_wk"]), (wn[:, WV, :], io["L0_gnn_wv"]), (wn[:, WQ, :], io["L0_gnn_wq"]),
                      (wn[:, WAO, :], io["L0_gnn_w_ao"]), (wn[:, WINT:WINT + 4, :], rows_of(io["L0_gnn_w_int"])),
                      (wn[:, WOUT:WOUT + 4, :], io["L0_gnn_w_out"].rearrange("p (k f) -> p k f", f=P)),
                      (wn[:, GIH:GIH + 3, :], rows_of(io["L0_gnn_w_ih"])), (wn[:, GHH:GHH + 3, :], rows_of(io["L0_gnn_w_hh"])),
                      (wn[:, GIN1, :], io["L1_gnn_W1"]), (wn[:, GIN2, :], io["L1_gnn_W2"]),
                      (wn[:, WEDGE:WEDGE + 4, :], io["L2_gnn_W_edge"].rearrange("t o d -> o t d")),
                      (wn[:, GGIH:GGIH + 3, :], rows_of(io["L2_gnn_W_ih"])), (wn[:, GGHH:GGHH + 3, :], rows_of(io["L2_gnn_W_hh"])),
                      (w3[:, 0, :], io["L3_gnn_Wq"]), (w3[:, 1, :], io["L3_gnn_Wk"]), (w3[:, 2, :], io["L3_gnn_Wv"]),
                      (w3[:, 3, :], io["L3_gnn_Wo"]), (w3[:, 4:6, :], io["L3_gnn_W1"].rearrange("p (k f) -> p k f", f=P)),
                      (w3[:, 6:8, :], rows_of(io["L3_gnn_W2"]))]
            for vname, k in vec_list:
                full = f"L{vname[0]}_gnn_{vname[2:]}" if vname[0].isdigit() else f"L0_gnn_{vname}"
                loads.append((vrow[VEC[vname]:VEC[vname] + k, :], io[full].rearrange("(k f) -> k f", f=P)))
            one_row = "(a d) -> a d"
            loads += [(brow[:, 0:D], io["L0_gnn_bq"].rearrange(one_row, a=1)),
                      (brow[:, D:2 * D], io["L0_gnn_bk"].rearrange(one_row, a=1)),
                      (brow[:, 2 * D:3 * D], io["L0_gnn_bv"].rearrange(one_row, a=1)),
                      (brow[:, 3 * D:7 * D].rearrange("a (t d) -> a t d", t=4), io["L2_gnn_b_edge"].rearrange("(a t) d -> a t d", a=1)),
                      (brow[:, 7 * D:7 * D + 1], io["L1_gnn_eps"].rearrange(one_row, a=1))]

            with block("constants", s_load, s_const, s_wt, s_wcopy, s_xl, s_rows) as b:
                @b.sync
                def _(sp):
                    for to, of in loads:
                        sp.dma_start(to, of).then_inc(s_load, 16)

                @b.gpsimd
                def _(pool):
                    pool.memset(ident[:], 0.0).then_inc(s_const, 1)
                    pool.wait_ge(s_const, 1)
                    pool.affine_select(out=ident[:], in_=ident[:], compare_op=ALU.not_equal, fill=1.0, base=0,
                                       pattern=[[-1, P]], channel_multiplier=1).then_inc(s_const, 1)
                    pool.memset(ones[:], 1.0).then_inc(s_const, 1)
                    pool.iota(iota_row[:], [[1, P]], base=0, channel_multiplier=0,
                              allow_small_or_imprecise_dtypes=True).then_inc(s_const, 1)
                    pool.memset(xrows[:, FULL_BLOCKS, :], 0.0).then_inc(s_const, 1)
                    pool.wait_ge(s_const, 5)
                    pool.dma_start(xrows[0:TAIL, FULL_BLOCKS, :], io["x"][FULL_BLOCKS * P:N, :]).then_inc(s_xl, 16)
                    pool.dma_start(xrows[:, 0:FULL_BLOCKS, :],
                                   io["x"][0:FULL_BLOCKS * P, :].rearrange("(b p) f -> p b f", p=P)).then_inc(s_xl, 16)
                    pool.wait_ge(s_xl, 32)

                n_wt = -(-NW // 4)
                n_x = BLOCKS // 4

                @b.tensor
                def _(pe):
                    pe.wait_ge(s_const, 5)
                    pe.wait_ge(s_load, 16 * len(loads))
                    for g in range(n_wt):
                        if g >= 4:
                            pe.wait_ge(s_wcopy, g - 3)
                        for k in range(4 * g, min(4 * g + 4, NW)):
                            ins = pe.transpose(psum[:, g % 4, (k % 4) * P:(k % 4 + 1) * P], wn[:, k, :], ident[:])
                        ins.then_inc(s_wt, 1)
                    pe.wait_ge(s_xl, 32)
                    for g in range(n_x):
                        pe.wait_ge(s_wcopy, n_wt + g - 3)
                        for k in range(4):
                            ins = pe.transpose(psum[:, (n_wt + g) % 4, k * P:(k + 1) * P], xrows[:, 4 * g + k, :], ident[:])
                        ins.then_inc(s_wt, 1)
                    pe.transpose(psum[:, 4, 0:n_vec], vrow[:], ident[0:n_vec, 0:n_vec])
                    pe.matmul(psum[:, 5, 0:3 * D], ones[0:1, :], brow[:, 0:3 * D], start=True, stop=True)
                    pe.matmul(psum[:, 6, :], ones[0:1, :], brow[:, 3 * D:7 * D], start=True, stop=True)
                    pe.matmul(psum[:, 7, 0:1], ones[0:1, :], brow[:, 7 * D:7 * D + 1], start=True, stop=True).then_inc(s_wt, 1)

                @b.scalar
                def _(act):
                    for g in range(n_wt):
                        n = min(4, NW - 4 * g)
                        act.wait_ge(s_wt, g + 1)
                        act.copy(wt[:, 4 * g:4 * g + n, :], bank4(psum[:, g % 4, 0:n * P])).then_inc(s_wcopy, 1)
                    for g in range(n_x):
                        act.wait_ge(s_wt, n_wt + g + 1)
                        act.copy(resT[:, g * CHUNK:(g + 1) * CHUNK], psum[:, (n_wt + g) % 4, :]).then_inc(s_wcopy, 1)

                @b.vector
                def _(dve):
                    dve.wait_ge(s_wt, n_wt + n_x + 1)
                    dve.tensor_copy(vec[:], psum[:, 4, 0:n_vec]).then_inc(s_rows, 1)
                    dve.tensor_copy(bq_rows[:], psum[:, 5, 0:D]).then_inc(s_rows, 1)
                    for u in range(GROUP):
                        dve.tensor_copy(bkv_rows[:, u, :], psum[:, 5, D:3 * D]).then_inc(s_rows, 1)
                    dve.tensor_copy(bedge_rows[:], psum[:, 6, :]).then_inc(s_rows, 1)
                    dve.tensor_scalar(eps_col[:], psum[:, 7, 0:1], 1.0, None, ALU.add).then_inc(s_rows, 1)
                    dve.wait_ge(s_rows, 1)
                    for k, (ih, hh) in enumerate((("b_ih", "b_hh"), ("2_b_ih", "2_b_hh"))):
                        dve.tensor_tensor(gate_bias[:, k, :], vec[:, VEC[ih]:VEC[ih] + 2], vec[:, VEC[hh]:VEC[hh] + 2],
                                          ALU.add).then_inc(s_rows, 1)

        s_in, s_dve, s_pe, s_mid, s_row, s_g = sems("edges_loaded", "table_step", "table_turned", "table_rows_made",
                                                    "table_rows_stored", "table_rows_gathered")
        with ExitStack() as tmp:
            per_p = E // P
            ea4 = t1[:, 0:4 * per_p].rearrange("p (e c) -> p e c", c=4)
            eq = xT[:, 0:3 * per_p].rearrange("p (c e) -> p c e", c=3)
            amax, etype = hT[:, 0:per_p], hT[:, per_p:2 * per_p]
            last_dst = sb("last_dst", [1, TILES], I32, tmp)
            last_block = sb("last_block", [1, TILES], I32, tmp)
            reach = sb("reach", [1, TILES], F32, tmp)
            tile_no = sb("tile_no", [1, TILES], F32, tmp)
            reach_all = acc[0:ROW_K, 0:TILES]
            passed = acc[0:ROW_K, TILES:2 * TILES]
            step_no = sb("step_no", [ROW_K, ROW_C], F32, tmp)
            tile_f = sb("tile_f", [ROW_K, ROW_C], F32, tmp)
            block_f = sb("block_f", [ROW_K, ROW_C], F32, tmp)
            tile_i = sb("tile_i", [ROW_K, ROW_C], I32, tmp)
            row_i = sb("row_i", [ROW_K, ROW_C], I32, tmp)
            block_i = sb("block_i", [ROW_K, ROW_C], I32, tmp)
            base_f = sb("base_f", [ROW_K, ROW_C], F32, tmp)
            src_i = sb("src_i", [ROW_K, ROW_C, P], I32, tmp)
            dst_i = sb("dst_i", [ROW_K, ROW_C, P], I32, tmp)
            typ_f = sb("typ_f", [ROW_K, ROW_C, P], F32, tmp)
            src_f = sb("src_f", [ROW_K, ROW_C, P], F32, tmp)
            dst_f = sb("dst_f", [ROW_K, ROW_C, P], F32, tmp)
            loc_f = sb("loc_f", [ROW_K, ROW_C, P], F32, tmp)
            key = sb("key", [ROW_K, ROW_C, P], F32, tmp)
            same = sb("same", [ROW_K, ROW_C, P], F32, tmp)
            ends = sb("ends", [ROW_K, 3, ROW_C], F32, tmp)
            ends_row = acc[0:GAT_HEADS, 2 * TILES:2 * TILES + 3 * STEPS].rearrange("h (a s) -> h a s", a=3)
            goes_on = acc[0:GAT_HEADS, 2 * TILES + 3 * STEPS:2 * TILES + 4 * STEPS + 1]

            with block("step_tables", s_in, s_dve, s_pe, s_mid, s_row, s_g) as b:
                @b.sync
                def _(sp):
                    sp.dma_start(ea4, io["edge_attr_4"].rearrange("(p e) c -> p e c", p=P)).then_inc(s_in, 16)
                    with nc.allow_non_contiguous_dma(reason="the last dst of each tile"):
                        sp.dma_start(last_dst[:], io["dst"].rearrange("(a t p) -> a t p", a=1, p=P)[:, :, P - 1]).then_inc(s_in, 16)
                    sp.wait_ge(s_mid, 1)
                    sp.dma_start(type_dram.ap().rearrange("t p -> (t p)").rearrange("(p e) -> p e", p=P), etype).then_inc(s_row, 16)
                    sp.wait_ge(s_mid, 2)
                    with nc.allow_non_contiguous_dma(reason="tables by step, once"):
                        sp.dma_start(step_block_dram.ap().rearrange("a (c k) -> k (a c)", k=ROW_K), block_i[:]).then_inc(s_row, 16)
                        sp.dma_start(step_row_dram.ap().rearrange("a (c k) -> k (a c)", k=ROW_K), row_i[:]).then_inc(s_row, 16)
                        sp.wait_ge(s_mid, 3)
                        sp.dma_start(ends_dram.ap().rearrange("a (c k) -> k a c", k=ROW_K), ends[:]).then_inc(s_row, 16)
                    sp.wait_ge(s_row, 64)
                    sp.dma_start(step_block[:], step_block_dram[:]).then_inc(s_in, 16)
                    sp.dma_start(step_row[:], step_row_dram[:]).then_inc(s_in, 16)
                    for h in range(GAT_HEADS):
                        sp.dma_start(ends_row[h:h + 1, :, :], ends_dram.ap().rearrange("(o a) s -> o a s", o=1)).then_inc(s_in, 16)
                    sp.wait_ge(s_in, 32 + 32 + 16 * GAT_HEADS)

                @b.gpsimd
                def _(pool):
                    pool.iota(tile_no[:], [[1, TILES]], base=0, channel_multiplier=0,
                              allow_small_or_imprecise_dtypes=True).then_inc(s_pe, 1)
                    pool.iota(step_no[:], [[ROW_K, ROW_C]], base=0, channel_multiplier=1,
                              allow_small_or_imprecise_dtypes=True).then_inc(s_pe, 1)
                    pool.wait_ge(s_mid, 2)
                    for c in range(ROW_C):
                        at = bass.IndirectOffsetOnAxis(ap=tile_i[:, c:c + 1], axis=0)
                        pool.indirect_dma_start(out=src_i[:, c, :], out_offset=None, in_=io["src"].rearrange("(t p) -> t p", p=P),
                                                in_offset=at).then_inc(s_g, 16)
                        pool.indirect_dma_start(out=dst_i[:, c, :], out_offset=None, in_=io["dst"].rearrange("(t p) -> t p", p=P),
                                                in_offset=at).then_inc(s_g, 16)
                    pool.wait_ge(s_row, 64)
                    for c in range(ROW_C):
                        at = bass.IndirectOffsetOnAxis(ap=tile_i[:, c:c + 1], axis=0)
                        pool.indirect_dma_start(out=typ_f[:, c, :], out_offset=None, in_=type_dram[:], in_offset=at).then_inc(s_g, 16)

                @b.vector
                def _(dve):
                    n = [0]

                    def link(ins):
                        n[0] += 1
                        ins.then_inc(s_dve, 1)
                        dve.wait_ge(s_dve, n[0])

                    dve.wait_ge(s_in, 32)
                    dve.wait_ge(s_pe, 2)
                    link(dve.tensor_scalar(last_block[:], last_dst[:], P.bit_length() - 1, None, ALU.logical_shift_right))
                    link(dve.tensor_copy(reach[:], last_block[:]))
                    link(dve.tensor_tensor(reach[:], reach[:], tile_no[:], ALU.add))
                    dve.wait_ge(s_pe, 3)
                    link(dve.tensor_copy(reach_all[:, 0:CHUNK], psum[0:ROW_K, 0, :]))
                    link(dve.tensor_copy(reach_all[:, CHUNK:TILES], psum[0:ROW_K, 1, 0:TILES - CHUNK]))
                    for c in range(ROW_C):
                        link(dve.tensor_scalar(passed, reach_all, step_no[:, c:c + 1], None, ALU.is_lt))
                        link(dve.tensor_reduce(tile_f[:, c:c + 1], passed, AX_X, ALU.add))
                    link(dve.tensor_scalar(tile_f[:], tile_f[:], float(TILES - 1), None, ALU.min))
                    link(dve.tensor_tensor(block_f[:], step_no[:], tile_f[:], ALU.subtract))
                    link(dve.tensor_scalar(block_f[:], block_f[:], float(BLOCKS), None, ALU.min))
                    link(dve.tensor_scalar(base_f[:], tile_f[:], float(P), None, ALU.mult))
                    link(dve.tensor_copy(row_i[:], base_f[:]))
                    link(dve.tensor_scalar(base_f[:], block_f[:], float(P), None, ALU.mult))
                    link(dve.tensor_copy(tile_i[:], tile_f[:]))
                    link(dve.tensor_reduce(amax, ea4, AX_X, ALU.max))
                    for t in range(3):
                        link(dve.tensor_tensor(eq[:, t, :], ea4[:, :, t], amax, ALU.is_equal))
                    link(dve.tensor_scalar(etype, eq[:, 2, :], -1.0, 2.0, ALU.mult, ALU.add))
                    for t in (1, 0):
                        link(dve.tensor_scalar(eq[:, t, :], eq[:, t, :], -1.0, 1.0, ALU.mult, ALU.add))
                        link(dve.tensor_tensor(etype, etype, eq[:, t, :], ALU.mult))
                        if t == 1:
                            link(dve.tensor_scalar(etype, etype, 1.0, None, ALU.add))
                    dve.sem_inc(s_mid, 1)
                    dve.tensor_copy(block_i[:], block_f[:]).then_inc(s_mid, 1)
                    dve.wait_ge(s_g, 16 * 2 * ROW_C)
                    link(dve.tensor_copy(src_f[:], src_i[:]))
                    link(dve.tensor_copy(dst_f[:], dst_i[:]))
                    for c in range(ROW_C):
                        link(dve.tensor_scalar(loc_f[:, c, :], dst_f[:, c, :], base_f[:, c:c + 1], None, ALU.subtract))
                    link(dve.tensor_scalar(key[:], loc_f[:], 0.0, None, ALU.is_ge))
                    link(dve.tensor_scalar(same[:], loc_f[:], float(P - 1), None, ALU.is_le))
                    link(dve.tensor_tensor(key[:], key[:], same[:], ALU.mult))
                    link(dve.tensor_scalar(dst_f[:], dst_f[:], 1.0, None, ALU.add))
                    link(dve.tensor_tensor(key[:], key[:], dst_f[:], ALU.mult))
                    link(dve.tensor_scalar(key[:], key[:], -1.0, None, ALU.add))
                    link(dve.memset(same[:], 1.0))
                    link(dve.tensor_tensor(same[:, :, 1:P], key[:, :, 1:P], key[:, :, 0:P - 1], ALU.is_equal))
                    link(dve.tensor_reduce(ends[:, 2, :], same[:], AX_X, ALU.min))
                    link(dve.tensor_copy(ends[:, 0, :], key[:, :, 0]))
                    link(dve.tensor_copy(ends[:, 1, :], key[:, :, P - 1]))
                    dve.sem_inc(s_mid, 1)
                    pf = key_pen_f[:].rearrange("k (c p) -> k c p", p=P)
                    pb = key_pen_b[:].rearrange("k (c p) -> k c p", p=P)
                    link(dve.memset(key_pen_f[:], -BIG))
                    link(dve.memset(key_pen_b[:], -BIG))
                    link(dve.tensor_scalar(pf[:, :, 1:P], same[:, :, 1:P], 1.0, BIG, ALU.subtract, ALU.mult))
                    link(dve.tensor_scalar(pb[:, :, 0:P - 1], same[:, :, 1:P], 1.0, BIG, ALU.subtract, ALU.mult))
                    for c in range(ROW_C):
                        for to, end in ((first_pen, 0), (last_pen, 1)):
                            link(dve.tensor_scalar(to[:, c, :], key[:, c, :], ends[:, end, c:c + 1], 1.0, ALU.is_equal, ALU.subtract))
                            link(dve.tensor_scalar(to[:, c, :], to[:, c, :], BIG, None, ALU.mult))
                    dve.wait_ge(s_in, 32 + 32 + 16 * GAT_HEADS)
                    link(dve.memset(goes_on, 0.0))
                    link(dve.tensor_tensor(goes_on[:, 1:STEPS], ends_row[:, 0, 1:STEPS], ends_row[:, 1, 0:STEPS - 1], ALU.is_equal))
                    for d in range(2):
                        link(dve.tensor_scalar(enter_pen[:, d, :], goes_on[:, d:STEPS + d], 1.0, BIG, ALU.subtract, ALU.mult))
                        link(dve.tensor_tensor(chain_pen[:, d, :], goes_on[:, d:STEPS + d], ends_row[:, 2, :], ALU.mult))
                        link(dve.tensor_scalar(chain_pen[:, d, :], chain_pen[:, d, :], 1.0, BIG, ALU.subtract, ALU.mult))
                    dve.wait_ge(s_g, 16 * 3 * ROW_C)
                    link(dve.scalar_tensor_tensor(out=typ_f[:], in0=src_f[:], scalar=4.0, in1=typ_f[:], op0=ALU.mult, op1=ALU.add))
                    link(dve.memset(dst_local[:, STEPS:PADDED], -1.0))
                    link(dve.memset(src_idx[:, STEPS:PADDED], 0))
                    dve.sem_inc(s_mid, 1)
                    for k, (to, of) in enumerate(((src_idx, 2), (typed_idx, 4), (dst_local, 6))):
                        dve.wait_ge(s_pe, 4 + k)
                        n_bank = CHUNK // ROW_K
                        link(dve.tensor_copy(to[:, 0:n_bank * ROW_K], psum[:, of, 0:n_bank * ROW_K]))
                        link(dve.tensor_copy(to[:, n_bank * ROW_K:STEPS], psum[:, of + 1, 0:STEPS - n_bank * ROW_K]))

                @b.tensor
                def _(pe):
                    pe.wait_ge(s_dve, 3)
                    pe.matmul(psum[0:ROW_K, 0, :], ones[0:1, 0:ROW_K], reach[:, 0:CHUNK], start=True, stop=True)
                    pe.matmul(psum[0:ROW_K, 1, 0:TILES - CHUNK], ones[0:1, 0:ROW_K], reach[:, CHUNK:TILES],
                              start=True, stop=True).then_inc(s_pe, 1)
                    pe.wait_ge(s_mid, 4)
                    n_bank = CHUNK // ROW_K
                    for of, bank in ((src_f, 2), (typ_f, 4), (loc_f, 6)):
                        for c in range(ROW_C):
                            at = (c % n_bank) * ROW_K
                            ins = pe.transpose(psum[:, bank + c // n_bank, at:at + ROW_K], of[:, c, :], ident[0:ROW_K, 0:ROW_K])
                        ins.then_inc(s_pe, 1)

        def at_least(eng, sem, value):
            if not (isinstance(value, int) and value <= 0):
                eng.wait_ge(sem, value)

        def turns(eng, body):
            body(0)
            with eng.Fori(1, LOOPS - 1) as i:
                body(i)
            body(LOOPS - 1)

        def led(i, r, lead=2):
            i2, r2 = i + (r + lead) // REGIONS, (r + lead) % REGIONS
            return None if isinstance(i2, int) and i2 >= LOOPS else (i2, r2)

        def step_of(i, r, u=0):
            return i * (REGIONS * GROUP) + (r * GROUP + u)

        def region_of(i, r):
            return i * REGIONS + r

        ROWS = LOOPS * GROUP * 16

        def landed(i, base):
            return base + (i + 1) * (GROUP * 16)

        def acc_rows(c, lo, n):
            return acc[:, bass.ds(c * (4 * ACC_W), 4 * ACC_W)].rearrange("p (b w) -> p b w", w=ACC_W)[:, :, lo:lo + n]

        def cols(c):
            return bass.ds(c * CHUNK, CHUNK)

        V = 2
        def pairs(eng, *stages):
            def turn(i):
                for stage in stages:
                    for u in range(V):
                        stage(i * V + u, u, i)
            turn(0)
            with eng.Fori(1, CHUNKS // V) as i:
                turn(i)

        ln_summed, ln_centred, ln_squared, ln_varied, ln_rooted, ln_step = sems(
            "ln_summed", "ln_centred", "ln_squared", "ln_varied", "ln_rooted", "ln_step")

        def layer_norm(name, src, dst, eps, gain=None, shift=None, also=None):
            with ExitStack() as tmp:
                xc = acc[:, 0:U * CHUNK].rearrange("p (u f) -> p u f", u=U)
                sq = acc[:, U * CHUNK:2 * U * CHUNK].rearrange("p (u f) -> p u f", u=U)
                std = sb(f"{name}_std", [P, U, CHUNK], F32, tmp)
                eps_t = sb(f"{name}_eps", [P, 1], F32, tmp)
                with block(name, ln_summed, ln_centred, ln_squared, ln_varied, ln_rooted, ln_step) as b:
                    @b.tensor
                    def _(pe):
                        with pe.Fori(0, CHUNKS // U) as i:
                            for u in range(U):
                                if u >= 4:
                                    pe.wait_ge(ln_centred, i * U + (u - 3))
                                pe.matmul(psum[:, u % 4, :], ones[:], src[:, cols(i * U + u)], start=True, stop=True).then_inc(ln_summed, 1)
                            for u in range(U):
                                pe.wait_ge(ln_squared, i * U + (u + 1))
                                if u >= 4:
                                    pe.wait_ge(ln_rooted, i * U + (u - 3))
                                pe.matmul(psum[:, 4 + u % 4, :], ones[:], sq[:, u, :], start=True, stop=True).then_inc(ln_varied, 1)
                            pe.wait_ge(ln_rooted, i * U + U)

                    @b.scalar
                    def _(act):
                        act.wait_ge(ln_step, 1)
                        with act.Fori(0, CHUNKS // U) as i:
                            for u in range(U):
                                act.wait_ge(ln_centred, i * U + (u + 1))
                                act.activation(sq[:, u, :], xc[:, u, :], ACT.Square).then_inc(ln_squared, 1)
                            for u in range(U):
                                act.wait_ge(ln_varied, i * U + (u + 1))
                                act.activation(std[:, u, :], psum[:, 4 + u % 4, :], ACT.Sqrt, bias=eps_t[:],
                                               scale=1.0 / D).then_inc(ln_rooted, 1)

                    @b.vector
                    def _(dve):
                        dve.memset(eps_t[:], eps).then_inc(ln_step, 1)
                        n_step = (2 if also is None else 3) * U + U
                        with dve.Fori(0, CHUNKS // U) as i:
                            dve.wait_ge(ln_step, i * n_step + 1)
                            for u in range(U):
                                dve.wait_ge(ln_summed, i * U + (u + 1))
                                dve.scalar_tensor_tensor(out=xc[:, u, :], in0=psum[:, u % 4, :], scalar=-1.0 / D, in1=src[:, cols(i * U + u)],
                                                         op0=ALU.mult, op1=ALU.add).then_inc(ln_centred, 1)
                            for u in range(U):
                                dve.wait_ge(ln_rooted, i * U + (u + 1))
                                dve.reciprocal(std[:, u, :], std[:, u, :]).then_inc(ln_step, 1)
                            for u in range(U):
                                dve.wait_ge(ln_step, i * n_step + (u + 2))
                                dve.tensor_tensor(xc[:, u, :], xc[:, u, :], std[:, u, :], ALU.mult).then_inc(ln_step, 1)
                            for u in range(U):
                                dve.wait_ge(ln_step, i * n_step + (U + u + 2))
                                for to in [dst] + ([also] if also is not None else []):
                                    if gain is None:
                                        ins = dve.tensor_scalar(to[:, cols(i * U + u)], xc[:, u, :], 0.0, None, ALU.max)
                                    else:
                                        ins = dve.tensor_scalar(to[:, cols(i * U + u)], xc[:, u, :], gain, shift, ALU.mult, ALU.add)
                                    ins.then_inc(ln_step, 1)

        r_staged, r_turned, r_copied, r_query = sems("rows_staged", "rows_turned", "rows_copied", "rows_query")
        r_stored = sems(*(f"rows_stored{u}" for u in range(V)))

        def node_rows(name, src, queries):
            with ExitStack() as tmp:
                xs = sb(f"{name}_xs", [P, V, CHUNK], F32, tmp)
                rows = sb(f"{name}_rows", [P, V, CHUNK], F32, tmp)
                with block(name, r_staged, r_turned, r_copied, r_query, *r_stored) as b:
                    @b.vector
                    def _(dve):
                        def stage(c, u, i):
                            at_least(dve, r_turned, c + 1 - V)
                            dve.tensor_scalar(xs[:, u, :], src[:, cols(c)], 0.0, None, ALU.add).then_inc(r_staged, 1)

                        def query(c, u, i):
                            dve.wait_ge(r_turned, c + 1)
                            dve.tensor_tensor(bank4(t1[:, cols(c)]), bank4(psum[:, 4 + u, :]),
                                              bq_rows[:].unsqueeze(1).broadcast_to([P, 4, P]), ALU.add).then_inc(r_query, 1)
                        dve.memset(t1[:, NP:], 0.0)
                        pairs(dve, *([stage, query] if queries else [stage]))

                    @b.tensor
                    def _(pe):
                        def turn(c, u, i):
                            pe.wait_ge(r_staged, c + 1)
                            at_least(pe, r_copied, c + 1 - V)
                            if queries:
                                at_least(pe, r_query, c + 1 - V)
                            for k in range(4):
                                at = slice(k * P, (k + 1) * P)
                                ins = pe.transpose(psum[:, u, at], xs[:, u, at], ident[:])
                                if queries:
                                    ins = pe.matmul(psum[:, 4 + u, at], xs[:, u, at], wt[:, WQ, :], start=True, stop=True)
                            ins.then_inc(r_turned, 1)
                        pairs(pe, turn)

                    @b.scalar
                    def _(act):
                        def copy(c, u, i):
                            act.wait_ge(r_turned, c + 1)
                            at_least(act, r_stored[u], i * 16)
                            act.copy(rows[:, u, :], psum[:, u, :]).then_inc(r_copied, 1)
                        pairs(act, copy)

                    @b.sync
                    def _(sp):
                        def leave(c, u, i):
                            sp.wait_ge(r_copied, c + 1)
                            sp.dma_start(table_x[cols(c), :].rearrange("(b p) f -> p b f", p=P), bank4(rows[:, u, :])).then_inc(r_stored[u], 16)
                        pairs(sp, leave)
                        for stored in r_stored:
                            sp.wait_ge(stored, 16 * (CHUNKS // V))

        def projected_rows(name, src, rhs, width, table, bias=None, query_width=0):
            left = width - query_width
            with ExitStack() as tmp:
                xs = sb(f"{name}_xs", [P, V, CHUNK], F32, tmp)
                rows = sb(f"{name}_rows", [P, V, 4, left], F32, tmp)
                with block(name, r_staged, r_turned, r_copied, r_query, *r_stored) as b:
                    @b.vector
                    def _(dve):
                        def stage(c, u, i):
                            at_least(dve, r_turned, (c + 1 - V) * 4)
                            dve.tensor_scalar(xs[:, u, :], src[:, cols(c)], 0.0, None, ALU.add).then_inc(r_staged, 1)

                        def add_bias(c, u, i):
                            at_least(dve, r_stored[u], i * 16)
                            for k in range(4):
                                dve.wait_ge(r_turned, c * 4 + (k + 1))
                                dve.tensor_tensor(rows[:, u, k, :], psum[:, 4 * u + k, 0:left], bias, ALU.add).then_inc(r_copied, 1)

                        def query(c, u, i):
                            for k in range(4):
                                dve.wait_ge(r_turned, c * 4 + (k + 1))
                                dve.tensor_scalar(t1[:, bass.ds(c * CHUNK + k * P, P)], psum[:, 4 * u + k, 0:query_width],
                                                  0.0, None, ALU.add).then_inc(r_query, 1)
                        dve.memset(t1[:, NP:], 0.0)
                        pairs(dve, stage, add_bias if bias is not None else query)

                    @b.tensor
                    def _(pe):
                        def project(c, u, i):
                            pe.wait_ge(r_staged, c + 1)
                            for k in range(4):
                                at_least(pe, r_copied, (c - V) * 4 + (k + 1))
                                if query_width:
                                    at_least(pe, r_query, (c - V) * 4 + (k + 1))
                                pe.matmul(psum[:, 4 * u + k, 0:width], xs[:, u, k * P:(k + 1) * P], rhs, start=True, stop=True).then_inc(r_turned, 1)
                        pairs(pe, project)

                    if bias is None:
                        @b.scalar
                        def _(act):
                            def copy(c, u, i):
                                at_least(act, r_stored[u], i * 16)
                                for k in range(4):
                                    act.wait_ge(r_query, c * 4 + (k + 1))
                                    act.copy(rows[:, u, k, :], psum[:, 4 * u + k, query_width:width]).then_inc(r_copied, 1)
                            pairs(act, copy)

                    @b.sync
                    def _(sp):
                        def leave(c, u, i):
                            sp.wait_ge(r_copied, c * 4 + 4)
                            sp.dma_start(table[cols(c), :].rearrange("(b p) f -> p b f", p=P), rows[:, u, :, :]).then_inc(r_stored[u], 16)
                        pairs(sp, leave)
                        for stored in r_stored:
                            sp.wait_ge(stored, 16 * (CHUNKS // V))

        p_index, p_selected, p_mixed, p_turned, p_spread, p_projected = sems(
            "index_copied", "selected", "mixed", "edges_turned", "turned_copied", "projected")
        p_evacuated, p_multiplied, p_scored, p_score_kept = sems("evacuated", "multiplied", "scored", "score_kept")
        p_weight, p_weighted, p_summed, p_added = sems("weight_placed", "weighted", "summed", "added")
        p_in = sems(*(f"edge_rows_in{r}" for r in range(REGIONS)))
        p_out = sems(*(f"values_out{r}" for r in range(REGIONS)))
        select = sb("select", [P, REGIONS, GROUP, P])
        index = sb("index", [P, REGIONS, GROUP], I32)
        score = sb("score", [P, STEPS, GAT_HEADS])

        def copy_index(act, table, i, r, base):
            if not (isinstance(i, int) and i == 0):
                act.wait_ge(gathered[r], landed(i - 1, base))
            act.copy(index[:, r, :], table[:, bass.ds(step_of(i, r), GROUP)]).then_inc(p_index, 1)

        def gather(pool, ring, table, i, r, freed):
            at_least(pool, freed, region_of(i, r) - (REGIONS - 1))
            pool.sem_inc(gather_go, 1)
            pool.wait_ge(p_index, region_of(i, r) + 1)
            pool.sem_inc(gather_go, 1)
            for u in range(GROUP):
                pool.indirect_dma_start(out=ring[:, r, u, :], out_offset=None, in_=table,
                                        in_offset=bass.IndirectOffsetOnAxis(ap=index[:, r, u:u + 1], axis=0)).then_inc(gathered[r], 16)

        def make_select(dve, i, r):
            for u in range(GROUP):
                ins = dve.tensor_scalar(select[:, r, u, :], iota_row[:], dst_local[:, bass.ds(step_of(i, r, u), 1)], None, ALU.is_equal)
            ins.then_inc(p_selected, 1)

        def block_of(eng, i, r, u):
            return eng.value_load(step_block[0:1, bass.ds(step_of(i, r, u), 1)], min_val=0, max_val=BLOCKS)

        def add_blocks(dve, sums, i, r, width):
            dve.wait_ge(p_summed, region_of(i, r) + 1)
            for u in range(GROUP):
                to = acc[:, bass.ds(block_of(dve, i, r, u) * ACC_W, width)]
                at_least(dve, p_added, region_of(i, r) * GROUP + u)
                dve.tensor_tensor(to, to, sums(r, u), ALU.add).then_inc(p_added, 1)

        def sum_pass(name, table, idx, base):
            with ExitStack() as tmp:
                ring = sb(f"{name}_ring", [P, REGIONS, GROUP, D], F32, tmp)

                def sums(r, u):
                    return psum[:, r, u * P:(u + 1) * P]

                with block(name, p_index, p_selected, p_summed, p_added) as b:
                    @b.gpsimd
                    def _(pool):
                        turns(pool, lambda i: [gather(pool, ring, table, i, r, p_summed) for r in range(REGIONS)])

                    @b.scalar
                    def _(act):
                        turns(act, lambda i: [copy_index(act, idx, i, r, base) for r in range(REGIONS)])

                    @b.vector
                    def _(dve):
                        dve.memset(acc[:], 0.0)
                        make_select(dve, 0, 0)
                        def body(i):
                            for r in range(REGIONS):
                                if nxt := led(i, r, 1):
                                    make_select(dve, *nxt)
                                add_blocks(dve, sums, i, r, D)
                        turns(dve, body)

                    @b.tensor
                    def _(pe):
                        def body(i):
                            for r in range(REGIONS):
                                pe.wait_ge(p_selected, region_of(i, r) + 1)
                                pe.wait_ge(gathered[r], landed(i, base))
                                at_least(pe, p_added, (region_of(i, r) - (REGIONS - 1)) * GROUP)
                                for u in range(GROUP):
                                    ins = pe.matmul(sums(r, u), select[:, r, u, :], ring[:, r, u, :], start=True, stop=True)
                                ins.then_inc(p_summed, 1)
                        turns(pe, body)

        def gat_score_pass(name, base):
            with ExitStack() as tmp:
                RING = REGIONS * GROUP * D
                ring = acc[:, 0:RING].rearrange("p (r u f) -> p r u f", r=REGIONS, u=GROUP)
                attr = acc[:, RING:2 * RING].rearrange("p (r u f) -> p r u f", r=REGIONS, u=GROUP)
                spread = sb(f"{name}_spread", [P, 2, GROUP, P], F32, tmp)
                mixT = sb(f"{name}_mixT", [P, 2, GROUP, P], F32, tmp)
                kv = sb(f"{name}_kv", [P, 2, GROUP, 2 * D], F32, tmp)
                part = sb(f"{name}_part", [P, REGIONS, GROUP, GAT_HEADS], F32, tmp)

                def kv_banks(r):
                    return psum[:, 2 + 2 * (r % 2):4 + 2 * (r % 2), :].rearrange("p a b -> p (a b)").rearrange("p (u w) -> p u w", w=2 * D)

                def q_bank(r):
                    return psum[:, 6 + r % 2, :]

                with block(name, p_index, p_selected, p_mixed, p_turned, p_spread, p_projected, p_evacuated, p_multiplied, p_scored,
                           p_score_kept, *p_in, *p_out) as b:
                    @b.gpsimd
                    def _(pool):
                        turns(pool, lambda i: [gather(pool, ring, table_x[:], i, r, p_turned) for r in range(REGIONS)])

                    @b.sync
                    def _(sp):
                        def load(i, r):
                            at_least(sp, p_mixed, region_of(i, r) - (REGIONS - 1))
                            for u in range(GROUP):
                                row = sp.value_load(step_row[0:1, bass.ds(step_of(i, r, u), 1)], min_val=0, max_val=E - P)
                                sp.dma_start(attr[:, r, u, :], io["edge_attr_128"][bass.ds(row, P), :]).then_inc(p_in[r], 16)

                        def body(i):
                            for r in range(REGIONS):
                                if nxt := led(i, r):
                                    load(*nxt)
                                sp.wait_ge(p_evacuated, region_of(i, r) + 1)
                                sp.dma_start(values_dram[bass.ds(region_of(i, r), 1), :, :].rearrange("a p (u f) -> (a p) u f", f=D),
                                             kv[:, r % 2, :, D:2 * D]).then_inc(p_out[r], 16)
                        load(0, 0)
                        load(0, 1)
                        turns(sp, body)
                        for r in range(REGIONS):
                            sp.wait_ge(p_out[r], 16 * LOOPS)

                    @b.scalar
                    def _(act):
                        def turned(i, r):
                            act.wait_ge(p_turned, region_of(i, r) + 1)
                            act.copy(spread[:, r % 2, :, :], bank4(psum[:, 0, :]))
                            act.copy(mixT[:, r % 2, :, :], bank4(psum[:, 1, :])).then_inc(p_spread, 1)

                        def body(i):
                            for r in range(REGIONS):
                                if nxt := led(i, r):
                                    copy_index(act, src_idx, *nxt, base)
                                    turned(*nxt)
                                act.wait_ge(p_scored, region_of(i, r) + 1)
                                act.copy(score[:, bass.ds(step_of(i, r), GROUP), :], part[:, r, :, :]).then_inc(p_score_kept, 1)
                        copy_index(act, src_idx, 0, 0, base)
                        copy_index(act, src_idx, 0, 1, base)
                        turned(0, 0)
                        turned(0, 1)
                        turns(act, body)

                    @b.vector
                    def _(dve):
                        def lead(i, r):
                            make_select(dve, i, r)
                            dve.wait_ge(gathered[r], landed(i, base))
                            dve.wait_ge(p_in[r], (i + 1) * (16 * GROUP))
                            dve.tensor_tensor(ring[:, r, :, :], ring[:, r, :, :], attr[:, r, :, :], ALU.add).then_inc(p_mixed, 1)

                        def body(i):
                            for r in range(REGIONS):
                                if nxt := led(i, r):
                                    lead(*nxt)
                                j = region_of(i, r)
                                dve.wait_ge(p_projected, j + 1)
                                before = led(i, r, -2)
                                if not (isinstance(before[0], int) and before[0] < 0):
                                    dve.wait_ge(p_out[before[1]], (before[0] + 1) * 16)
                                dve.tensor_tensor(kv[:, r % 2, :, :], kv_banks(r), bkv_rows[:], ALU.add).then_inc(p_evacuated, 1)
                                dve.wait_ge(p_evacuated, j + 1)
                                dve.tensor_tensor(select[:, r, :, :], kv[:, r % 2, :, 0:D], bank4(q_bank(r)), ALU.mult).then_inc(p_multiplied, 1)
                                at_least(dve, p_score_kept, j - (REGIONS - 1))
                                dve.wait_ge(p_multiplied, j + 1)
                                dve.tensor_reduce(part[:, r, :, :], select[:, r, :, :].rearrange("p u (h e) -> p u h e", h=GAT_HEADS),
                                                  AX_X, ALU.add).then_inc(p_scored, 1)
                        lead(0, 0)
                        lead(0, 1)
                        turns(dve, body)

                    @b.tensor
                    def _(pe):
                        def turn(i, r):
                            j = region_of(i, r)
                            pe.wait_ge(p_selected, j + 1)
                            at_least(pe, p_spread, j)
                            for u in range(GROUP):
                                pe.transpose(psum[:, 0, u * P:(u + 1) * P], select[:, r, u, :], ident[:])
                            pe.wait_ge(p_mixed, j + 1)
                            for u in range(GROUP):
                                ins = pe.transpose(psum[:, 1, u * P:(u + 1) * P], ring[:, r, u, :], ident[:])
                            ins.then_inc(p_turned, 1)

                        def body(i):
                            for r in range(REGIONS):
                                j = region_of(i, r)
                                pe.wait_ge(p_spread, j + 1)
                                at_least(pe, p_multiplied, j - 1)
                                for u in range(GROUP):
                                    pe.matmul(kv_banks(r)[:, u, :], mixT[:, r % 2, u, :], wt[:, WK:WK + 2, :].rearrange("p a b -> p (a b)"),
                                              start=True, stop=True)
                                for u in range(GROUP):
                                    q = t1[:, bass.ds(block_of(pe, i, r, u) * D, D)]
                                    ins = pe.matmul(q_bank(r)[:, u * P:(u + 1) * P], spread[:, r % 2, u, :], q, start=True, stop=True)
                                ins.then_inc(p_projected, 1)
                                if nxt := led(i, r):
                                    turn(*nxt)
                        turn(0, 0)
                        turn(0, 1)
                        turns(pe, body)

        def gat_value_pass(name):
            W = D + GAT_HEADS
            with ExitStack() as tmp:
                ring = sb(f"{name}_ring", [P, REGIONS, GROUP, D], F32, tmp)
                msg = sb(f"{name}_msg", [P, REGIONS, GROUP, W], F32, tmp)

                def sums(r, u):
                    return psum[:, 2 * r + u // 2, (u % 2) * W:(u % 2 + 1) * W]

                with block(name, p_selected, p_weight, p_weighted, p_summed, p_added, *p_in) as b:
                    @b.sync
                    def _(sp):
                        def body(i):
                            for r in range(REGIONS):
                                at_least(sp, p_weighted, region_of(i, r) - (REGIONS - 1))
                                sp.dma_start(ring[:, r, :, :], values_dram[bass.ds(region_of(i, r), 1), :, :].rearrange(
                                    "a p (u f) -> (a p) u f", f=D)).then_inc(p_in[r], 16)
                        turns(sp, body)

                    @b.scalar
                    def _(act):
                        def body(i):
                            for r in range(REGIONS):
                                at_least(act, p_summed, region_of(i, r) - (REGIONS - 1))
                                act.copy(msg[:, r, :, D:W], score[:, bass.ds(step_of(i, r), GROUP), :]).then_inc(p_weight, 1)
                        turns(act, body)

                    @b.vector
                    def _(dve):
                        dve.memset(acc[:], 0.0)
                        make_select(dve, 0, 0)
                        def body(i):
                            for r in range(REGIONS):
                                dve.wait_ge(p_in[r], (i + 1) * 16)
                                dve.wait_ge(p_weight, region_of(i, r) + 1)
                                for u in range(GROUP):
                                    ins = dve.tensor_tensor(msg[:, r, u, 0:D].rearrange("p (h e) -> p h e", h=GAT_HEADS),
                                                            ring[:, r, u, :].rearrange("p (h e) -> p h e", h=GAT_HEADS),
                                                            msg[:, r, u, D:W].unsqueeze(2).broadcast_to([P, GAT_HEADS, D // GAT_HEADS]), ALU.mult)
                                ins.then_inc(p_weighted, 1)
                                if nxt := led(i, r, 1):
                                    make_select(dve, *nxt)
                                last = led(i, r, -1)
                                if not (isinstance(last[0], int) and last[0] < 0):
                                    add_blocks(dve, sums, *last, W)
                        turns(dve, body)
                        add_blocks(dve, sums, LOOPS - 1, REGIONS - 1, W)

                    @b.tensor
                    def _(pe):
                        def body(i):
                            for r in range(REGIONS):
                                pe.wait_ge(p_selected, region_of(i, r) + 1)
                                pe.wait_ge(p_weighted, region_of(i, r) + 1)
                                at_least(pe, p_added, (region_of(i, r) - (REGIONS - 1)) * GROUP)
                                for u in range(GROUP):
                                    ins = pe.matmul(sums(r, u), select[:, r, u, :], msg[:, r, u, :], start=True, stop=True)
                                ins.then_inc(p_summed, 1)
                        turns(pe, body)

        def transformer_pass(name, base):
            W = D + L3_HEADS
            HD = D // L3_HEADS
            with ExitStack() as tmp:
                ring = sb(f"{name}_ring", [P, REGIONS, GROUP, 2 * D], F32, tmp)
                part = sb(f"{name}_part", [P, 2, GROUP, L3_HEADS], F32, tmp)
                room = score[:].rearrange("p s h -> p (s h)")
                spread = room[:, 0:2 * GROUP * P].rearrange("p (a u f) -> p a u f", a=2, u=GROUP)
                prod = room[:, 2 * GROUP * P:3 * GROUP * P].rearrange("p (u f) -> p u f", u=GROUP)
                msg = room[:, 3 * GROUP * P:3 * GROUP * P + 2 * GROUP * W].rearrange("p (a u f) -> p a u f", a=2, u=GROUP)

                def q_bank(r):
                    return psum[:, 1 + r % 2, :]

                def sums(r, u):
                    return psum[:, 4 + 2 * (r % 2) + u // 2, (u % 2) * W:(u % 2 + 1) * W]

                with block(name, p_index, p_selected, p_turned, p_spread, p_projected, p_multiplied, p_evacuated, p_scored,
                           p_weight, p_weighted, p_summed, p_added) as b:
                    @b.gpsimd
                    def _(pool):
                        turns(pool, lambda i: [gather(pool, ring, table_kv[:], i, r, p_weighted) for r in range(REGIONS)])

                    @b.scalar
                    def _(act):
                        def turned(i, r):
                            act.wait_ge(p_turned, region_of(i, r) + 1)
                            act.copy(spread[:, r % 2, :, :], bank4(psum[:, 0, :])).then_inc(p_spread, 1)

                        def body(i):
                            for r in range(REGIONS):
                                if nxt := led(i, r):
                                    copy_index(act, src_idx, *nxt, base)
                                    turned(*nxt)
                                act.wait_ge(p_scored, region_of(i, r) + 1)
                                at_least(act, p_summed, region_of(i, r) - 1)
                                act.activation(msg[:, r % 2, :, D:W], part[:, r % 2, :, :], ACT.Exp, scale=HD ** -0.5).then_inc(p_weight, 1)
                        copy_index(act, src_idx, 0, 0, base)
                        copy_index(act, src_idx, 0, 1, base)
                        turned(0, 0)
                        turned(0, 1)
                        turns(act, body)

                    @b.vector
                    def _(dve):
                        dve.memset(acc[:], 0.0)
                        def body(i):
                            for r in range(REGIONS):
                                j = region_of(i, r)
                                if nxt := led(i, r):
                                    make_select(dve, *nxt)
                                dve.wait_ge(p_projected, j + 1)
                                dve.wait_ge(gathered[r], landed(i, base))
                                dve.tensor_tensor(prod, ring[:, r, :, 0:D], bank4(q_bank(r)), ALU.mult).then_inc(p_multiplied, 1)
                                dve.wait_ge(p_multiplied, j + 1)
                                dve.tensor_reduce(part[:, r % 2, :, :], prod.rearrange("p u (h e) -> p u h e", h=L3_HEADS),
                                                  AX_X, ALU.add).then_inc(p_evacuated, 1)
                                dve.wait_ge(p_evacuated, j + 1)
                                dve.tensor_scalar(part[:, r % 2, :, :], part[:, r % 2, :, :], 5.0 * HD ** 0.5, -5.0 * HD ** 0.5,
                                                  ALU.min, ALU.max).then_inc(p_scored, 1)
                                last = led(i, r, -1)
                                if not (isinstance(last[0], int) and last[0] < 0):
                                    add_blocks(dve, sums, *last, W)
                                dve.wait_ge(p_weight, j + 1)
                                for u in range(GROUP):
                                    ins = dve.tensor_tensor(msg[:, r % 2, u, 0:D].rearrange("p (h e) -> p h e", h=L3_HEADS),
                                                            ring[:, r, u, D:2 * D].rearrange("p (h e) -> p h e", h=L3_HEADS),
                                                            msg[:, r % 2, u, D:W].unsqueeze(2).broadcast_to([P, L3_HEADS, HD]), ALU.mult)
                                ins.then_inc(p_weighted, 1)
                        make_select(dve, 0, 0)
                        make_select(dve, 0, 1)
                        turns(dve, body)
                        add_blocks(dve, sums, LOOPS - 1, REGIONS - 1, W)

                    @b.tensor
                    def _(pe):
                        def turn(i, r):
                            pe.wait_ge(p_selected, region_of(i, r) + 1)
                            at_least(pe, p_spread, region_of(i, r))
                            for u in range(GROUP):
                                ins = pe.transpose(psum[:, 0, u * P:(u + 1) * P], select[:, r, u, :], ident[:])
                            ins.then_inc(p_turned, 1)

                        def queries(i, r):
                            pe.wait_ge(p_spread, region_of(i, r) + 1)
                            at_least(pe, p_multiplied, region_of(i, r) - 1)
                            for u in range(GROUP):
                                q = t1[:, bass.ds(block_of(pe, i, r, u) * D, D)]
                                ins = pe.matmul(q_bank(r)[:, u * P:(u + 1) * P], spread[:, r % 2, u, :], q, start=True, stop=True)
                            ins.then_inc(p_projected, 1)

                        def body(i):
                            for r in range(REGIONS):
                                if nxt := led(i, r, 1):
                                    queries(*nxt)
                                if nxt := led(i, r):
                                    turn(*nxt)
                                pe.wait_ge(p_weighted, region_of(i, r) + 1)
                                at_least(pe, p_added, (region_of(i, r) - 1) * GROUP)
                                for u in range(GROUP):
                                    ins = pe.matmul(sums(r, u), select[:, r, u, :], msg[:, r % 2, u, :], start=True, stop=True)
                                ins.then_inc(p_summed, 1)
                        turn(0, 0)
                        turn(0, 1)
                        queries(0, 0)
                        turns(pe, body)

        s_scores_turned, s_scores_copied, s_max, s_ends_turned, s_chain, s_chain_io, s_exp, s_weights_turned, s_weights_kept = sems(
            "scores_turned", "scores_copied", "max_step", "ends_turned", "chain_ready", "chain_moved", "weights_made",
            "weights_turned", "weights_kept")
        s_in_dram, = sems("enter_in_dram")
        max_done = [8 + 3 * (h + 1) for h in range(GAT_HEADS)]
        carry_dram = nc.dram_tensor("carry_dram", [2 * GAT_HEADS * ROW_C, ROW_K], F32)
        enter_dram = nc.dram_tensor("enter_dram", [2 * GAT_HEADS * ROW_C, ROW_K], F32)

        def gat_softmax(name):
            HC = GAT_HEADS * ROW_C
            RUN = ROW_C * P
            per_bank = CHUNK // ROW_K
            with ExitStack() as tmp:
                scores = sb(f"{name}_scores", [ROW_K, HC, P], F32, tmp)
                run_f = acc[0:ROW_K, 0:HC * P].rearrange("k (a p) -> k a p", p=P)
                run_b = t1[0:ROW_K, 0:HC * P].rearrange("k (a p) -> k a p", p=P)
                ends = sb(f"{name}_ends", [ROW_K, 2, HC], F32, tmp)
                ends_t = sb(f"{name}_ends_t", [2 * HC, ROW_K], F32, tmp)
                enter_t = sb(f"{name}_enter_t", [2 * HC, ROW_K], F32, tmp)
                enter = sb(f"{name}_enter", [ROW_K, 2, HC], F32, tmp)
                row_max = t1[0:GAT_HEADS, HC * P:HC * P + 2 * STEPS].rearrange("h (d s) -> h d s", d=2)
                chain = acc[0:GAT_HEADS, HC * P:HC * P + 2 * STEPS].rearrange("h (d s) -> h d s", d=2)
                with block(name, s_scores_turned, s_scores_copied, s_max, s_ends_turned, s_chain, s_chain_io, s_exp,
                           s_weights_turned, s_weights_kept, s_in_dram) as b:
                    @b.tensor
                    def _(pe):
                        for a in range(HC):
                            h, c = divmod(a, ROW_C)
                            ins = pe.transpose(psum[0:ROW_K, a // 4, (a % 4) * P:(a % 4 + 1) * P],
                                               score[:, c * ROW_K:(c + 1) * ROW_K, h], ident[:])
                            if a % 4 == 3:
                                ins.then_inc(s_scores_turned, 1)
                        pe.wait_ge(s_chain, 1)
                        pe.transpose(psum[0:2 * HC, 7, 0:ROW_K], ends[:].rearrange("k a b -> k (a b)"),
                                     ident[0:ROW_K, 0:ROW_K]).then_inc(s_ends_turned, 1)
                        pe.wait_ge(s_chain_io, 48)
                        pe.transpose(psum[0:ROW_K, 7, ROW_K:ROW_K + 2 * HC], enter_t[:],
                                     ident[0:2 * HC, 0:2 * HC]).then_inc(s_ends_turned, 1)
                        pe.wait_ge(s_chain, 4)
                        for h in range(GAT_HEADS):
                            pe.wait_ge(s_exp, h + 1)
                            for c in range(ROW_C):
                                ins = pe.transpose(psum[:, 2 * h + c // per_bank, (c % per_bank) * ROW_K:(c % per_bank + 1) * ROW_K],
                                                   scores[:, h * ROW_C + c, :], ident[0:ROW_K, 0:ROW_K])
                            ins.then_inc(s_weights_turned, 1)

                    @b.sync
                    def _(sp):
                        sp.wait_ge(s_chain, 2)
                        sp.dma_start(carry_dram[:], ends_t[:]).then_inc(s_chain_io, 16)
                        sp.wait_ge(s_chain_io, 16)
                        sp.dma_start(row_max, carry_dram.ap().rearrange("(d h c) k -> h d (c k)", d=2, h=GAT_HEADS)).then_inc(s_chain_io, 16)
                        sp.wait_ge(s_chain, 3)
                        sp.dma_start(enter_dram.ap().rearrange("(d h c) k -> h d (c k)", d=2, h=GAT_HEADS), row_max).then_inc(s_in_dram, 16)
                        sp.wait_ge(s_in_dram, 16)
                        sp.dma_start(enter_t[:], enter_dram[:]).then_inc(s_chain_io, 16)

                    @b.scalar
                    def _(act):
                        for g in range(HC // 4):
                            act.wait_ge(s_scores_turned, g + 1)
                            act.copy(scores[:, 4 * g:4 * g + 4, :], bank4(psum[0:ROW_K, g, :])).then_inc(s_scores_copied, 1)
                        for h in range(GAT_HEADS):
                            act.wait_ge(s_max, max_done[h])
                            act.activation(scores[:, h * ROW_C:(h + 1) * ROW_C, :], scores[:, h * ROW_C:(h + 1) * ROW_C, :], ACT.Exp,
                                           scale=(D // GAT_HEADS) ** -0.5).then_inc(s_exp, 1)
                        for h in range(0, GAT_HEADS, 2):
                            act.wait_ge(s_weights_turned, h + 1)
                            act.copy(score[:, 0:per_bank * ROW_K, h], psum[:, 2 * h, 0:per_bank * ROW_K])
                            act.copy(score[:, per_bank * ROW_K:STEPS, h], psum[:, 2 * h + 1, 0:STEPS - per_bank * ROW_K]).then_inc(s_weights_kept, 1)

                    @b.vector
                    def _(dve):
                        n = [0]

                        def link(ins):
                            n[0] += 1
                            ins.then_inc(s_max, 1)
                            dve.wait_ge(s_max, n[0])

                        def flat(ap, h):
                            return ap[:, h * ROW_C:(h + 1) * ROW_C, :].rearrange("k a p -> k (a p)")

                        for h in range(GAT_HEADS):
                            dve.wait_ge(s_scores_copied, -(-(h + 1) * ROW_C // 4))
                            dve.tensor_tensor_scan(flat(run_f, h), key_pen_f[:], flat(scores, h), -BIG, ALU.add, ALU.max)
                            ins = dve.tensor_tensor_scan(flat(run_b, h)[:, ::-1], key_pen_b[:, ::-1], flat(scores, h)[:, ::-1], -BIG,
                                                         ALU.add, ALU.max)
                        link(ins)
                        link(dve.tensor_copy(ends[:, 0, :], run_f[:, :, P - 1]))
                        link(dve.tensor_copy(ends[:, 1, :], run_b[:, :, 0]))
                        dve.sem_inc(s_chain, 1)
                        link(dve.tensor_tensor(run_f, run_f, run_b, ALU.max))
                        dve.wait_ge(s_ends_turned, 1)
                        dve.tensor_copy(ends_t[:], psum[0:2 * HC, 7, 0:ROW_K]).then_inc(s_chain, 1)
                        dve.wait_ge(s_chain_io, 32)
                        dve.tensor_tensor_scan(chain[:, 0, :], chain_pen[:, 0, :], row_max[:, 0, :], -BIG, ALU.add, ALU.max)
                        link(dve.tensor_tensor_scan(chain[:, 1, ::-1], chain_pen[:, 1, ::-1], row_max[:, 1, ::-1], -BIG, ALU.add, ALU.max))
                        link(dve.memset(row_max, -BIG))
                        link(dve.tensor_tensor(row_max[:, 0, 1:STEPS], chain[:, 0, 0:STEPS - 1], enter_pen[:, 0, 1:STEPS], ALU.add))
                        link(dve.tensor_tensor(row_max[:, 1, 0:STEPS - 1], chain[:, 1, 1:STEPS], enter_pen[:, 1, 0:STEPS - 1], ALU.add))
                        dve.sem_inc(s_chain, 1)
                        dve.wait_ge(s_ends_turned, 2)
                        dve.tensor_copy(enter[:].rearrange("k a b -> k (a b)"), psum[0:ROW_K, 7, ROW_K:ROW_K + 2 * HC]).then_inc(s_chain, 1)
                        dve.wait_ge(s_chain, 4)
                        for h in range(GAT_HEADS):
                            for d, pen in enumerate((first_pen, last_pen)):
                                for c in range(ROW_C):
                                    a = h * ROW_C + c
                                    ins = dve.scalar_tensor_tensor(out=run_f[:, a, :], in0=pen[:, c, :], scalar=enter[:, d, a:a + 1],
                                                                   in1=run_f[:, a, :], op0=ALU.add, op1=ALU.max)
                                link(ins)
                            link(dve.tensor_tensor(flat(scores, h), flat(scores, h), flat(run_f, h), ALU.subtract))
                            assert n[0] == max_done[h]
                        for h in range(1, GAT_HEADS, 2):
                            dve.wait_ge(s_weights_turned, h + 1)
                            dve.tensor_copy(score[:, 0:per_bank * ROW_K, h], psum[:, 2 * h, 0:per_bank * ROW_K])
                            dve.tensor_copy(score[:, per_bank * ROW_K:STEPS, h], psum[:, 2 * h + 1, 0:STEPS - per_bank * ROW_K])


        d_rows, d_turned, d_mixed, d_product, d_done, d_link = sems(
            "rows_ready", "turned_ready", "mixed_ready", "product_ready", "chunk_done", "rows_step")

        def from_rows(name, dst, heads=0, eps=0.0, mix=None, weight=None, bias=None, residual=None):
            with ExitStack() as tmp:
                rows = sb(f"{name}_rows", [P, V, 4, D], F32, tmp)
                den = sb(f"{name}_den", [P, V, 4, max(heads, 1)], F32, tmp)
                mixed = sb(f"{name}_mixed", [P, V, CHUNK], F32, tmp)
                with block(name, d_rows, d_turned, d_mixed, d_product, d_done, d_link) as b:
                    @b.vector
                    def _(dve):
                        def stage(c, u, i):
                            at_least(dve, d_turned, c + 1 - V)
                            if not heads:
                                dve.tensor_scalar(rows[:, u, :, :], acc_rows(c, 0, D), 0.0, None, ALU.add).then_inc(d_rows, 1)
                                return
                            dve.tensor_scalar(den[:, u, :, :], acc_rows(c, D, heads), eps, None, ALU.add).then_inc(d_link, 1)
                            dve.wait_ge(d_link, c * 2 + 1)
                            dve.reciprocal(den[:, u, :, :], den[:, u, :, :]).then_inc(d_link, 1)
                            dve.wait_ge(d_link, c * 2 + 2)
                            dve.tensor_tensor(rows[:, u, :, :].rearrange("p b (h e) -> p b h e", h=heads),
                                              acc_rows(c, 0, D).rearrange("p b (h e) -> p b h e", h=heads),
                                              den[:, u, :, :].unsqueeze(3).broadcast_to([P, 4, heads, D // heads]), ALU.mult).then_inc(d_rows, 1)

                        def add_state(c, u, i):
                            dve.wait_ge(d_turned, c + 1)
                            at_least(dve, d_product, c + 1 - V)
                            dve.scalar_tensor_tensor(out=mixed[:, u, :], in0=mix[:, cols(c)], scalar=eps_col[:], in1=psum[:, u, :],
                                                     op0=ALU.mult, op1=ALU.add).then_inc(d_mixed, 1)

                        def finish(c, u, i):
                            if weight is None:
                                dve.wait_ge(d_turned, c + 1)
                                ins = dve.tensor_scalar(dst[:, cols(c)], psum[:, u, :], 0.0, None, ALU.add)
                            else:
                                dve.wait_ge(d_product, c + 1)
                                if residual is None:
                                    ins = dve.tensor_scalar(dst[:, cols(c)], psum[:, 4 + u, :], bias, None, ALU.add)
                                else:
                                    ins = dve.scalar_tensor_tensor(out=dst[:, cols(c)], in0=psum[:, 4 + u, :], scalar=bias,
                                                                   in1=residual[:, cols(c)], op0=ALU.add, op1=ALU.add)
                            ins.then_inc(d_done, 1)
                        pairs(dve, *([stage, add_state, finish] if mix is not None else [stage, finish]))

                    if weight is not None and mix is None:
                        @b.scalar
                        def _(act):
                            def copy(c, u, i):
                                act.wait_ge(d_turned, c + 1)
                                at_least(act, d_product, c + 1 - V)
                                act.copy(mixed[:, u, :], psum[:, u, :]).then_inc(d_mixed, 1)
                            pairs(act, copy)

                    @b.tensor
                    def _(pe):
                        def turn(c, u, i):
                            pe.wait_ge(d_rows, c + 1)
                            at_least(pe, d_done if weight is None else d_mixed, c + 1 - V)
                            for k in range(4):
                                ins = pe.transpose(psum[:, u, k * P:(k + 1) * P], rows[:, u, k, :], ident[:])
                            ins.then_inc(d_turned, 1)

                        def project(c, u, i):
                            pe.wait_ge(d_mixed, c + 1)
                            at_least(pe, d_done, c + 1 - V)
                            pe.matmul(psum[:, 4 + u, :], weight, mixed[:, u, :], start=True, stop=True).then_inc(d_product, 1)
                        pairs(pe, *([turn] if weight is None else [turn, project]))

        def feed_forward(name, src, dst, function, w_in, b_in, w_out, b_out):
            K = len(w_in)
            with ExitStack() as tmp:
                inner = sb(f"{name}_inner", [P, V, K, CHUNK], F32, tmp)
                with block(name, d_turned, d_mixed, d_product, d_done) as b:
                    @b.tensor
                    def _(pe):
                        def expand(c, u, i):
                            for k in range(K):
                                at_least(pe, d_mixed, c * K + (k + 1 - 4))
                                pe.matmul(psum[:, (u * K + k) % 4, :], w_in[k], src[:, cols(c)], start=True, stop=True).then_inc(d_turned, 1)

                        def contract(c, u, i):
                            at_least(pe, d_done, c + 1 - V)
                            for k in range(K):
                                pe.wait_ge(d_mixed, c * K + (k + 1))
                                ins = pe.matmul(psum[:, 4 + u, :], w_out[k], inner[:, u, k, :], start=k == 0, stop=k == K - 1)
                            ins.then_inc(d_product, 1)

                        def both(c, u, i):
                            expand(c, u, i)
                            contract(c, u, i)
                        pairs(pe, both)

                    @b.scalar
                    def _(act):
                        def bend(c, u, i):
                            at_least(act, d_product, c + 1 - V)
                            for k in range(K):
                                act.wait_ge(d_turned, c * K + (k + 1))
                                act.activation(inner[:, u, k, :], psum[:, (u * K + k) % 4, :], function, bias=b_in[k]).then_inc(d_mixed, 1)
                        pairs(act, bend)

                    @b.vector
                    def _(dve):
                        def finish(c, u, i):
                            dve.wait_ge(d_product, c + 1)
                            dve.scalar_tensor_tensor(out=dst[:, cols(c)], in0=psum[:, 4 + u, :], scalar=b_out, in1=src[:, cols(c)],
                                                     op0=ALU.add, op1=ALU.add).then_inc(d_done, 1)
                        pairs(dve, finish)

        g_product, g_gated, g_reset, g_new, g_read, g_step = sems(
            "gru_products", "gru_gates", "gru_reset_applied", "gru_new", "gru_banks_read", "gru_step")

        def gru(name, msg, h, w_ih, w_hh, gates, b_in, b_hn):
            with ExitStack() as tmp:
                gate = sb(f"{name}_gate", [P, V, 2, CHUNK], F32, tmp)
                new = sb(f"{name}_new", [P, V, CHUNK], F32, tmp)
                with block(name, g_product, g_gated, g_reset, g_new, g_read, g_step) as b:
                    @b.tensor
                    def _(pe):
                        def project(c, u, i):
                            at_least(pe, g_gated, c + 1 - V)
                            at_least(pe, g_read, c + 1 - V)
                            for k in range(2):
                                pe.matmul(psum[:, 4 * u + k, :], w_ih[k], msg[:, cols(c)], start=True, stop=False)
                                pe.matmul(psum[:, 4 * u + k, :], w_hh[k], h[:, cols(c)], start=False, stop=True)
                            pe.matmul(psum[:, 4 * u + 2, :], w_ih[2], msg[:, cols(c)], start=True, stop=True)
                            pe.matmul(psum[:, 4 * u + 3, :], w_hh[2], h[:, cols(c)], start=True, stop=True).then_inc(g_product, 1)
                        pairs(pe, project)

                    @b.scalar
                    def _(act):
                        def bend(c, u, i):
                            act.wait_ge(g_product, c + 1)
                            at_least(act, g_step, (c + 1 - V) * 3)
                            act.activation(gate[:, u, 0, :], psum[:, 4 * u, :], ACT.Sigmoid, bias=gates[:, 0:1])
                            act.activation(gate[:, u, 1, :], psum[:, 4 * u + 1, :], ACT.Sigmoid, bias=gates[:, 1:2]).then_inc(g_gated, 1)

                        def renew(c, u, i):
                            act.wait_ge(g_read, c + 1)
                            act.activation(new[:, u, :], new[:, u, :], ACT.Tanh, bias=b_in).then_inc(g_new, 1)
                        pairs(act, bend, renew)

                    @b.vector
                    def _(dve):
                        def reset(c, u, i):
                            dve.wait_ge(g_gated, c + 1)
                            dve.scalar_tensor_tensor(out=new[:, u, :], in0=psum[:, 4 * u + 3, :], scalar=b_hn, in1=gate[:, u, 0, :],
                                                     op0=ALU.add, op1=ALU.mult).then_inc(g_reset, 1)
                            dve.wait_ge(g_reset, c + 1)
                            dve.tensor_tensor(new[:, u, :], new[:, u, :], psum[:, 4 * u + 2, :], ALU.add).then_inc(g_read, 1)

                        def update(c, u, i):
                            dve.wait_ge(g_new, c + 1)
                            dve.tensor_tensor(gate[:, u, 0, :], h[:, cols(c)], new[:, u, :], ALU.subtract).then_inc(g_step, 1)
                            dve.wait_ge(g_step, c * 3 + 1)
                            dve.tensor_tensor(gate[:, u, 0, :], gate[:, u, 0, :], gate[:, u, 1, :], ALU.mult).then_inc(g_step, 1)
                            dve.wait_ge(g_step, c * 3 + 2)
                            dve.tensor_tensor(h[:, cols(c)], new[:, u, :], gate[:, u, 0, :], ALU.add).then_inc(g_step, 1)
                        pairs(dve, reset, update)

        b_stats, b_root, b_applied, b_scale, b_done = sems("bn_step", "bn_rooted", "bn_applied", "bn_product", "bn_done")

        def batch_norm(name, src, gain, shift, dst=None, residual=None, weight=None, bias=None):
            with ExitStack() as tmp:
                stats = sb(f"{name}_stats", [P, CHUNKS, 6], F32, tmp)
                moments = sb(f"{name}_moments", [P, 2], F32, tmp)
                coef = sb(f"{name}_coef", [P, 3], F32, tmp)
                normed = sb(f"{name}_normed", [P, V, CHUNK], F32, tmp)
                with block(name, b_stats, b_root, b_applied, b_scale, b_done) as b:
                    @b.vector
                    def _(dve):
                        dve.memset(coef[:, 2:3], BN_EPS).then_inc(b_stats, 1)
                        for k in range(CHUNKS):
                            dve.bn_stats(stats[:, k, :], src[:, k * BN_CHUNK:(k + 1) * BN_CHUNK]).then_inc(b_stats, 1)
                        dve.wait_ge(b_stats, CHUNKS + 1)
                        dve.bn_aggr(moments[:], stats[:]).then_inc(b_stats, 1)
                        dve.wait_ge(b_root, 1)
                        dve.reciprocal(moments[:, 1:2], moments[:, 1:2]).then_inc(b_stats, 1)
                        dve.wait_ge(b_stats, CHUNKS + 3)
                        dve.tensor_tensor(coef[:, 0:1], moments[:, 1:2], gain, ALU.mult).then_inc(b_stats, 1)
                        dve.wait_ge(b_stats, CHUNKS + 4)
                        dve.tensor_tensor(moments[:, 0:1], moments[:, 0:1], coef[:, 0:1], ALU.mult).then_inc(b_stats, 1)
                        dve.wait_ge(b_stats, CHUNKS + 5)
                        dve.tensor_tensor(coef[:, 1:2], shift, moments[:, 0:1], ALU.subtract).then_inc(b_stats, 1)
                        dve.wait_ge(b_stats, CHUNKS + 6)
                        if dst is not None:
                            dve.tensor_scalar(dst[:], src[:, 0:NP], coef[:, 0:1], coef[:, 1:2], ALU.mult, ALU.add)
                            return

                        def finish(c, u, i):
                            dve.wait_ge(b_scale if weight is not None else b_applied, c + 1)
                            if weight is not None:
                                ins = dve.scalar_tensor_tensor(out=residual[:, cols(c)], in0=psum[:, u, :], scalar=bias, in1=residual[:, cols(c)],
                                                               op0=ALU.add, op1=ALU.add)
                            else:
                                ins = dve.tensor_tensor(residual[:, cols(c)], residual[:, cols(c)], normed[:, u, :], ALU.add)
                            ins.then_inc(b_done, 1)
                        pairs(dve, finish)

                    @b.scalar
                    def _(act):
                        act.wait_ge(b_stats, CHUNKS + 2)
                        act.activation(moments[:, 1:2], moments[:, 1:2], ACT.Sqrt, bias=coef[:, 2:3]).then_inc(b_root, 1)
                        if dst is not None:
                            return
                        act.wait_ge(b_stats, CHUNKS + 6)

                        def apply(c, u, i):
                            at_least(act, b_scale if weight is not None else b_done, c + 1 - V)
                            act.activation(normed[:, u, :], src[:, cols(c)], ACT.Relu if weight is not None else ACT.Identity,
                                           bias=coef[:, 1:2], scale=coef[:, 0:1]).then_inc(b_applied, 1)
                        pairs(act, apply)

                    if weight is not None:
                        @b.tensor
                        def _(pe):
                            def project(c, u, i):
                                pe.wait_ge(b_applied, c + 1)
                                at_least(pe, b_done, c + 1 - V)
                                pe.matmul(psum[:, u, :], weight, normed[:, u, :], start=True, stop=True).then_inc(b_scale, 1)
                            pairs(pe, project)

        a_added, = sems("state_added")

        def add_state(name, src):
            with block(name, a_added) as b:
                @b.vector
                def _(dve):
                    dve.tensor_tensor(resT[:], resT[:], src[:], ALU.add).then_inc(a_added, 1)

        o_staged, o_turned, o_copied = sems("out_staged", "out_turned", "out_copied")
        o_stored = sems(*(f"out_stored{u}" for u in range(V)))

        def store(name):
            with ExitStack() as tmp:
                rows = sb(f"{name}_rows", [P, V, CHUNK], F32, tmp)
                state = sb(f"{name}_state", [P, V, CHUNK], F32, tmp)
                with block(name, o_staged, o_turned, o_copied, *o_stored) as b:
                    @b.vector
                    def _(dve):
                        def stage(c, u, i):
                            at_least(dve, o_turned, c + 1 - V)
                            dve.tensor_scalar(state[:, u, :], resT[:, cols(c)], 0.0, None, ALU.add).then_inc(o_staged, 1)
                        pairs(dve, stage)

                    @b.tensor
                    def _(pe):
                        def turn(c, u, i):
                            pe.wait_ge(o_staged, c + 1)
                            at_least(pe, o_copied, c + 1 - V)
                            for k in range(4):
                                ins = pe.transpose(psum[:, u, k * P:(k + 1) * P], state[:, u, k * P:(k + 1) * P], ident[:])
                            ins.then_inc(o_turned, 1)
                        pairs(pe, turn)

                    @b.scalar
                    def _(act):
                        def copy(c, u, i):
                            act.wait_ge(o_turned, c + 1)
                            at_least(act, o_stored[u], i * 16)
                            act.copy(rows[:, u, :], psum[:, u, :]).then_inc(o_copied, 1)
                        pairs(act, copy)

                    @b.sync
                    def _(sp):
                        def leave(c, u, i):
                            sp.wait_ge(o_copied, c + 1)
                            sp.dma_start(out[cols(c), :].rearrange("(b p) f -> p b f", p=P), bank4(rows[:, u, :])).then_inc(o_stored[u], 16)
                        for c in range(V):
                            leave(c, c, 0)
                        with sp.Fori(1, CHUNKS // V - 1) as i:
                            for u in range(V):
                                leave(i * V + u, u, i)
                        leave(CHUNKS - 2, 0, CHUNKS // V - 1)
                        sp.wait_ge(o_copied, CHUNKS)
                        first = (CHUNKS - 1) * CHUNK
                        sp.dma_start(out[first:FULL_BLOCKS * P, :].rearrange("(b p) f -> p b f", p=P),
                                     bank4(rows[:, 1, :])[:, 0:FULL_BLOCKS - first // P, :]).then_inc(o_stored[1], 16)
                        sp.dma_start(out[FULL_BLOCKS * P:N, :], rows[0:TAIL, 1, (FULL_BLOCKS - first // P) * P:(FULL_BLOCKS - first // P + 1) * P]
                                     ).then_inc(o_stored[1], 16)
                        sp.wait_ge(o_stored[0], 16 * (CHUNKS // V))
                        sp.wait_ge(o_stored[1], 16 * (CHUNKS // V + 1))

        def blocks_of(w, first, count):
            return [w[:, first + k, :] for k in range(count)]

        layer_norm("l0_norm", resT, xT, LN_EPS, also=hT)
        with nc.Fori(0, GAT_ITERS) as it:
            node_rows("l0_rows", xT, queries=True)
            gat_score_pass("l0_scores", it * ROWS)
            gat_softmax("l0_softmax")
            gat_value_pass("l0_values")
            from_rows("l0_attention", t1, heads=GAT_HEADS, eps=1e-16, weight=wt[:, WAO, :], bias=wcol("b_ao"), residual=xT)
            layer_norm("l0_ln1", t1, xT, 1e-12, wcol("ln1_g"), wcol("ln1_b"))
            feed_forward("l0_ffn", xT, t1, ACT.Gelu, blocks_of(wt, WINT, GAT_FF), [wcol("b_int", k) for k in range(GAT_FF)],
                         blocks_of(wt, WOUT, GAT_FF), wcol("b_out"))
            layer_norm("l0_ln2", t1, xT, 1e-12, wcol("ln2_g"), wcol("ln2_b"))
            gru("l0_gru", xT, hT, blocks_of(wt, GIH, 3), blocks_of(wt, GHH, 3), gate_bias[:, 0, :], wcol("b_ih", 2), wcol("b_hh", 2))
            layer_norm("l0_ln3", hT, xT, 1e-12, wcol("ln3_g"), wcol("ln3_b"))
            clear_block("l0_end")
        add_state("l0_residual", xT)

        layer_norm("l1_norm", resT, hT, LN_EPS)
        node_rows("l1_rows", hT, queries=False)
        sum_pass("l1_sums", table_x[:], src_idx, GAT_ITERS * ROWS)
        from_rows("l1_first", t1, mix=hT, weight=wt[:, GIN1, :], bias=wcol("1_b1"))
        batch_norm("l1_second", t1, wcol("1_gamma"), wcol("1_beta"), residual=resT, weight=wt[:, GIN2, :], bias=wcol("1_b2"))

        layer_norm("l2_norm", resT, hT, LN_EPS)
        with nc.Fori(0, L2_STEPS) as it:
            projected_rows("l2_rows", hT, wt[:, WEDGE:WEDGE + 4, :].rearrange("p a b -> p (a b)"), 4 * D, table_typed, bias=bedge_rows[:])
            sum_pass("l2_sums", table_typed.ap().rearrange("n (t f) -> (n t) f", f=D), typed_idx, (GAT_ITERS + 1) * ROWS + it * ROWS)
            from_rows("l2_messages", t1)
            gru("l2_gru", t1, hT, blocks_of(wt, GGIH, 3), blocks_of(wt, GGHH, 3), gate_bias[:, 1, :], wcol("2_b_ih", 2), wcol("2_b_hh", 2))
            clear_block("l2_end")
        add_state("l2_residual", hT)

        layer_norm("l3_norm", resT, xT, LN_EPS)
        projected_rows("l3_rows", xT, w3[:, 0:3, :].rearrange("p a b -> p (a b)"), 3 * D, table_kv, query_width=D)
        transformer_pass("l3_pass", (GAT_ITERS + 1 + L2_STEPS) * ROWS)
        from_rows("l3_attention", t1, heads=L3_HEADS, eps=1e-6, weight=w3[:, 3, :], bias=wcol("3_bo"), residual=xT)
        batch_norm("l3_bn1", t1, wcol("3_bn1_g"), wcol("3_bn1_b"), dst=xT)
        feed_forward("l3_ffn", xT, t1, ACT.Relu, blocks_of(w3, 4, 2), [wcol("3_b1", k) for k in range(2)], blocks_of(w3, 6, 2), wcol("3_b2"))
        batch_norm("l3_bn2", t1, wcol("3_bn2_g"), wcol("3_bn2_b"), residual=resT)
        store("store")


def kernel(**inputs):
    import numpy as _np
    import concourse.bacc as _bacc
    from concourse import mybir as _mybir
    from concourse.bass_utils import run_bass_kernel_spmd as _run

    nc = _bacc.Bacc("TRN2", target_bir_lowering=False, num_devices=1)
    arrays, io = {}, {}
    for name in inputs:
        a = _np.ascontiguousarray(inputs[name])
        arrays[f"in_{name}_dram"] = a
        io[name] = nc.dram_tensor(f"in_{name}_dram", a.shape, _mybir.dt.from_np(a.dtype), kind="ExternalInput").ap()
    out = nc.dram_tensor("out_0_dram", (N, D), F32, kind="ExternalOutput").ap()
    program(nc, io, out)
    r = _run(nc, [arrays], core_ids=[0])
    return r.results[0]["out_0_dram"]
```

```python
from contextlib import ExitStack, contextmanager
from itertools import count

import concourse.bass as bass
from concourse import mybir

F32 = mybir.dt.float32
I32 = mybir.dt.int32
ALU = mybir.AluOpType
ACT = mybir.ActivationFunctionType
AX_X = mybir.AxisListType.X

P = 128
N, E, D = 5000, 80000, 128
TILES = E // P
BLOCKS = -(-N // P)
NP = BLOCKS * P
FULL_BLOCKS = N // P
TAIL = N - FULL_BLOCKS * P
GROUP = 4
REGIONS = 4
ROW_C, ROW_K = 7, 96
STEPS = ROW_C * ROW_K
LOOPS = STEPS // (GROUP * REGIONS)
assert STEPS == LOOPS * GROUP * REGIONS and STEPS >= TILES + BLOCKS - 1
PADDED = STEPS + GROUP
ACC_W = 136
ACC_BLOCKS = BLOCKS + 1
Q_W = D + 4
CHUNK = 512
CHUNKS = NP // CHUNK
U = 5
BIG = 1.0e38
GAT_HEADS, GAT_ITERS, GAT_FF = 4, 3, 4
L3_HEADS, L2_STEPS = 8, 4
LN_EPS, BN_EPS = 1e-5, 1e-5
BN_CHUNK = N // CHUNKS


def bank4(ap):
    return ap.rearrange("p (a b) -> p a b", b=P)


def program(nc, io, out):
    ctx = ExitStack()
    with ctx:
        def sb(name, shape, dt=F32, where=ctx):
            return where.enter_context(nc.sbuf_tensor(name, shape, dt))

        def sems(*names):
            return [ctx.enter_context(nc.semaphore(n)) for n in names]

        spent = []

        @contextmanager
        def block(name, *used):
            with nc.Block(name) as b:
                cleared = [s for s in spent if s not in used]
                assert len(cleared) == len(spent), name
                spent.clear()

                @b.sync
                def _(sp):
                    for s in cleared:
                        sp.sem_clear(s)
                yield b
            spent.extend(used)

        def clear_block(name):
            with block(name):
                pass

        table_x = nc.dram_tensor("table_x", [NP, D], F32)
        table_kv = nc.dram_tensor("table_kv", [NP, 2 * D], F32)
        table_typed = nc.dram_tensor("table_typed", [NP, 4 * D], F32)
        rows_dram = nc.dram_tensor("rows_dram", [STEPS // GROUP, P, GROUP * D], F32)
        type_dram = nc.dram_tensor("type_dram", [TILES, P], F32)
        step_block_dram = nc.dram_tensor("step_block_dram", [1, STEPS], I32)
        step_row_dram = nc.dram_tensor("step_row_dram", [1, STEPS], I32)
        ends_dram = nc.dram_tensor("ends_dram", [3, STEPS], F32)

        ident = sb("ident", [P, P])
        iota_row = sb("iota_row", [P, P])
        ones = sb("ones", [P, P])
        (WK, WV, WQ, WAO, WINT, WOUT, GIH, GHH, GIN1, GIN2, WEDGE, GGIH, GGHH, NW) = (
            0, 1, 2, 3, 4, 8, 12, 15, 18, 19, 20, 24, 27, 30)
        wt = sb("wt", [P, NW, P])
        w3 = sb("w3", [P, 8, P])
        VEC = {}
        vec_list = [("b_ao", 1), ("ln1_g", 1), ("ln1_b", 1), ("b_int", 4), ("b_out", 1), ("ln2_g", 1), ("ln2_b", 1),
                    ("b_ih", 3), ("b_hh", 3), ("ln3_g", 1), ("ln3_b", 1), ("1_b1", 1), ("1_gamma", 1), ("1_beta", 1),
                    ("1_b2", 1), ("2_b_ih", 3), ("2_b_hh", 3), ("3_bo", 1), ("3_b1", 2), ("3_b2", 1), ("3_bn1_g", 1),
                    ("3_bn1_b", 1), ("3_bn2_g", 1), ("3_bn2_b", 1)]
        n_vec = 0
        for vname, k in vec_list:
            VEC[vname] = n_vec
            n_vec += k
        vec = sb("vec", [P, n_vec])
        gate_bias = sb("gate_bias", [P, 2, 2])
        eps_col = sb("eps_col", [P, 1])
        bq_rows = sb("bq_rows", [P, D])
        bk_rows = sb("bk_rows", [P, D])
        bv_rows = sb("bv_rows", [P, D])
        bedge_rows = sb("bedge_rows", [P, 4 * D])
        src_idx = sb("src_idx", [P, PADDED], I32)
        typed_idx = sb("typed_idx", [P, PADDED], I32)
        dst_local = sb("dst_local", [P, PADDED])
        step_block = sb("step_block", [1, STEPS], I32)
        step_row = sb("step_row", [1, STEPS], I32)
        key_pen_f = sb("key_pen_f", [ROW_K, ROW_C * P])
        key_pen_b = sb("key_pen_b", [ROW_K, ROW_C * P])
        first_pen = sb("first_pen", [ROW_K, ROW_C, P])
        last_pen = sb("last_pen", [ROW_K, ROW_C, P])
        chain_pen = sb("chain_pen", [GAT_HEADS, 2, STEPS])
        enter_pen = sb("enter_pen", [GAT_HEADS, 2, STEPS])
        xT = sb("xT", [P, NP])
        hT = sb("hT", [P, NP])
        resT = sb("resT", [P, NP])
        t1 = sb("t1", [P, ACC_BLOCKS * Q_W])
        acc = sb("acc", [P, ACC_BLOCKS * ACC_W])
        psum = ctx.enter_context(nc.psum_tensor("psum", [P, 8, CHUNK], F32))

        gathered = sems(*(f"gathered{r}" for r in range(REGIONS)))
        gather_go, act_go = sems("gather_go", "act_go")

        def wcol(name, k=0):
            return vec[:, VEC[name] + k:VEC[name] + k + 1]

        s_load, s_const, s_wt, s_wcopy = sems("weights_loaded", "constant_made", "weight_turned", "weight_copied")
        s_xl, s_rows = sems("x_loaded", "bias_spread")
        with ExitStack() as tmp:
            wn = sb("wn", [P, NW, P], F32, tmp)
            vrow = sb("vrow", [n_vec, P], F32, tmp)
            brow = sb("brow", [1, D + 2 * D + 4 * D + 1], F32, tmp)
            xrows = acc[:, 0:NP].rearrange("p (b f) -> p b f", f=D)
            loads = []

            def rows_of(w):
                return w.rearrange("(k p) f -> p k f", p=P)
            loads += [(wn[:, WK, :], io["L0_gnn_wk"]), (wn[:, WV, :], io["L0_gnn_wv"]), (wn[:, WQ, :], io["L0_gnn_wq"]),
                      (wn[:, WAO, :], io["L0_gnn_w_ao"]), (wn[:, WINT:WINT + 4, :], rows_of(io["L0_gnn_w_int"])),
                      (wn[:, WOUT:WOUT + 4, :], io["L0_gnn_w_out"].rearrange("p (k f) -> p k f", f=P)),
                      (wn[:, GIH:GIH + 3, :], rows_of(io["L0_gnn_w_ih"])), (wn[:, GHH:GHH + 3, :], rows_of(io["L0_gnn_w_hh"])),
                      (wn[:, GIN1, :], io["L1_gnn_W1"]), (wn[:, GIN2, :], io["L1_gnn_W2"]),
                      (wn[:, WEDGE:WEDGE + 4, :], io["L2_gnn_W_edge"].rearrange("t o d -> o t d")),
                      (wn[:, GGIH:GGIH + 3, :], rows_of(io["L2_gnn_W_ih"])), (wn[:, GGHH:GGHH + 3, :], rows_of(io["L2_gnn_W_hh"])),
                      (w3[:, 0, :], io["L3_gnn_Wq"]), (w3[:, 1, :], io["L3_gnn_Wk"]), (w3[:, 2, :], io["L3_gnn_Wv"]),
                      (w3[:, 3, :], io["L3_gnn_Wo"]), (w3[:, 4:6, :], io["L3_gnn_W1"].rearrange("p (k f) -> p k f", f=P)),
                      (w3[:, 6:8, :], rows_of(io["L3_gnn_W2"]))]
            for vname, k in vec_list:
                full = f"L{vname[0]}_gnn_{vname[2:]}" if vname[0].isdigit() else f"L0_gnn_{vname}"
                loads.append((vrow[VEC[vname]:VEC[vname] + k, :], io[full].rearrange("(k f) -> k f", f=P)))
            one_row = "(a d) -> a d"
            loads += [(brow[:, 0:D], io["L0_gnn_bq"].rearrange(one_row, a=1)),
                      (brow[:, D:2 * D], io["L0_gnn_bk"].rearrange(one_row, a=1)),
                      (brow[:, 2 * D:3 * D], io["L0_gnn_bv"].rearrange(one_row, a=1)),
                      (brow[:, 3 * D:7 * D].rearrange("a (t d) -> a t d", t=4), io["L2_gnn_b_edge"].rearrange("(a t) d -> a t d", a=1)),
                      (brow[:, 7 * D:7 * D + 1], io["L1_gnn_eps"].rearrange(one_row, a=1))]

            with block("constants", s_load, s_const, s_wt, s_wcopy, s_xl, s_rows) as b:
                @b.sync
                def _(sp):
                    for to, of in loads:
                        sp.dma_start(to, of).then_inc(s_load, 16)

                @b.gpsimd
                def _(pool):
                    pool.memset(ident[:], 0.0).then_inc(s_const, 1)
                    pool.wait_ge(s_const, 1)
                    pool.affine_select(out=ident[:], in_=ident[:], compare_op=ALU.not_equal, fill=1.0, base=0,
                                       pattern=[[-1, P]], channel_multiplier=1).then_inc(s_const, 1)
                    pool.memset(ones[:], 1.0).then_inc(s_const, 1)
                    pool.iota(iota_row[:], [[1, P]], base=0, channel_multiplier=0,
                              allow_small_or_imprecise_dtypes=True).then_inc(s_const, 1)
                    pool.memset(xrows[:, FULL_BLOCKS, :], 0.0).then_inc(s_const, 1)
                    pool.wait_ge(s_const, 5)
                    pool.dma_start(xrows[0:TAIL, FULL_BLOCKS, :], io["x"][FULL_BLOCKS * P:N, :]).then_inc(s_xl, 16)
                    pool.dma_start(xrows[:, 0:FULL_BLOCKS, :],
                                   io["x"][0:FULL_BLOCKS * P, :].rearrange("(b p) f -> p b f", p=P)).then_inc(s_xl, 16)
                    pool.wait_ge(s_xl, 32)

                n_wt = -(-NW // 4)
                n_x = BLOCKS // 4

                @b.tensor
                def _(pe):
                    pe.wait_ge(s_const, 5)
                    pe.wait_ge(s_load, 16 * len(loads))
                    for g in range(n_wt):
                        if g >= 4:
                            pe.wait_ge(s_wcopy, g - 3)
                        for k in range(4 * g, min(4 * g + 4, NW)):
                            ins = pe.transpose(psum[:, g % 4, (k % 4) * P:(k % 4 + 1) * P], wn[:, k, :], ident[:])
                        ins.then_inc(s_wt, 1)
                    pe.wait_ge(s_xl, 32)
                    for g in range(n_x):
                        pe.wait_ge(s_wcopy, n_wt + g - 3)
                        for k in range(4):
                            ins = pe.transpose(psum[:, (n_wt + g) % 4, k * P:(k + 1) * P], xrows[:, 4 * g + k, :], ident[:])
                        ins.then_inc(s_wt, 1)
                    pe.transpose(psum[:, 4, 0:n_vec], vrow[:], ident[0:n_vec, 0:n_vec])
                    pe.matmul(psum[:, 5, 0:3 * D], ones[0:1, :], brow[:, 0:3 * D], start=True, stop=True)
                    pe.matmul(psum[:, 6, :], ones[0:1, :], brow[:, 3 * D:7 * D], start=True, stop=True)
                    pe.matmul(psum[:, 7, 0:1], ones[0:1, :], brow[:, 7 * D:7 * D + 1], start=True, stop=True).then_inc(s_wt, 1)

                @b.scalar
                def _(act):
                    for g in range(n_wt):
                        n = min(4, NW - 4 * g)
                        act.wait_ge(s_wt, g + 1)
                        act.copy(wt[:, 4 * g:4 * g + n, :], bank4(psum[:, g % 4, 0:n * P])).then_inc(s_wcopy, 1)
                    for g in range(n_x):
                        act.wait_ge(s_wt, n_wt + g + 1)
                        act.copy(resT[:, g * CHUNK:(g + 1) * CHUNK], psum[:, (n_wt + g) % 4, :]).then_inc(s_wcopy, 1)

                @b.vector
                def _(dve):
                    dve.wait_ge(s_wt, n_wt + n_x + 1)
                    dve.tensor_copy(vec[:], psum[:, 4, 0:n_vec]).then_inc(s_rows, 1)
                    dve.tensor_copy(bq_rows[:], psum[:, 5, 0:D]).then_inc(s_rows, 1)
                    dve.tensor_copy(bk_rows[:], psum[:, 5, D:2 * D]).then_inc(s_rows, 1)
                    dve.tensor_copy(bv_rows[:], psum[:, 5, 2 * D:3 * D]).then_inc(s_rows, 1)
                    dve.tensor_copy(bedge_rows[:], psum[:, 6, :]).then_inc(s_rows, 1)
                    dve.tensor_scalar(eps_col[:], psum[:, 7, 0:1], 1.0, None, ALU.add).then_inc(s_rows, 1)
                    dve.wait_ge(s_rows, 1)
                    for k, (ih, hh) in enumerate((("b_ih", "b_hh"), ("2_b_ih", "2_b_hh"))):
                        dve.tensor_tensor(gate_bias[:, k, :], vec[:, VEC[ih]:VEC[ih] + 2], vec[:, VEC[hh]:VEC[hh] + 2],
                                          ALU.add).then_inc(s_rows, 1)

        s_in, s_dve, s_pe, s_mid, s_row, s_g = sems("edges_loaded", "table_step", "table_turned", "table_rows_made",
                                                    "table_rows_stored", "table_rows_gathered")
        with ExitStack() as tmp:
            per_p = E // P
            ea4 = t1[:, 0:4 * per_p].rearrange("p (e c) -> p e c", c=4)
            eq = xT[:, 0:3 * per_p].rearrange("p (c e) -> p c e", c=3)
            amax, etype = hT[:, 0:per_p], hT[:, per_p:2 * per_p]
            last_dst = sb("last_dst", [1, TILES], I32, tmp)
            last_block = sb("last_block", [1, TILES], I32, tmp)
            reach = sb("reach", [1, TILES], F32, tmp)
            tile_no = sb("tile_no", [1, TILES], F32, tmp)
            reach_all = acc[0:ROW_K, 0:TILES]
            passed = acc[0:ROW_K, TILES:2 * TILES]
            step_no = sb("step_no", [ROW_K, ROW_C], F32, tmp)
            tile_f = sb("tile_f", [ROW_K, ROW_C], F32, tmp)
            block_f = sb("block_f", [ROW_K, ROW_C], F32, tmp)
            tile_i = sb("tile_i", [ROW_K, ROW_C], I32, tmp)
            row_i = sb("row_i", [ROW_K, ROW_C], I32, tmp)
            block_i = sb("block_i", [ROW_K, ROW_C], I32, tmp)
            base_f = sb("base_f", [ROW_K, ROW_C], F32, tmp)
            src_i = sb("src_i", [ROW_K, ROW_C, P], I32, tmp)
            dst_i = sb("dst_i", [ROW_K, ROW_C, P], I32, tmp)
            typ_f = sb("typ_f", [ROW_K, ROW_C, P], F32, tmp)
            src_f = sb("src_f", [ROW_K, ROW_C, P], F32, tmp)
            dst_f = sb("dst_f", [ROW_K, ROW_C, P], F32, tmp)
            loc_f = sb("loc_f", [ROW_K, ROW_C, P], F32, tmp)
            key = sb("key", [ROW_K, ROW_C, P], F32, tmp)
            same = sb("same", [ROW_K, ROW_C, P], F32, tmp)
            ends = sb("ends", [ROW_K, 3, ROW_C], F32, tmp)
            ends_row = acc[0:GAT_HEADS, 2 * TILES:2 * TILES + 3 * STEPS].rearrange("h (a s) -> h a s", a=3)
            goes_on = acc[0:GAT_HEADS, 2 * TILES + 3 * STEPS:2 * TILES + 4 * STEPS + 1]

            with block("step_tables", s_in, s_dve, s_pe, s_mid, s_row, s_g) as b:
                @b.sync
                def _(sp):
                    sp.dma_start(ea4, io["edge_attr_4"].rearrange("(p e) c -> p e c", p=P)).then_inc(s_in, 16)
                    with nc.allow_non_contiguous_dma(reason="the last dst of each tile"):
                        sp.dma_start(last_dst[:], io["dst"].rearrange("(a t p) -> a t p", a=1, p=P)[:, :, P - 1]).then_inc(s_in, 16)
                    sp.wait_ge(s_mid, 1)
                    sp.dma_start(type_dram.ap().rearrange("t p -> (t p)").rearrange("(p e) -> p e", p=P), etype).then_inc(s_row, 16)
                    sp.wait_ge(s_mid, 2)
                    with nc.allow_non_contiguous_dma(reason="tables by step, once"):
                        sp.dma_start(step_block_dram.ap().rearrange("a (c k) -> k (a c)", k=ROW_K), block_i[:]).then_inc(s_row, 16)
                        sp.dma_start(step_row_dram.ap().rearrange("a (c k) -> k (a c)", k=ROW_K), row_i[:]).then_inc(s_row, 16)
                        sp.wait_ge(s_mid, 3)
                        sp.dma_start(ends_dram.ap().rearrange("a (c k) -> k a c", k=ROW_K), ends[:]).then_inc(s_row, 16)
                    sp.wait_ge(s_row, 64)
                    sp.dma_start(step_block[:], step_block_dram[:]).then_inc(s_in, 16)
                    sp.dma_start(step_row[:], step_row_dram[:]).then_inc(s_in, 16)
                    for h in range(GAT_HEADS):
                        sp.dma_start(ends_row[h:h + 1, :, :], ends_dram.ap().rearrange("(o a) s -> o a s", o=1)).then_inc(s_in, 16)
                    sp.wait_ge(s_in, 32 + 32 + 16 * GAT_HEADS)

                @b.gpsimd
                def _(pool):
                    pool.iota(tile_no[:], [[1, TILES]], base=0, channel_multiplier=0,
                              allow_small_or_imprecise_dtypes=True).then_inc(s_pe, 1)
                    pool.iota(step_no[:], [[ROW_K, ROW_C]], base=0, channel_multiplier=1,
                              allow_small_or_imprecise_dtypes=True).then_inc(s_pe, 1)
                    pool.wait_ge(s_mid, 2)
                    for c in range(ROW_C):
                        at = bass.IndirectOffsetOnAxis(ap=tile_i[:, c:c + 1], axis=0)
                        pool.indirect_dma_start(out=src_i[:, c, :], out_offset=None, in_=io["src"].rearrange("(t p) -> t p", p=P),
                                                in_offset=at).then_inc(s_g, 16)
                        pool.indirect_dma_start(out=dst_i[:, c, :], out_offset=None, in_=io["dst"].rearrange("(t p) -> t p", p=P),
                                                in_offset=at).then_inc(s_g, 16)
                    pool.wait_ge(s_row, 64)
                    for c in range(ROW_C):
                        at = bass.IndirectOffsetOnAxis(ap=tile_i[:, c:c + 1], axis=0)
                        pool.indirect_dma_start(out=typ_f[:, c, :], out_offset=None, in_=type_dram[:], in_offset=at).then_inc(s_g, 16)

                @b.vector
                def _(dve):
                    n = [0]

                    def link(ins):
                        n[0] += 1
                        ins.then_inc(s_dve, 1)
                        dve.wait_ge(s_dve, n[0])

                    dve.wait_ge(s_in, 32)
                    dve.wait_ge(s_pe, 2)
                    link(dve.tensor_scalar(last_block[:], last_dst[:], P.bit_length() - 1, None, ALU.logical_shift_right))
                    link(dve.tensor_copy(reach[:], last_block[:]))
                    link(dve.tensor_tensor(reach[:], reach[:], tile_no[:], ALU.add))
                    dve.wait_ge(s_pe, 3)
                    link(dve.tensor_copy(reach_all[:, 0:CHUNK], psum[0:ROW_K, 0, :]))
                    link(dve.tensor_copy(reach_all[:, CHUNK:TILES], psum[0:ROW_K, 1, 0:TILES - CHUNK]))
                    for c in range(ROW_C):
                        link(dve.tensor_scalar(passed, reach_all, step_no[:, c:c + 1], None, ALU.is_lt))
                        link(dve.tensor_reduce(tile_f[:, c:c + 1], passed, AX_X, ALU.add))
                    link(dve.tensor_scalar(tile_f[:], tile_f[:], float(TILES - 1), None, ALU.min))
                    link(dve.tensor_tensor(block_f[:], step_no[:], tile_f[:], ALU.subtract))
                    link(dve.tensor_scalar(block_f[:], block_f[:], float(BLOCKS), None, ALU.min))
                    link(dve.tensor_scalar(base_f[:], tile_f[:], float(P), None, ALU.mult))
                    link(dve.tensor_copy(row_i[:], base_f[:]))
                    link(dve.tensor_scalar(base_f[:], block_f[:], float(P), None, ALU.mult))
                    link(dve.tensor_copy(tile_i[:], tile_f[:]))
                    link(dve.tensor_reduce(amax, ea4, AX_X, ALU.max))
                    for t in range(3):
                        link(dve.tensor_tensor(eq[:, t, :], ea4[:, :, t], amax, ALU.is_equal))
                    link(dve.tensor_scalar(etype, eq[:, 2, :], -1.0, 2.0, ALU.mult, ALU.add))
                    for t in (1, 0):
                        link(dve.tensor_scalar(eq[:, t, :], eq[:, t, :], -1.0, 1.0, ALU.mult, ALU.add))
                        link(dve.tensor_tensor(etype, etype, eq[:, t, :], ALU.mult))
                        if t == 1:
                            link(dve.tensor_scalar(etype, etype, 1.0, None, ALU.add))
                    dve.sem_inc(s_mid, 1)
                    dve.tensor_copy(block_i[:], block_f[:]).then_inc(s_mid, 1)
                    dve.wait_ge(s_g, 16 * 2 * ROW_C)
                    link(dve.tensor_copy(src_f[:], src_i[:]))
                    link(dve.tensor_copy(dst_f[:], dst_i[:]))
                    for c in range(ROW_C):
                        link(dve.tensor_scalar(loc_f[:, c, :], dst_f[:, c, :], base_f[:, c:c + 1], None, ALU.subtract))
                    link(dve.tensor_scalar(key[:], loc_f[:], 0.0, None, ALU.is_ge))
                    link(dve.tensor_scalar(same[:], loc_f[:], float(P - 1), None, ALU.is_le))
                    link(dve.tensor_tensor(key[:], key[:], same[:], ALU.mult))
                    link(dve.tensor_scalar(dst_f[:], dst_f[:], 1.0, None, ALU.add))
                    link(dve.tensor_tensor(key[:], key[:], dst_f[:], ALU.mult))
                    link(dve.tensor_scalar(key[:], key[:], -1.0, None, ALU.add))
                    link(dve.memset(same[:], 1.0))
                    link(dve.tensor_tensor(same[:, :, 1:P], key[:, :, 1:P], key[:, :, 0:P - 1], ALU.is_equal))
                    link(dve.tensor_reduce(ends[:, 2, :], same[:], AX_X, ALU.min))
                    link(dve.tensor_copy(ends[:, 0, :], key[:, :, 0]))
                    link(dve.tensor_copy(ends[:, 1, :], key[:, :, P - 1]))
                    dve.sem_inc(s_mid, 1)
                    pf = key_pen_f[:].rearrange("k (c p) -> k c p", p=P)
                    pb = key_pen_b[:].rearrange("k (c p) -> k c p", p=P)
                    link(dve.memset(key_pen_f[:], -BIG))
                    link(dve.memset(key_pen_b[:], -BIG))
                    link(dve.tensor_scalar(pf[:, :, 1:P], same[:, :, 1:P], 1.0, BIG, ALU.subtract, ALU.mult))
                    link(dve.tensor_scalar(pb[:, :, 0:P - 1], same[:, :, 1:P], 1.0, BIG, ALU.subtract, ALU.mult))
                    for c in range(ROW_C):
                        for to, end in ((first_pen, 0), (last_pen, 1)):
                            link(dve.tensor_scalar(to[:, c, :], key[:, c, :], ends[:, end, c:c + 1], 1.0, ALU.is_equal, ALU.subtract))
                            link(dve.tensor_scalar(to[:, c, :], to[:, c, :], BIG, None, ALU.mult))
                    dve.wait_ge(s_in, 32 + 32 + 16 * GAT_HEADS)
                    link(dve.memset(goes_on, 0.0))
                    link(dve.tensor_tensor(goes_on[:, 1:STEPS], ends_row[:, 0, 1:STEPS], ends_row[:, 1, 0:STEPS - 1], ALU.is_equal))
                    for d in range(2):
                        link(dve.tensor_scalar(enter_pen[:, d, :], goes_on[:, d:STEPS + d], 1.0, BIG, ALU.subtract, ALU.mult))
                        link(dve.tensor_tensor(chain_pen[:, d, :], goes_on[:, d:STEPS + d], ends_row[:, 2, :], ALU.mult))
                        link(dve.tensor_scalar(chain_pen[:, d, :], chain_pen[:, d, :], 1.0, BIG, ALU.subtract, ALU.mult))
                    dve.wait_ge(s_g, 16 * 3 * ROW_C)
                    link(dve.scalar_tensor_tensor(out=typ_f[:], in0=src_f[:], scalar=4.0, in1=typ_f[:], op0=ALU.mult, op1=ALU.add))
                    link(dve.memset(dst_local[:, STEPS:PADDED], -1.0))
                    link(dve.memset(src_idx[:, STEPS:PADDED], 0))
                    dve.sem_inc(s_mid, 1)
                    for k, (to, of) in enumerate(((src_idx, 2), (typed_idx, 4), (dst_local, 6))):
                        dve.wait_ge(s_pe, 4 + k)
                        n_bank = CHUNK // ROW_K
                        link(dve.tensor_copy(to[:, 0:n_bank * ROW_K], psum[:, of, 0:n_bank * ROW_K]))
                        link(dve.tensor_copy(to[:, n_bank * ROW_K:STEPS], psum[:, of + 1, 0:STEPS - n_bank * ROW_K]))

                @b.tensor
                def _(pe):
                    pe.wait_ge(s_dve, 3)
                    pe.matmul(psum[0:ROW_K, 0, :], ones[0:1, 0:ROW_K], reach[:, 0:CHUNK], start=True, stop=True)
                    pe.matmul(psum[0:ROW_K, 1, 0:TILES - CHUNK], ones[0:1, 0:ROW_K], reach[:, CHUNK:TILES],
                              start=True, stop=True).then_inc(s_pe, 1)
                    pe.wait_ge(s_mid, 4)
                    n_bank = CHUNK // ROW_K
                    for of, bank in ((src_f, 2), (typ_f, 4), (loc_f, 6)):
                        for c in range(ROW_C):
                            at = (c % n_bank) * ROW_K
                            ins = pe.transpose(psum[:, bank + c // n_bank, at:at + ROW_K], of[:, c, :], ident[0:ROW_K, 0:ROW_K])
                        ins.then_inc(s_pe, 1)

        def at_least(eng, sem, value):
            if not (isinstance(value, int) and value <= 0):
                eng.wait_ge(sem, value)

        def turns(eng, body):
            body(0)
            with eng.Fori(1, LOOPS - 1) as i:
                body(i)
            body(LOOPS - 1)

        def led(i, r, lead=2):
            i2, r2 = i + (r + lead) // REGIONS, (r + lead) % REGIONS
            return None if isinstance(i2, int) and i2 >= LOOPS else (i2, r2)

        def step_of(i, r, u=0):
            return i * (REGIONS * GROUP) + (r * GROUP + u)

        def region_of(i, r):
            return i * REGIONS + r

        ROWS = LOOPS * GROUP * 16

        def landed(i, base):
            return base + (i + 1) * (GROUP * 16)

        def acc_rows(c, lo, n):
            return acc[:, bass.ds(c * (4 * ACC_W), 4 * ACC_W)].rearrange("p (b w) -> p b w", w=ACC_W)[:, :, lo:lo + n]

        def cols(c):
            return bass.ds(c * CHUNK, CHUNK)

        V = 2
        def pairs(eng, *stages):
            def turn(i):
                for stage in stages:
                    for u in range(V):
                        stage(i * V + u, u, i)
            turn(0)
            with eng.Fori(1, CHUNKS // V) as i:
                turn(i)

        ln_summed, ln_centred, ln_squared, ln_varied, ln_rooted, ln_inverse, ln_spread, ln_normed, ln_done, ln_eps = sems(
            "ln_summed", "ln_centred", "ln_squared", "ln_varied", "ln_rooted", "ln_inverse", "ln_spread", "ln_normed", "ln_done", "ln_eps")

        def layer_norm(name, src, dst, eps, gain=None, shift=None, also=None):
            with ExitStack() as tmp:
                xc = acc[:, 0:U * CHUNK].rearrange("p (u f) -> p u f", u=U)
                sq = acc[:, U * CHUNK:2 * U * CHUNK].rearrange("p (u f) -> p u f", u=U)
                std = sb(f"{name}_std", [P, 4 * U], F32, tmp)
                eps_t = sb(f"{name}_eps", [P, 1], F32, tmp)
                with block(name, ln_summed, ln_centred, ln_squared, ln_varied, ln_rooted, ln_inverse, ln_spread, ln_normed, ln_done,
                           ln_eps) as b:
                    @b.tensor
                    def _(pe):
                        with pe.Fori(0, CHUNKS // U) as i:
                            for u in range(U):
                                if u >= 3:
                                    pe.wait_ge(ln_centred, i * U + (u - 2))
                                pe.matmul(psum[:, u % 3, :], ones[:], src[:, cols(i * U + u)], start=True, stop=True).then_inc(ln_summed, 1)
                            for u in range(U):
                                pe.wait_ge(ln_squared, i * U + (u + 1))
                                for k in range(4):
                                    ins = pe.matmul(psum[:, 3, 4 * u + k:4 * u + k + 1], sq[:, u, k * P:(k + 1) * P], ones[:, 0:1],
                                                    start=True, stop=True)
                            ins.then_inc(ln_varied, 1)
                            pe.wait_ge(ln_inverse, i + 1)
                            for u in range(U):
                                if u >= 4:
                                    pe.wait_ge(ln_normed, i * U + (u - 3))
                                for k in range(4):
                                    ins = pe.transpose(psum[:, 4 + u % 4, k * P:(k + 1) * P],
                                                       std[:, 4 * u + k:4 * u + k + 1].broadcast_to([P, P]), ident[:])
                                ins.then_inc(ln_spread, 1)
                            pe.wait_ge(ln_normed, i * U + U)

                    @b.scalar
                    def _(act):
                        act.wait_ge(ln_eps, 1)
                        with act.Fori(0, CHUNKS // U) as i:
                            for u in range(U):
                                act.wait_ge(ln_centred, i * U + (u + 1))
                                act.activation(sq[:, u, :], xc[:, u, :], ACT.Square).then_inc(ln_squared, 1)
                            act.wait_ge(ln_varied, i + 1)
                            act.activation(std[:], psum[:, 3, 0:4 * U], ACT.Sqrt, bias=eps_t[:], scale=1.0 / D).then_inc(ln_rooted, 1)
                            for u in range(U):
                                act.wait_ge(ln_normed, i * U + (u + 1))
                                for to in [dst] + ([also] if also is not None else []):
                                    if gain is None:
                                        ins = act.activation(to[:, cols(i * U + u)], xc[:, u, :], ACT.Relu)
                                    else:
                                        ins = act.activation(to[:, cols(i * U + u)], xc[:, u, :], ACT.Identity, bias=shift, scale=gain)
                                ins.then_inc(ln_done, 1)

                    @b.vector
                    def _(dve):
                        dve.memset(eps_t[:], eps).then_inc(ln_eps, 1)
                        with dve.Fori(0, CHUNKS // U) as i:
                            for u in range(U):
                                dve.wait_ge(ln_summed, i * U + (u + 1))
                                dve.scalar_tensor_tensor(out=xc[:, u, :], in0=psum[:, u % 3, :], scalar=-1.0 / D, in1=src[:, cols(i * U + u)],
                                                         op0=ALU.mult, op1=ALU.add).then_inc(ln_centred, 1)
                            dve.wait_ge(ln_rooted, i + 1)
                            dve.reciprocal(std[:], std[:]).then_inc(ln_inverse, 1)
                            for u in range(U):
                                dve.wait_ge(ln_spread, i * U + (u + 1))
                                dve.tensor_tensor(xc[:, u, :], xc[:, u, :], psum[:, 4 + u % 4, :], ALU.mult).then_inc(ln_normed, 1)
                            dve.wait_ge(ln_done, i * U + U)

        r_staged, r_turned, r_copied, r_query, r_bias = sems("rows_staged", "rows_turned", "rows_copied", "rows_query", "rows_bias")
        r_stored = sems(*(f"rows_stored{u}" for u in range(V)))

        def node_rows(name, src, queries):
            with ExitStack() as tmp:
                xs = sb(f"{name}_xs", [P, V, CHUNK], F32, tmp)
                rows = sb(f"{name}_rows", [P, V, CHUNK], F32, tmp)
                prod = sb(f"{name}_prod", [P, 4, D], F32, tmp)
                with block(name, r_staged, r_turned, r_copied, r_query, r_bias, *r_stored) as b:
                    @b.vector
                    def _(dve):
                        def stage(c, u, i):
                            at_least(dve, r_turned, c + 1 - V)
                            dve.tensor_scalar(xs[:, u, :], src[:, cols(c)], 0.0, None, ALU.add).then_inc(r_staged, 1)

                        def query(c, u, i):
                            dve.wait_ge(r_turned, c + 1)
                            q = t1[:, bass.ds(c * (4 * Q_W), 4 * Q_W)].rearrange("p (b w) -> p b w", w=Q_W)
                            dve.tensor_tensor(q[:, :, 0:D], bank4(psum[:, 4 + u, :]), bq_rows[:].unsqueeze(1).broadcast_to([P, 4, P]),
                                              ALU.add).then_inc(r_query, 1)
                            dve.wait_ge(r_query, c + 1)
                            at_least(dve, r_bias, c * 2)
                            dve.tensor_tensor(prod[:], q[:, :, 0:D], bk_rows[:].unsqueeze(1).broadcast_to([P, 4, P]), ALU.mult).then_inc(r_bias, 1)
                            dve.wait_ge(r_bias, c * 2 + 1)
                            dve.tensor_reduce(q[:, :, D:Q_W], prod[:].rearrange("p b (h e) -> p b h e", h=GAT_HEADS), AX_X, ALU.add).then_inc(r_bias, 1)
                        dve.memset(t1[:, BLOCKS * Q_W:], 0.0)
                        pairs(dve, *([stage, query] if queries else [stage]))

                    @b.tensor
                    def _(pe):
                        def turn(c, u, i):
                            pe.wait_ge(r_staged, c + 1)
                            at_least(pe, r_copied, c + 1 - V)
                            if queries:
                                at_least(pe, r_query, c + 1 - V)
                            for k in range(4):
                                at = slice(k * P, (k + 1) * P)
                                ins = pe.transpose(psum[:, u, at], xs[:, u, at], ident[:])
                                if queries:
                                    ins = pe.matmul(psum[:, 4 + u, at], xs[:, u, at], wt[:, WQ, :], start=True, stop=True)
                            ins.then_inc(r_turned, 1)
                        pairs(pe, turn)

                    @b.scalar
                    def _(act):
                        def copy(c, u, i):
                            act.wait_ge(r_turned, c + 1)
                            at_least(act, r_stored[u], i * 16)
                            act.copy(rows[:, u, :], psum[:, u, :]).then_inc(r_copied, 1)
                        pairs(act, copy)

                    @b.sync
                    def _(sp):
                        def leave(c, u, i):
                            sp.wait_ge(r_copied, c + 1)
                            sp.dma_start(table_x[cols(c), :].rearrange("(b p) f -> p b f", p=P), bank4(rows[:, u, :])).then_inc(r_stored[u], 16)
                        pairs(sp, leave)
                        for stored in r_stored:
                            sp.wait_ge(stored, 16 * (CHUNKS // V))

        def projected_rows(name, src, rhs, width, table, bias=None, query_width=0):
            left = width - query_width
            with ExitStack() as tmp:
                xs = sb(f"{name}_xs", [P, V, CHUNK], F32, tmp)
                rows = sb(f"{name}_rows", [P, V, 4, left], F32, tmp)
                with block(name, r_staged, r_turned, r_copied, r_query, *r_stored) as b:
                    @b.vector
                    def _(dve):
                        def stage(c, u, i):
                            at_least(dve, r_turned, (c + 1 - V) * 4)
                            dve.tensor_scalar(xs[:, u, :], src[:, cols(c)], 0.0, None, ALU.add).then_inc(r_staged, 1)

                        def add_bias(c, u, i):
                            at_least(dve, r_stored[u], i * 16)
                            for k in range(4):
                                dve.wait_ge(r_turned, c * 4 + (k + 1))
                                dve.tensor_tensor(rows[:, u, k, :], psum[:, 4 * u + k, 0:left], bias, ALU.add).then_inc(r_copied, 1)

                        def query(c, u, i):
                            for k in range(4):
                                dve.wait_ge(r_turned, c * 4 + (k + 1))
                                dve.tensor_scalar(t1[:, bass.ds(c * CHUNK + k * P, P)], psum[:, 4 * u + k, 0:query_width],
                                                  0.0, None, ALU.add).then_inc(r_query, 1)
                        dve.memset(t1[:, NP:ACC_BLOCKS * D], 0.0)
                        pairs(dve, stage, add_bias if bias is not None else query)

                    @b.tensor
                    def _(pe):
                        def project(c, u, i):
                            pe.wait_ge(r_staged, c + 1)
                            for k in range(4):
                                at_least(pe, r_copied, (c - V) * 4 + (k + 1))
                                if query_width:
                                    at_least(pe, r_query, (c - V) * 4 + (k + 1))
                                pe.matmul(psum[:, 4 * u + k, 0:width], xs[:, u, k * P:(k + 1) * P], rhs, start=True, stop=True).then_inc(r_turned, 1)
                        pairs(pe, project)

                    if bias is None:
                        @b.scalar
                        def _(act):
                            def copy(c, u, i):
                                at_least(act, r_stored[u], i * 16)
                                for k in range(4):
                                    act.wait_ge(r_query, c * 4 + (k + 1))
                                    act.copy(rows[:, u, k, :], psum[:, 4 * u + k, query_width:width]).then_inc(r_copied, 1)
                            pairs(act, copy)

                    @b.sync
                    def _(sp):
                        def leave(c, u, i):
                            sp.wait_ge(r_copied, c * 4 + 4)
                            sp.dma_start(table[cols(c), :].rearrange("(b p) f -> p b f", p=P), rows[:, u, :, :]).then_inc(r_stored[u], 16)
                        pairs(sp, leave)
                        for stored in r_stored:
                            sp.wait_ge(stored, 16 * (CHUNKS // V))

        p_index, p_selected, p_mixed, p_turned, p_spread, p_projected = sems(
            "index_copied", "selected", "mixed", "edges_turned", "turned_copied", "projected")
        p_evacuated, p_multiplied, p_scored, p_score_kept = sems("evacuated", "multiplied", "scored", "score_kept")
        p_weight, p_weighted, p_summed, p_added = sems("weight_placed", "weighted", "summed", "added")
        p_in = sems(*(f"edge_rows_in{r}" for r in range(REGIONS)))
        p_out = sems(*(f"values_out{r}" for r in range(REGIONS)))
        select = sb("select", [P, REGIONS, GROUP, P])
        index = sb("index", [P, REGIONS, GROUP], I32)
        score = sb("score", [P, STEPS, GAT_HEADS])

        def copy_index(eng, table, i, r, base=None, freed=None):
            if freed is not None:
                if not (isinstance(i, int) and i == 0):
                    eng.wait_ge(gathered[r], landed(i - 1, base))
                at_least(eng, freed, region_of(i, r) - (REGIONS - 1))
            copy = eng.copy if freed is not None else eng.tensor_copy
            copy(index[:, r, :], table[:, bass.ds(step_of(i, r), GROUP)]).then_inc(p_index, 1)

        def gathers(pool, ring, table):
            def body(i):
                for r in range(0, REGIONS, 2):
                    pool.wait_ge(p_index, region_of(i, r) + 2)
                    pool.sem_inc(gather_go, 1)
                    for at in (r, r + 1):
                        for u in range(GROUP):
                            pool.indirect_dma_start(out=ring[:, at, u, :], out_offset=None, in_=table,
                                                    in_offset=bass.IndirectOffsetOnAxis(ap=index[:, at, u:u + 1], axis=0)
                                                    ).then_inc(gathered[at], 16)
            turns(pool, body)

        def make_select(dve, i, r, lo=0, n=GROUP):
            dve.tensor_tensor(select[:, r, lo:lo + n, :], iota_row[:].unsqueeze(1).broadcast_to([P, n, P]),
                              dst_local[:, bass.ds(step_of(i, r, lo), n)].unsqueeze(2).broadcast_to([P, n, P]),
                              ALU.is_equal).then_inc(p_selected, 1)

        loaded = count()

        def by_step(eng, table, i, r, top):
            regs = [eng.alloc_register(name=f"{table.name}_of_step{next(loaded)}") for _ in range(GROUP)]
            eng.load(regs, table[0:1, bass.ds(step_of(i, r), GROUP)])
            return [eng.snap(reg, donate=True).with_bounds(min_val=0, max_val=top) for reg in regs]

        def blocks_of(eng, i, r):
            return by_step(eng, step_block, i, r, BLOCKS)

        def add_blocks(dve, sums, i, r, width, between=()):
            blocks = blocks_of(dve, i, r)
            dve.wait_ge(p_summed, region_of(i, r) + 1)
            for u in range(GROUP):
                to = acc[:, bass.ds(blocks[u] * ACC_W, width)]
                at_least(dve, p_added, region_of(i, r) * GROUP + u)
                dve.tensor_tensor(to, to, sums(r, u), ALU.add).then_inc(p_added, 1)
                if u < len(between):
                    between[u]()

        def sum_pass(name, table, idx, base):
            with ExitStack() as tmp:
                ring = sb(f"{name}_ring", [P, REGIONS, GROUP, D], F32, tmp)

                def sums(r, u):
                    return psum[:, r, u * P:(u + 1) * P]

                with block(name, p_index, p_selected, p_summed, p_added) as b:
                    @b.gpsimd
                    def _(pool):
                        gathers(pool, ring, table)

                    @b.scalar
                    def _(act):
                        turns(act, lambda i: [copy_index(act, idx, i, r, base, p_summed) for r in range(REGIONS)])

                    @b.vector
                    def _(dve):
                        dve.memset(acc[:], 0.0)
                        make_select(dve, 0, 0)
                        def body(i):
                            for r in range(REGIONS):
                                if nxt := led(i, r, 1):
                                    make_select(dve, *nxt)
                                add_blocks(dve, sums, i, r, D)
                        turns(dve, body)

                    @b.tensor
                    def _(pe):
                        def body(i):
                            for r in range(REGIONS):
                                pe.wait_ge(p_selected, region_of(i, r) + 1)
                                pe.wait_ge(gathered[r], landed(i, base))
                                at_least(pe, p_added, (region_of(i, r) - (REGIONS - 1)) * GROUP)
                                for u in range(GROUP):
                                    ins = pe.matmul(sums(r, u), select[:, r, u, :], ring[:, r, u, :], start=True, stop=True)
                                ins.then_inc(p_summed, 1)
                        turns(pe, body)

        def gat_score_pass(name, base):
            with ExitStack() as tmp:
                RING = REGIONS * GROUP * D
                ring = acc[:, 0:RING].rearrange("p (r u f) -> p r u f", r=REGIONS, u=GROUP)
                attr = acc[:, RING:2 * RING].rearrange("p (r u f) -> p r u f", r=REGIONS, u=GROUP)
                spread = sb(f"{name}_spread", [P, 2, GROUP, P], F32, tmp)
                mixT = sb(f"{name}_mixT", [P, REGIONS, GROUP, P], F32, tmp)
                key = sb(f"{name}_key", [P, 2, GROUP, D], F32, tmp)
                prod = sb(f"{name}_prod", [P, GROUP, D], F32, tmp)
                part = sb(f"{name}_part", [P, GROUP, GAT_HEADS], F32, tmp)
                pair = GROUP // 2

                def keys(r):
                    return bank4(psum[:, 2 + r % 2, :])

                def queries(r):
                    return psum[:, 4 + 2 * (r % 2):6 + 2 * (r % 2), 0:pair * Q_W].rearrange("p a (b w) -> p a b w", w=Q_W)

                with block(name, p_index, p_selected, p_mixed, p_turned, p_spread, p_projected, p_evacuated, p_multiplied, p_scored,
                           p_score_kept, *p_in, *p_out) as b:
                    @b.gpsimd
                    def _(pool):
                        gathers(pool, ring, table_x[:])

                    @b.sync
                    def _(sp):
                        def load(i, r):
                            at_least(sp, p_mixed, region_of(i, r) - (REGIONS - 1))
                            for u, row in enumerate(by_step(sp, step_row, i, r, E - P)):
                                sp.dma_start(attr[:, r, u, :], io["edge_attr_128"][bass.ds(row, P), :]).then_inc(p_in[r], 16)

                        def body(i):
                            for r in range(REGIONS):
                                if nxt := led(i, r, 3):
                                    load(*nxt)
                                sp.wait_ge(p_spread, region_of(i, r) + 1)
                                sp.dma_start(rows_dram[bass.ds(region_of(i, r), 1), :, :].rearrange("a p (u f) -> (a p) u f", f=D),
                                             mixT[:, r, :, :]).then_inc(p_out[r], 16)
                        for r in range(3):
                            load(0, r)
                        turns(sp, body)
                        for r in range(REGIONS):
                            sp.wait_ge(p_out[r], 16 * LOOPS)

                    @b.scalar
                    def _(act):
                        def turned(i, r):
                            act.wait_ge(p_turned, region_of(i, r) + 1)
                            if not (isinstance(i, int) and i == 0):
                                act.wait_ge(p_out[r], i * 16)
                            at_least(act, p_projected, region_of(i, r) - 1)
                            act.copy(spread[:, r % 2, :, :], bank4(psum[:, 0, :]))
                            act.copy(mixT[:, r, :, :], bank4(psum[:, 1, :])).then_inc(p_spread, 1)

                        def body(i):
                            for r in range(REGIONS):
                                if nxt := led(i, r, 1):
                                    turned(*nxt)
                                act.wait_ge(p_projected, region_of(i, r) + 1)
                                at_least(act, p_multiplied, region_of(i, r) - 1)
                                act.copy(key[:, r % 2, :, :], keys(r)).then_inc(p_evacuated, 1)
                        turned(0, 0)
                        turns(act, body)

                    @b.vector
                    def _(dve):
                        def lead(i, r):
                            at_least(dve, p_turned, region_of(i, r) - (REGIONS - 1))
                            make_select(dve, i, r)
                            dve.wait_ge(gathered[r], landed(i, base))
                            dve.wait_ge(p_in[r], (i + 1) * (16 * GROUP))
                            dve.tensor_tensor(ring[:, r, :, :], ring[:, r, :, :], attr[:, r, :, :], ALU.add).then_inc(p_mixed, 1)

                        def ask(i, r):
                            dve.wait_ge(p_turned, region_of(i, r) + 1)
                            if nxt := led(i, r, REGIONS):
                                copy_index(dve, src_idx, *nxt)

                        def body(i):
                            for r in range(REGIONS):
                                ask(i, r)
                                if nxt := led(i, r):
                                    lead(*nxt)
                                j = region_of(i, r)
                                dve.wait_ge(p_evacuated, j + 1)
                                at_least(dve, p_scored, j)
                                dve.tensor_tensor(prod[:].rearrange("p (a b) f -> p a b f", a=2),
                                                  key[:, r % 2, :, :].rearrange("p (a b) f -> p a b f", a=2), queries(r)[:, :, :, 0:D],
                                                  ALU.mult).then_inc(p_multiplied, 1)
                                dve.wait_ge(p_multiplied, j + 1)
                                at_least(dve, p_score_kept, j)
                                dve.tensor_reduce(part[:], prod[:].rearrange("p u (h e) -> p u h e", h=GAT_HEADS), AX_X, ALU.add).then_inc(p_scored, 1)
                                dve.wait_ge(p_scored, j + 1)
                                dve.tensor_tensor(score[:, bass.ds(step_of(i, r), GROUP), :].rearrange("p (a b) h -> p a b h", a=2),
                                                  part[:].rearrange("p (a b) h -> p a b h", a=2), queries(r)[:, :, :, D:Q_W],
                                                  ALU.add).then_inc(p_score_kept, 1)
                        for r in range(REGIONS):
                            copy_index(dve, src_idx, 0, r)
                        lead(0, 0)
                        lead(0, 1)
                        turns(dve, body)

                    @b.tensor
                    def _(pe):

                        def turn(i, r):
                            j = region_of(i, r)
                            pe.wait_ge(p_mixed, j + 1)
                            at_least(pe, p_spread, j)
                            for u in range(GROUP):
                                pe.transpose(psum[:, 0, u * P:(u + 1) * P], select[:, r, u, :], ident[:])
                            for u in range(GROUP):
                                ins = pe.transpose(psum[:, 1, u * P:(u + 1) * P], ring[:, r, u, :], ident[:])
                            ins.then_inc(p_turned, 1)

                        def body(i):
                            for r in range(REGIONS):
                                j = region_of(i, r)
                                if nxt := led(i, r, 1):
                                    turn(*nxt)
                                blocks = blocks_of(pe, i, r)
                                pe.wait_ge(p_spread, j + 1)
                                at_least(pe, p_score_kept, j - 1)
                                for u in range(GROUP):
                                    pe.matmul(keys(r)[:, u, :], mixT[:, r, u, :], wt[:, WK, :], start=True, stop=True)
                                for u in range(GROUP):
                                    q = t1[:, bass.ds(blocks[u] * Q_W, Q_W)]
                                    ins = pe.matmul(queries(r)[:, u // pair, u % pair, :], spread[:, r % 2, u, :], q, start=True, stop=True)
                                ins.then_inc(p_projected, 1)
                        turn(0, 0)
                        turns(pe, body)

        def gat_value_pass(name):
            W = D + GAT_HEADS
            with ExitStack() as tmp:
                ring = sb(f"{name}_ring", [P, REGIONS, GROUP, D], F32, tmp)
                msg = sb(f"{name}_msg", [P, REGIONS, GROUP, W], F32, tmp)

                def values(r):
                    return psum[:, r % 2, :].rearrange("p (u f) -> p u f", f=D)

                def sums(r, u):
                    return psum[:, 2 + 2 * (r % 2) + u // 2, (u % 2) * W:(u % 2 + 1) * W]

                with block(name, p_selected, p_weight, p_weighted, p_summed, p_added, p_projected, *p_in) as b:
                    @b.sync
                    def _(sp):
                        def body(i):
                            for r in range(REGIONS):
                                at_least(sp, p_projected, region_of(i, r) - (REGIONS - 1))
                                sp.dma_start(ring[:, r, :, :], rows_dram[bass.ds(region_of(i, r), 1), :, :].rearrange(
                                    "a p (u f) -> (a p) u f", f=D)).then_inc(p_in[r], 16)
                        turns(sp, body)

                    @b.scalar
                    def _(act):
                        def body(i):
                            for r in range(REGIONS):
                                at_least(act, p_summed, region_of(i, r) - (REGIONS - 1))
                                act.copy(msg[:, r, :, D:W], score[:, bass.ds(step_of(i, r), GROUP), :]).then_inc(p_weight, 1)
                        turns(act, body)

                    @b.vector
                    def _(dve):

                        def weigh(i, r):
                            dve.tensor_tensor(msg[:, r, :, 0:D].rearrange("p u (h e) -> p u h e", h=GAT_HEADS),
                                              values(r).rearrange("p u (h e) -> p u h e", h=GAT_HEADS),
                                              msg[:, r, :, D:W].unsqueeze(3).broadcast_to([P, GROUP, GAT_HEADS, D // GAT_HEADS]),
                                              ALU.mult).then_inc(p_weighted, 1)
                        half = GROUP // 2
                        dve.memset(acc[:], 0.0)
                        make_select(dve, 0, 0, 0, half)
                        make_select(dve, 0, 0, half, half)

                        def body(i):
                            for r in range(REGIONS):
                                dve.wait_ge(p_projected, region_of(i, r) + 1)
                                dve.wait_ge(p_weight, region_of(i, r) + 1)
                                weigh(i, r)
                                nxt, last = led(i, r, 1), led(i, r, -1)
                                between = []
                                if nxt:
                                    at_least(dve, p_summed, region_of(*nxt) - (REGIONS - 1))
                                    between = [lambda: make_select(dve, *nxt, 0, half), lambda: make_select(dve, *nxt, half, half)]
                                if isinstance(last[0], int) and last[0] < 0:
                                    for piece in between:
                                        piece()
                                else:
                                    add_blocks(dve, sums, *last, W, between)
                        turns(dve, body)
                        add_blocks(dve, sums, LOOPS - 1, REGIONS - 1, W)

                    @b.tensor
                    def _(pe):
                        def project(i, r):
                            pe.wait_ge(p_in[r], (i + 1) * 16)
                            at_least(pe, p_weighted, region_of(i, r) - 1)
                            for u in range(GROUP):
                                ins = pe.matmul(values(r)[:, u, :], ring[:, r, u, :], wt[:, WV, :], start=True, stop=True)
                            ins.then_inc(p_projected, 1)

                        def body(i):
                            for r in range(REGIONS):
                                if nxt := led(i, r, 1):
                                    project(*nxt)
                                pe.wait_ge(p_selected, region_of(i, r) * 2 + 2)
                                pe.wait_ge(p_weighted, region_of(i, r) + 1)
                                at_least(pe, p_added, (region_of(i, r) - 1) * GROUP)
                                for u in range(GROUP):
                                    ins = pe.matmul(sums(r, u), select[:, r, u, :], msg[:, r, u, :], start=True, stop=True)
                                ins.then_inc(p_summed, 1)
                        project(0, 0)
                        turns(pe, body)

        def transformer_pass(name, base):
            W = D + L3_HEADS
            HD = D // L3_HEADS
            with ExitStack() as tmp:
                ring = sb(f"{name}_ring", [P, REGIONS, GROUP, 2 * D], F32, tmp)
                part = sb(f"{name}_part", [P, 2, GROUP, L3_HEADS], F32, tmp)
                room = score[:].rearrange("p s h -> p (s h)")
                spread = room[:, 0:2 * GROUP * P].rearrange("p (a u f) -> p a u f", a=2, u=GROUP)
                prod = room[:, 2 * GROUP * P:3 * GROUP * P].rearrange("p (u f) -> p u f", u=GROUP)
                msg = room[:, 3 * GROUP * P:3 * GROUP * P + 2 * GROUP * W].rearrange("p (a u f) -> p a u f", a=2, u=GROUP)

                def q_bank(r):
                    return psum[:, 1 + r % 2, :]

                def sums(r, u):
                    return psum[:, 4 + 2 * (r % 2) + u // 2, (u % 2) * W:(u % 2 + 1) * W]

                with block(name, p_index, p_selected, p_turned, p_spread, p_projected, p_multiplied, p_evacuated, p_scored,
                           p_weight, p_weighted, p_summed, p_added) as b:
                    @b.gpsimd
                    def _(pool):
                        gathers(pool, ring, table_kv[:])

                    @b.scalar
                    def _(act):
                        def turned(i, r):
                            act.wait_ge(p_turned, region_of(i, r) + 1)
                            act.copy(spread[:, r % 2, :, :], bank4(psum[:, 0, :])).then_inc(p_spread, 1)

                        def body(i):
                            for r in range(REGIONS):
                                act.wait_ge(p_scored, region_of(i, r) + 1)
                                at_least(act, p_summed, region_of(i, r) - 1)
                                act.activation(msg[:, r % 2, :, D:W], part[:, r % 2, :, :], ACT.Exp, scale=HD ** -0.5).then_inc(p_weight, 1)
                                if nxt := led(i, r):
                                    turned(*nxt)
                        turned(0, 0)
                        turned(0, 1)
                        turns(act, body)

                    @b.vector
                    def _(dve):
                        half = GROUP // 2
                        dve.memset(acc[:], 0.0)
                        def body(i):
                            for r in range(REGIONS):
                                j = region_of(i, r)
                                nxt, last = led(i, r), led(i, r, -1)
                                dve.wait_ge(p_projected, j + 1)
                                dve.wait_ge(gathered[r], landed(i, base))
                                dve.tensor_tensor(prod, ring[:, r, :, 0:D], bank4(q_bank(r)), ALU.mult).then_inc(p_multiplied, 1)
                                if nxt:
                                    at_least(dve, p_summed, region_of(*nxt) - (REGIONS - 1))
                                    make_select(dve, *nxt, 0, half)

                                def reduce():
                                    dve.wait_ge(p_multiplied, j + 1)
                                    dve.tensor_reduce(part[:, r % 2, :, :], prod.rearrange("p u (h e) -> p u h e", h=L3_HEADS),
                                                      AX_X, ALU.add).then_inc(p_evacuated, 1)

                                def clip():
                                    dve.wait_ge(p_evacuated, j + 1)
                                    dve.tensor_scalar(part[:, r % 2, :, :], part[:, r % 2, :, :], 5.0 * HD ** 0.5, -5.0 * HD ** 0.5,
                                                      ALU.min, ALU.max).then_inc(p_scored, 1)

                                between = [reduce, clip] + ([lambda: make_select(dve, *nxt, half, half)] if nxt else [])
                                if isinstance(last[0], int) and last[0] < 0:
                                    for piece in between:
                                        piece()
                                else:
                                    add_blocks(dve, sums, *last, W, between)
                                dve.wait_ge(p_weight, j + 1)
                                dve.tensor_tensor(msg[:, r % 2, :, 0:D].rearrange("p u (h e) -> p u h e", h=L3_HEADS),
                                                  ring[:, r, :, D:2 * D].rearrange("p u (h e) -> p u h e", h=L3_HEADS),
                                                  msg[:, r % 2, :, D:W].unsqueeze(3).broadcast_to([P, GROUP, L3_HEADS, HD]),
                                                  ALU.mult).then_inc(p_weighted, 1)
                                if nxt := led(i, r, REGIONS):
                                    dve.wait_ge(p_weighted, j + 1)
                                    copy_index(dve, src_idx, *nxt)
                        for r in range(REGIONS):
                            copy_index(dve, src_idx, 0, r)
                        for r in range(2):
                            make_select(dve, 0, r, 0, half)
                            make_select(dve, 0, r, half, half)
                        turns(dve, body)
                        add_blocks(dve, sums, LOOPS - 1, REGIONS - 1, W)

                    @b.tensor
                    def _(pe):
                        def turn(i, r):
                            pe.wait_ge(p_selected, region_of(i, r) * 2 + 2)
                            at_least(pe, p_spread, region_of(i, r))
                            for u in range(GROUP):
                                ins = pe.transpose(psum[:, 0, u * P:(u + 1) * P], select[:, r, u, :], ident[:])
                            ins.then_inc(p_turned, 1)


                        def queries(i, r):
                            blocks = blocks_of(pe, i, r)
                            pe.wait_ge(p_spread, region_of(i, r) + 1)
                            at_least(pe, p_multiplied, region_of(i, r) - 1)
                            for u in range(GROUP):
                                q = t1[:, bass.ds(blocks[u] * D, D)]
                                ins = pe.matmul(q_bank(r)[:, u * P:(u + 1) * P], spread[:, r % 2, u, :], q, start=True, stop=True)
                            ins.then_inc(p_projected, 1)

                        def body(i):
                            for r in range(REGIONS):
                                if nxt := led(i, r, 1):
                                    queries(*nxt)
                                if nxt := led(i, r):
                                    turn(*nxt)
                                pe.wait_ge(p_weighted, region_of(i, r) + 1)
                                at_least(pe, p_added, (region_of(i, r) - 1) * GROUP)
                                for u in range(GROUP):
                                    ins = pe.matmul(sums(r, u), select[:, r, u, :], msg[:, r % 2, u, :], start=True, stop=True)
                                ins.then_inc(p_summed, 1)
                        turn(0, 0)
                        turn(0, 1)
                        queries(0, 0)
                        turns(pe, body)

        s_scores_turned, s_scores_copied, s_max, s_ends_turned, s_chain, s_chain_io, s_exp, s_weights_turned, s_weights_kept = sems(
            "scores_turned", "scores_copied", "max_step", "ends_turned", "chain_ready", "chain_moved", "weights_made",
            "weights_turned", "weights_kept")
        s_in_dram, = sems("enter_in_dram")
        max_done = [8 + 3 * (h + 1) for h in range(GAT_HEADS)]
        carry_dram = nc.dram_tensor("carry_dram", [2 * GAT_HEADS * ROW_C, ROW_K], F32)
        enter_dram = nc.dram_tensor("enter_dram", [2 * GAT_HEADS * ROW_C, ROW_K], F32)

        def gat_softmax(name):
            HC = GAT_HEADS * ROW_C
            RUN = ROW_C * P
            per_bank = CHUNK // ROW_K
            with ExitStack() as tmp:
                scores = sb(f"{name}_scores", [ROW_K, HC, P], F32, tmp)
                run_f = acc[0:ROW_K, 0:HC * P].rearrange("k (a p) -> k a p", p=P)
                run_b = t1[0:ROW_K, 0:HC * P].rearrange("k (a p) -> k a p", p=P)
                ends = sb(f"{name}_ends", [ROW_K, 2, HC], F32, tmp)
                ends_t = sb(f"{name}_ends_t", [2 * HC, ROW_K], F32, tmp)
                enter_t = sb(f"{name}_enter_t", [2 * HC, ROW_K], F32, tmp)
                enter = sb(f"{name}_enter", [ROW_K, 2, HC], F32, tmp)
                row_max = t1[0:GAT_HEADS, HC * P:HC * P + 2 * STEPS].rearrange("h (d s) -> h d s", d=2)
                chain = acc[0:GAT_HEADS, HC * P:HC * P + 2 * STEPS].rearrange("h (d s) -> h d s", d=2)
                with block(name, s_scores_turned, s_scores_copied, s_max, s_ends_turned, s_chain, s_chain_io, s_exp,
                           s_weights_turned, s_weights_kept, s_in_dram) as b:
                    @b.tensor
                    def _(pe):
                        for a in range(HC):
                            h, c = divmod(a, ROW_C)
                            ins = pe.transpose(psum[0:ROW_K, a // 4, (a % 4) * P:(a % 4 + 1) * P],
                                               score[:, c * ROW_K:(c + 1) * ROW_K, h], ident[:])
                            if a % 4 == 3:
                                ins.then_inc(s_scores_turned, 1)
                        pe.wait_ge(s_chain, 1)
                        pe.transpose(psum[0:2 * HC, 7, 0:ROW_K], ends[:].rearrange("k a b -> k (a b)"),
                                     ident[0:ROW_K, 0:ROW_K]).then_inc(s_ends_turned, 1)
                        pe.wait_ge(s_chain_io, 48)
                        pe.transpose(psum[0:ROW_K, 7, ROW_K:ROW_K + 2 * HC], enter_t[:],
                                     ident[0:2 * HC, 0:2 * HC]).then_inc(s_ends_turned, 1)
                        pe.wait_ge(s_chain, 4)
                        for h in range(GAT_HEADS):
                            pe.wait_ge(s_exp, h + 1)
                            for c in range(ROW_C):
                                ins = pe.transpose(psum[:, 2 * h + c // per_bank, (c % per_bank) * ROW_K:(c % per_bank + 1) * ROW_K],
                                                   scores[:, h * ROW_C + c, :], ident[0:ROW_K, 0:ROW_K])
                            ins.then_inc(s_weights_turned, 1)

                    @b.sync
                    def _(sp):
                        sp.wait_ge(s_chain, 2)
                        sp.dma_start(carry_dram[:], ends_t[:]).then_inc(s_chain_io, 16)
                        sp.wait_ge(s_chain_io, 16)
                        sp.dma_start(row_max, carry_dram.ap().rearrange("(d h c) k -> h d (c k)", d=2, h=GAT_HEADS)).then_inc(s_chain_io, 16)
                        sp.wait_ge(s_chain, 3)
                        sp.dma_start(enter_dram.ap().rearrange("(d h c) k -> h d (c k)", d=2, h=GAT_HEADS), row_max).then_inc(s_in_dram, 16)
                        sp.wait_ge(s_in_dram, 16)
                        sp.dma_start(enter_t[:], enter_dram[:]).then_inc(s_chain_io, 16)

                    @b.scalar
                    def _(act):
                        for g in range(HC // 4):
                            act.wait_ge(s_scores_turned, g + 1)
                            act.copy(scores[:, 4 * g:4 * g + 4, :], bank4(psum[0:ROW_K, g, :])).then_inc(s_scores_copied, 1)
                        for h in range(GAT_HEADS):
                            act.wait_ge(s_max, max_done[h])
                            act.activation(scores[:, h * ROW_C:(h + 1) * ROW_C, :], scores[:, h * ROW_C:(h + 1) * ROW_C, :], ACT.Exp,
                                           scale=(D // GAT_HEADS) ** -0.5).then_inc(s_exp, 1)
                        for h in range(0, GAT_HEADS, 2):
                            act.wait_ge(s_weights_turned, h + 1)
                            act.copy(score[:, 0:per_bank * ROW_K, h], psum[:, 2 * h, 0:per_bank * ROW_K])
                            act.copy(score[:, per_bank * ROW_K:STEPS, h], psum[:, 2 * h + 1, 0:STEPS - per_bank * ROW_K]).then_inc(s_weights_kept, 1)

                    @b.vector
                    def _(dve):
                        n = [0]

                        def link(ins):
                            n[0] += 1
                            ins.then_inc(s_max, 1)
                            dve.wait_ge(s_max, n[0])

                        def flat(ap, h):
                            return ap[:, h * ROW_C:(h + 1) * ROW_C, :].rearrange("k a p -> k (a p)")

                        for h in range(GAT_HEADS):
                            dve.wait_ge(s_scores_copied, -(-(h + 1) * ROW_C // 4))
                            dve.tensor_tensor_scan(flat(run_f, h), key_pen_f[:], flat(scores, h), -BIG, ALU.add, ALU.max)
                            ins = dve.tensor_tensor_scan(flat(run_b, h)[:, ::-1], key_pen_b[:, ::-1], flat(scores, h)[:, ::-1], -BIG,
                                                         ALU.add, ALU.max)
                        link(ins)
                        link(dve.tensor_copy(ends[:, 0, :], run_f[:, :, P - 1]))
                        link(dve.tensor_copy(ends[:, 1, :], run_b[:, :, 0]))
                        dve.sem_inc(s_chain, 1)
                        link(dve.tensor_tensor(run_f, run_f, run_b, ALU.max))
                        dve.wait_ge(s_ends_turned, 1)
                        dve.tensor_copy(ends_t[:], psum[0:2 * HC, 7, 0:ROW_K]).then_inc(s_chain, 1)
                        dve.wait_ge(s_chain_io, 32)
                        dve.tensor_tensor_scan(chain[:, 0, :], chain_pen[:, 0, :], row_max[:, 0, :], -BIG, ALU.add, ALU.max)
                        link(dve.tensor_tensor_scan(chain[:, 1, ::-1], chain_pen[:, 1, ::-1], row_max[:, 1, ::-1], -BIG, ALU.add, ALU.max))
                        link(dve.memset(row_max, -BIG))
                        link(dve.tensor_tensor(row_max[:, 0, 1:STEPS], chain[:, 0, 0:STEPS - 1], enter_pen[:, 0, 1:STEPS], ALU.add))
                        link(dve.tensor_tensor(row_max[:, 1, 0:STEPS - 1], chain[:, 1, 1:STEPS], enter_pen[:, 1, 0:STEPS - 1], ALU.add))
                        dve.sem_inc(s_chain, 1)
                        dve.wait_ge(s_ends_turned, 2)
                        dve.tensor_copy(enter[:].rearrange("k a b -> k (a b)"), psum[0:ROW_K, 7, ROW_K:ROW_K + 2 * HC]).then_inc(s_chain, 1)
                        dve.wait_ge(s_chain, 4)
                        for h in range(GAT_HEADS):
                            for d, pen in enumerate((first_pen, last_pen)):
                                for c in range(ROW_C):
                                    a = h * ROW_C + c
                                    ins = dve.scalar_tensor_tensor(out=run_f[:, a, :], in0=pen[:, c, :], scalar=enter[:, d, a:a + 1],
                                                                   in1=run_f[:, a, :], op0=ALU.add, op1=ALU.max)
                                link(ins)
                            link(dve.tensor_tensor(flat(scores, h), flat(scores, h), flat(run_f, h), ALU.subtract))
                            assert n[0] == max_done[h]
                        for h in range(1, GAT_HEADS, 2):
                            dve.wait_ge(s_weights_turned, h + 1)
                            dve.tensor_copy(score[:, 0:per_bank * ROW_K, h], psum[:, 2 * h, 0:per_bank * ROW_K])
                            dve.tensor_copy(score[:, per_bank * ROW_K:STEPS, h], psum[:, 2 * h + 1, 0:STEPS - per_bank * ROW_K])


        d_rows, d_turned, d_mixed, d_product, d_done, d_link = sems(
            "rows_ready", "turned_ready", "mixed_ready", "product_ready", "chunk_done", "rows_step")

        def from_rows(name, dst, heads=0, eps=0.0, offset=None, mix=None, weight=None, bias=None, residual=None):
            with ExitStack() as tmp:
                rows = sb(f"{name}_rows", [P, V, 4, D], F32, tmp)
                den = sb(f"{name}_den", [P, V, 4, max(heads, 1)], F32, tmp)
                mixed = sb(f"{name}_mixed", [P, V, CHUNK], F32, tmp)
                with block(name, d_rows, d_turned, d_mixed, d_product, d_done, d_link) as b:
                    @b.vector
                    def _(dve):
                        def stage(c, u, i):
                            at_least(dve, d_turned, c + 1 - V)
                            if not heads:
                                dve.tensor_scalar(rows[:, u, :, :], acc_rows(c, 0, D), 0.0, None, ALU.add).then_inc(d_rows, 1)
                                return
                            links = 2 if offset is None else 4

                            def by_head(ap):
                                return ap.rearrange("p b (h e) -> p b h e", h=heads)

                            def over_head(ap):
                                return ap.unsqueeze(3).broadcast_to([P, 4, heads, D // heads])
                            dve.tensor_scalar(den[:, u, :, :], acc_rows(c, D, heads), eps, None, ALU.add).then_inc(d_link, 1)
                            dve.wait_ge(d_link, c * links + 1)
                            dve.reciprocal(den[:, u, :, :], den[:, u, :, :]).then_inc(d_link, 1)
                            total = by_head(acc_rows(c, 0, D))
                            if offset is not None:
                                shifted = by_head(rows[:, u, :, :])
                                dve.tensor_tensor(shifted, over_head(acc_rows(c, D, heads)),
                                                  by_head(offset.unsqueeze(1).broadcast_to([P, 4, D])), ALU.mult).then_inc(d_link, 1)
                                dve.wait_ge(d_link, c * links + 3)
                                dve.tensor_tensor(shifted, shifted, total, ALU.add).then_inc(d_link, 1)
                                total = shifted
                            dve.wait_ge(d_link, c * links + links)
                            dve.tensor_tensor(by_head(rows[:, u, :, :]), total, over_head(den[:, u, :, :]), ALU.mult).then_inc(d_rows, 1)

                        def add_state(c, u, i):
                            dve.wait_ge(d_turned, c + 1)
                            at_least(dve, d_product, c + 1 - V)
                            dve.scalar_tensor_tensor(out=mixed[:, u, :], in0=mix[:, cols(c)], scalar=eps_col[:], in1=psum[:, u, :],
                                                     op0=ALU.mult, op1=ALU.add).then_inc(d_mixed, 1)

                        def finish(c, u, i):
                            if weight is None:
                                dve.wait_ge(d_turned, c + 1)
                                ins = dve.tensor_scalar(dst[:, cols(c)], psum[:, u, :], 0.0, None, ALU.add)
                            else:
                                dve.wait_ge(d_product, c + 1)
                                if residual is None:
                                    ins = dve.tensor_scalar(dst[:, cols(c)], psum[:, 4 + u, :], bias, None, ALU.add)
                                else:
                                    ins = dve.scalar_tensor_tensor(out=dst[:, cols(c)], in0=psum[:, 4 + u, :], scalar=bias,
                                                                   in1=residual[:, cols(c)], op0=ALU.add, op1=ALU.add)
                            ins.then_inc(d_done, 1)
                        pairs(dve, *([stage, add_state, finish] if mix is not None else [stage, finish]))

                    if weight is not None and mix is None:
                        @b.scalar
                        def _(act):
                            def copy(c, u, i):
                                act.wait_ge(d_turned, c + 1)
                                at_least(act, d_product, c + 1 - V)
                                act.copy(mixed[:, u, :], psum[:, u, :]).then_inc(d_mixed, 1)
                            pairs(act, copy)

                    @b.tensor
                    def _(pe):
                        def turn(c, u, i):
                            pe.wait_ge(d_rows, c + 1)
                            at_least(pe, d_done if weight is None else d_mixed, c + 1 - V)
                            for k in range(4):
                                ins = pe.transpose(psum[:, u, k * P:(k + 1) * P], rows[:, u, k, :], ident[:])
                            ins.then_inc(d_turned, 1)

                        def project(c, u, i):
                            pe.wait_ge(d_mixed, c + 1)
                            at_least(pe, d_done, c + 1 - V)
                            pe.matmul(psum[:, 4 + u, :], weight, mixed[:, u, :], start=True, stop=True).then_inc(d_product, 1)
                        pairs(pe, *([turn] if weight is None else [turn, project]))

        def feed_forward(name, src, dst, function, w_in, b_in, w_out, b_out):
            K = len(w_in)
            with ExitStack() as tmp:
                inner = sb(f"{name}_inner", [P, V, K, CHUNK], F32, tmp)
                with block(name, d_turned, d_mixed, d_product, d_done) as b:
                    @b.tensor
                    def _(pe):
                        def expand(c, u, i):
                            for k in range(K):
                                at_least(pe, d_mixed, c * K + (k + 1 - 4))
                                pe.matmul(psum[:, (u * K + k) % 4, :], w_in[k], src[:, cols(c)], start=True, stop=True).then_inc(d_turned, 1)

                        def contract(c, u, i):
                            at_least(pe, d_done, c + 1 - V)
                            for k in range(K):
                                pe.wait_ge(d_mixed, c * K + (k + 1))
                                ins = pe.matmul(psum[:, 4 + u, :], w_out[k], inner[:, u, k, :], start=k == 0, stop=k == K - 1)
                            ins.then_inc(d_product, 1)

                        def both(c, u, i):
                            expand(c, u, i)
                            contract(c, u, i)
                        pairs(pe, both)

                    @b.scalar
                    def _(act):
                        def bend(c, u, i):
                            at_least(act, d_product, c + 1 - V)
                            for k in range(K):
                                act.wait_ge(d_turned, c * K + (k + 1))
                                act.activation(inner[:, u, k, :], psum[:, (u * K + k) % 4, :], function, bias=b_in[k]).then_inc(d_mixed, 1)
                        pairs(act, bend)

                    @b.vector
                    def _(dve):
                        def finish(c, u, i):
                            dve.wait_ge(d_product, c + 1)
                            dve.scalar_tensor_tensor(out=dst[:, cols(c)], in0=psum[:, 4 + u, :], scalar=b_out, in1=src[:, cols(c)],
                                                     op0=ALU.add, op1=ALU.add).then_inc(d_done, 1)
                        pairs(dve, finish)

        g_product, g_gated, g_reset, g_new, g_read, g_step = sems(
            "gru_products", "gru_gates", "gru_reset_applied", "gru_new", "gru_banks_read", "gru_step")

        def gru(name, msg, h, w_ih, w_hh, gates, b_in, b_hn):
            with ExitStack() as tmp:
                gate = sb(f"{name}_gate", [P, V, 2, CHUNK], F32, tmp)
                new = sb(f"{name}_new", [P, V, CHUNK], F32, tmp)
                with block(name, g_product, g_gated, g_reset, g_new, g_read, g_step) as b:
                    @b.tensor
                    def _(pe):
                        def project(c, u, i):
                            at_least(pe, g_gated, c + 1 - V)
                            at_least(pe, g_read, c + 1 - V)
                            for k in range(2):
                                pe.matmul(psum[:, 4 * u + k, :], w_ih[k], msg[:, cols(c)], start=True, stop=False)
                                pe.matmul(psum[:, 4 * u + k, :], w_hh[k], h[:, cols(c)], start=False, stop=True)
                            pe.matmul(psum[:, 4 * u + 2, :], w_ih[2], msg[:, cols(c)], start=True, stop=True)
                            pe.matmul(psum[:, 4 * u + 3, :], w_hh[2], h[:, cols(c)], start=True, stop=True).then_inc(g_product, 1)
                        pairs(pe, project)

                    @b.scalar
                    def _(act):
                        def bend(c, u, i):
                            act.wait_ge(g_product, c + 1)
                            at_least(act, g_step, (c + 1 - V) * 3)
                            act.activation(gate[:, u, 0, :], psum[:, 4 * u, :], ACT.Sigmoid, bias=gates[:, 0:1])
                            act.activation(gate[:, u, 1, :], psum[:, 4 * u + 1, :], ACT.Sigmoid, bias=gates[:, 1:2]).then_inc(g_gated, 1)

                        def renew(c, u, i):
                            act.wait_ge(g_read, c + 1)
                            act.activation(new[:, u, :], new[:, u, :], ACT.Tanh, bias=b_in).then_inc(g_new, 1)
                        pairs(act, bend, renew)

                    @b.vector
                    def _(dve):
                        def reset(c, u, i):
                            dve.wait_ge(g_gated, c + 1)
                            dve.scalar_tensor_tensor(out=new[:, u, :], in0=psum[:, 4 * u + 3, :], scalar=b_hn, in1=gate[:, u, 0, :],
                                                     op0=ALU.add, op1=ALU.mult).then_inc(g_reset, 1)
                            dve.wait_ge(g_reset, c + 1)
                            dve.tensor_tensor(new[:, u, :], new[:, u, :], psum[:, 4 * u + 2, :], ALU.add).then_inc(g_read, 1)

                        def update(c, u, i):
                            dve.wait_ge(g_new, c + 1)
                            dve.tensor_tensor(gate[:, u, 0, :], h[:, cols(c)], new[:, u, :], ALU.subtract).then_inc(g_step, 1)
                            dve.wait_ge(g_step, c * 3 + 1)
                            dve.tensor_tensor(gate[:, u, 0, :], gate[:, u, 0, :], gate[:, u, 1, :], ALU.mult).then_inc(g_step, 1)
                            dve.wait_ge(g_step, c * 3 + 2)
                            dve.tensor_tensor(h[:, cols(c)], new[:, u, :], gate[:, u, 0, :], ALU.add).then_inc(g_step, 1)
                        pairs(dve, reset, update)

        b_stats, b_root, b_applied, b_scale, b_done = sems("bn_step", "bn_rooted", "bn_applied", "bn_product", "bn_done")

        def batch_norm(name, src, gain, shift, dst=None, residual=None, weight=None, bias=None):
            with ExitStack() as tmp:
                stats = sb(f"{name}_stats", [P, CHUNKS, 6], F32, tmp)
                moments = sb(f"{name}_moments", [P, 2], F32, tmp)
                coef = sb(f"{name}_coef", [P, 3], F32, tmp)
                normed = sb(f"{name}_normed", [P, V, CHUNK], F32, tmp)
                with block(name, b_stats, b_root, b_applied, b_scale, b_done) as b:
                    @b.vector
                    def _(dve):
                        dve.memset(coef[:, 2:3], BN_EPS).then_inc(b_stats, 1)
                        for k in range(CHUNKS):
                            dve.bn_stats(stats[:, k, :], src[:, k * BN_CHUNK:(k + 1) * BN_CHUNK]).then_inc(b_stats, 1)
                        dve.wait_ge(b_stats, CHUNKS + 1)
                        dve.bn_aggr(moments[:], stats[:]).then_inc(b_stats, 1)
                        dve.wait_ge(b_root, 1)
                        dve.reciprocal(moments[:, 1:2], moments[:, 1:2]).then_inc(b_stats, 1)
                        dve.wait_ge(b_stats, CHUNKS + 3)
                        dve.tensor_tensor(coef[:, 0:1], moments[:, 1:2], gain, ALU.mult).then_inc(b_stats, 1)
                        dve.wait_ge(b_stats, CHUNKS + 4)
                        dve.tensor_tensor(moments[:, 0:1], moments[:, 0:1], coef[:, 0:1], ALU.mult).then_inc(b_stats, 1)
                        dve.wait_ge(b_stats, CHUNKS + 5)
                        dve.tensor_tensor(coef[:, 1:2], shift, moments[:, 0:1], ALU.subtract).then_inc(b_stats, 1)
                        dve.wait_ge(b_stats, CHUNKS + 6)
                        if dst is not None:
                            dve.tensor_scalar(dst[:], src[:, 0:NP], coef[:, 0:1], coef[:, 1:2], ALU.mult, ALU.add)
                            return

                        def finish(c, u, i):
                            dve.wait_ge(b_scale if weight is not None else b_applied, c + 1)
                            if weight is not None:
                                ins = dve.scalar_tensor_tensor(out=residual[:, cols(c)], in0=psum[:, u, :], scalar=bias, in1=residual[:, cols(c)],
                                                               op0=ALU.add, op1=ALU.add)
                            else:
                                ins = dve.tensor_tensor(residual[:, cols(c)], residual[:, cols(c)], normed[:, u, :], ALU.add)
                            ins.then_inc(b_done, 1)
                        pairs(dve, finish)

                    @b.scalar
                    def _(act):
                        act.wait_ge(b_stats, CHUNKS + 2)
                        act.activation(moments[:, 1:2], moments[:, 1:2], ACT.Sqrt, bias=coef[:, 2:3]).then_inc(b_root, 1)
                        if dst is not None:
                            return
                        act.wait_ge(b_stats, CHUNKS + 6)

                        def apply(c, u, i):
                            at_least(act, b_scale if weight is not None else b_done, c + 1 - V)
                            act.activation(normed[:, u, :], src[:, cols(c)], ACT.Relu if weight is not None else ACT.Identity,
                                           bias=coef[:, 1:2], scale=coef[:, 0:1]).then_inc(b_applied, 1)
                        pairs(act, apply)

                    if weight is not None:
                        @b.tensor
                        def _(pe):
                            def project(c, u, i):
                                pe.wait_ge(b_applied, c + 1)
                                at_least(pe, b_done, c + 1 - V)
                                pe.matmul(psum[:, u, :], weight, normed[:, u, :], start=True, stop=True).then_inc(b_scale, 1)
                            pairs(pe, project)

        a_added, = sems("state_added")

        def add_state(name, src):
            with block(name, a_added) as b:
                @b.vector
                def _(dve):
                    dve.tensor_tensor(resT[:], resT[:], src[:], ALU.add).then_inc(a_added, 1)

        o_staged, o_turned, o_copied = sems("out_staged", "out_turned", "out_copied")
        o_stored = sems(*(f"out_stored{u}" for u in range(V)))

        def store(name):
            with ExitStack() as tmp:
                rows = sb(f"{name}_rows", [P, V, CHUNK], F32, tmp)
                state = sb(f"{name}_state", [P, V, CHUNK], F32, tmp)
                with block(name, o_staged, o_turned, o_copied, *o_stored) as b:
                    @b.vector
                    def _(dve):
                        def stage(c, u, i):
                            at_least(dve, o_turned, c + 1 - V)
                            dve.tensor_scalar(state[:, u, :], resT[:, cols(c)], 0.0, None, ALU.add).then_inc(o_staged, 1)
                        pairs(dve, stage)

                    @b.tensor
                    def _(pe):
                        def turn(c, u, i):
                            pe.wait_ge(o_staged, c + 1)
                            at_least(pe, o_copied, c + 1 - V)
                            for k in range(4):
                                ins = pe.transpose(psum[:, u, k * P:(k + 1) * P], state[:, u, k * P:(k + 1) * P], ident[:])
                            ins.then_inc(o_turned, 1)
                        pairs(pe, turn)

                    @b.scalar
                    def _(act):
                        def copy(c, u, i):
                            act.wait_ge(o_turned, c + 1)
                            at_least(act, o_stored[u], i * 16)
                            act.copy(rows[:, u, :], psum[:, u, :]).then_inc(o_copied, 1)
                        pairs(act, copy)

                    @b.sync
                    def _(sp):
                        def leave(c, u, i):
                            sp.wait_ge(o_copied, c + 1)
                            sp.dma_start(out[cols(c), :].rearrange("(b p) f -> p b f", p=P), bank4(rows[:, u, :])).then_inc(o_stored[u], 16)
                        for c in range(V):
                            leave(c, c, 0)
                        with sp.Fori(1, CHUNKS // V - 1) as i:
                            for u in range(V):
                                leave(i * V + u, u, i)
                        leave(CHUNKS - 2, 0, CHUNKS // V - 1)
                        sp.wait_ge(o_copied, CHUNKS)
                        first = (CHUNKS - 1) * CHUNK
                        sp.dma_start(out[first:FULL_BLOCKS * P, :].rearrange("(b p) f -> p b f", p=P),
                                     bank4(rows[:, 1, :])[:, 0:FULL_BLOCKS - first // P, :]).then_inc(o_stored[1], 16)
                        sp.dma_start(out[FULL_BLOCKS * P:N, :], rows[0:TAIL, 1, (FULL_BLOCKS - first // P) * P:(FULL_BLOCKS - first // P + 1) * P]
                                     ).then_inc(o_stored[1], 16)
                        sp.wait_ge(o_stored[0], 16 * (CHUNKS // V))
                        sp.wait_ge(o_stored[1], 16 * (CHUNKS // V + 1))

        def parts_of(w, first, count):
            return [w[:, first + k, :] for k in range(count)]

        layer_norm("l0_norm", resT, xT, LN_EPS, also=hT)
        with nc.Fori(0, GAT_ITERS) as it:
            node_rows("l0_rows", xT, queries=True)
            gat_score_pass("l0_scores", it * ROWS)
            gat_softmax("l0_softmax")
            gat_value_pass("l0_values")
            from_rows("l0_attention", t1, heads=GAT_HEADS, eps=1e-16, offset=bv_rows[:], weight=wt[:, WAO, :], bias=wcol("b_ao"), residual=xT)
            layer_norm("l0_ln1", t1, xT, 1e-12, wcol("ln1_g"), wcol("ln1_b"))
            feed_forward("l0_ffn", xT, t1, ACT.Gelu, parts_of(wt, WINT, GAT_FF), [wcol("b_int", k) for k in range(GAT_FF)],
                         parts_of(wt, WOUT, GAT_FF), wcol("b_out"))
            layer_norm("l0_ln2", t1, xT, 1e-12, wcol("ln2_g"), wcol("ln2_b"))
            gru("l0_gru", xT, hT, parts_of(wt, GIH, 3), parts_of(wt, GHH, 3), gate_bias[:, 0, :], wcol("b_ih", 2), wcol("b_hh", 2))
            layer_norm("l0_ln3", hT, xT, 1e-12, wcol("ln3_g"), wcol("ln3_b"))
            clear_block("l0_end")
        add_state("l0_residual", xT)

        layer_norm("l1_norm", resT, hT, LN_EPS)
        node_rows("l1_rows", hT, queries=False)
        sum_pass("l1_sums", table_x[:], src_idx, GAT_ITERS * ROWS)
        from_rows("l1_first", t1, mix=hT, weight=wt[:, GIN1, :], bias=wcol("1_b1"))
        batch_norm("l1_second", t1, wcol("1_gamma"), wcol("1_beta"), residual=resT, weight=wt[:, GIN2, :], bias=wcol("1_b2"))

        layer_norm("l2_norm", resT, hT, LN_EPS)
        with nc.Fori(0, L2_STEPS) as it:
            projected_rows("l2_rows", hT, wt[:, WEDGE:WEDGE + 4, :].rearrange("p a b -> p (a b)"), 4 * D, table_typed, bias=bedge_rows[:])
            sum_pass("l2_sums", table_typed.ap().rearrange("n (t f) -> (n t) f", f=D), typed_idx, (GAT_ITERS + 1) * ROWS + it * ROWS)
            from_rows("l2_messages", t1)
            gru("l2_gru", t1, hT, parts_of(wt, GGIH, 3), parts_of(wt, GGHH, 3), gate_bias[:, 1, :], wcol("2_b_ih", 2), wcol("2_b_hh", 2))
            clear_block("l2_end")
        add_state("l2_residual", hT)

        layer_norm("l3_norm", resT, xT, LN_EPS)
        projected_rows("l3_rows", xT, w3[:, 0:3, :].rearrange("p a b -> p (a b)"), 3 * D, table_kv, query_width=D)
        transformer_pass("l3_pass", (GAT_ITERS + 1 + L2_STEPS) * ROWS)
        from_rows("l3_attention", t1, heads=L3_HEADS, eps=1e-6, weight=w3[:, 3, :], bias=wcol("3_bo"), residual=xT)
        batch_norm("l3_bn1", t1, wcol("3_bn1_g"), wcol("3_bn1_b"), dst=xT)
        feed_forward("l3_ffn", xT, t1, ACT.Relu, parts_of(w3, 4, 2), [wcol("3_b1", k) for k in range(2)], parts_of(w3, 6, 2), wcol("3_b2"))
        batch_norm("l3_bn2", t1, wcol("3_bn2_g"), wcol("3_bn2_b"), residual=resT)
        store("store")


def kernel(**inputs):
    import numpy as _np
    import concourse.bacc as _bacc
    from concourse import mybir as _mybir
    from concourse.bass_utils import run_bass_kernel_spmd as _run

    nc = _bacc.Bacc("TRN2", target_bir_lowering=False, num_devices=1)
    arrays, io = {}, {}
    for name in inputs:
        a = _np.ascontiguousarray(inputs[name])
        arrays[f"in_{name}_dram"] = a
        io[name] = nc.dram_tensor(f"in_{name}_dram", a.shape, _mybir.dt.from_np(a.dtype), kind="ExternalInput").ap()
    out = nc.dram_tensor("out_0_dram", (N, D), F32, kind="ExternalOutput").ap()
    program(nc, io, out)
    r = _run(nc, [arrays], core_ids=[0])
    return r.results[0]["out_0_dram"]
```
